# Optimizing a Trainium2 kernel written in Bass

```python
import numpy as np
import jax
import jax.numpy as jnp

def _softmax(x, axis=-1):
    return jax.nn.softmax(x, axis=axis)

def _gelu(x):
    return jax.nn.gelu(x, approximate=True)

def _silu(x):
    return jax.nn.silu(x)

def _sigmoid(x):
    return jax.nn.sigmoid(x)

def _layernorm(x, axis=-1, eps=1e-05):
    m = jnp.mean(x, axis=axis, keepdims=True)
    v = jnp.var(x, axis=axis, keepdims=True)
    return (x - m) / jnp.sqrt(v + eps)

def _scatter_add(tgt, idx, src, axis=0):
    return tgt.at[idx].add(src)

def _segment_sum(src, seg, n):
    return jax.ops.segment_sum(src, seg, n)
kernel_name = 'mk_perceiver_d1_seqx_r2_9f35d9'

def setup_inputs(seed: int=0):
    np.random.seed(seed)
    _w = jnp.asarray

    def _rec_inputs():
        import jax
        import jax.numpy as jnp
        _rk = jax.random.key(seed)
        x = 7.22e-05 + 1 * jax.random.normal(jax.random.fold_in(_rk, 1), (16, 64, 512), jnp.float32)
        _lenS = 64 - jax.random.randint(jax.random.fold_in(_rk, 7), (16,), 0, max(1, 64 // 4) + 1, jnp.int32)
        _lenS2 = 512 - jax.random.randint(jax.random.fold_in(_rk, 8), (16,), 0, max(1, 512 // 4) + 1, jnp.int32)
        _ctx_1024P = jax.random.normal(jax.random.fold_in(_rk, 11), (16, 16, 512), jnp.float32)
        _ctx_1024c = jax.random.dirichlet(jax.random.fold_in(_rk, 511), 0.3 * jnp.ones((16,), jnp.float32), (16, 512))
        _ctx_1024t = jnp.einsum('bsk,bkd->bsd', _ctx_1024c, _ctx_1024P)
        _ctx_1024t = _ctx_1024t * jax.lax.rsqrt(jnp.mean(jnp.square(_ctx_1024t)) + 1e-12) * 0.953939
        ctx_1024 = 4.13588e-05 + 0.999923 * (_ctx_1024t + 0.3 * jax.random.normal(jax.random.fold_in(_rk, 611), (16, 512, 512), jnp.float32))
        _validS = jnp.arange(64)[None, :] < _lenS[:, None]
        _validS2 = jnp.arange(512)[None, :] < _lenS2[:, None]
        _causal = jnp.tril(jnp.ones((64, 64), dtype=bool))
        mask_BxS2_bk0 = jnp.logical_not(jnp.broadcast_to(_validS2[:, :], (16, 512)))
        return (x, ctx_1024, mask_BxS2_bk0)
    x, ctx_1024, mask_BxS2_bk0 = _rec_inputs()

    def _L0_xattn_setup():
        import jax, jax.numpy as jnp
        import numpy as np
        B, LQ, LK = (4, 1024, 1024)
        DQ = DK = DV = DH = 512

        def _xavier(key, shape):
            fan_out, fan_in = shape
            bound = float(np.sqrt(6.0 / (fan_in + fan_out)))
            return jax.random.uniform(key, shape, jnp.float32, -bound, bound)
        key = jax.random.key(seed)
        ks = jax.random.split(key, 6)
        query = jax.random.normal(ks[0], (B, LQ, DQ), jnp.float32)
        k_in = jax.random.normal(ks[1], (B, LK, DK), jnp.float32)
        key_mask = jax.random.randint(ks[2], (B, LK), 0, 2).astype(bool)
        Wk = _xavier(ks[3], (2 * DH, DK))
        bk = jnp.zeros((2 * DH,), jnp.float32)
        Wq = _xavier(ks[4], (DH, DQ))
        bq = jnp.zeros((DH,), jnp.float32)
        Wfc = _xavier(ks[5], (DV, DH))
        bfc = jnp.zeros((DV,), jnp.float32)
        return {'query': query, 'key': k_in, 'key_mask': key_mask, 'Wq': Wq, 'bq': bq, 'Wk': Wk, 'bk': bk, 'Wfc': Wfc, 'bfc': bfc}
    _L0_xattn_all = _L0_xattn_setup()
    _L0_xattn_in = {k: v for k, v in _L0_xattn_all.items() if k in ('Wq', 'bq', 'Wk', 'bk', 'Wfc', 'bfc')}
    del _L0_xattn_all

    def _L0_attn_setup():
        import jax, jax.numpy as jnp
        import numpy as np
        H = 16
        BUCKETS = 128
        MAX_REL = 256

        def _log_bucket(rel, bucket_size, max_position):
            mid = bucket_size // 2
            sign = jnp.sign(rel).astype(jnp.float32)
            abs_pos = jnp.where((rel < mid) & (rel > -mid), mid - 1, jnp.abs(rel)).astype(jnp.float32)
            log_pos = jnp.ceil(jnp.log(abs_pos / mid) / np.log((max_position - 1) / mid) * (mid - 1)) + mid
            bucket = jnp.where(abs_pos <= mid, rel.astype(jnp.float32), log_pos * sign)
            return bucket.astype(jnp.int32)

        def _rel_pos(seq_len):
            ids = jnp.arange(seq_len)
            rel = ids[:, None] - ids[None, :]
            return _log_bucket(rel, BUCKETS, MAX_REL)
        key = jax.random.key(seed)
        ks = jax.random.split(key, 16)
        B, S, D = (4, 512, 512)
        K2 = 2 * BUCKETS
        s = 0.02

        def lin(k, din, dout):
            return jax.random.normal(k, (din, dout), jnp.float32) * s
        return {'hidden_states': jax.random.normal(ks[0], (B, S, D), jnp.float32), 'Wq': lin(ks[1], D, D), 'bq': jnp.zeros((D,), jnp.float32), 'Wk': lin(ks[2], D, D), 'bk': jnp.zeros((D,), jnp.float32), 'Wv': lin(ks[3], D, D), 'bv': jnp.zeros((D,), jnp.float32), 'Wo': lin(ks[4], D, D), 'bo': jnp.zeros((D,), jnp.float32), 'rel_emb': jax.random.normal(ks[5], (K2, D), jnp.float32) * s, 'ln_g': jnp.ones((D,), jnp.float32), 'ln_b': jnp.zeros((D,), jnp.float32), 'Wpk': lin(ks[6], D, D), 'bpk': jnp.zeros((D,), jnp.float32), 'Wpq': lin(ks[7], D, D), 'bpq': jnp.zeros((D,), jnp.float32)}
    _L0_attn_all = _L0_attn_setup()
    _L0_attn_in = {k: v for k, v in _L0_attn_all.items() if k in ('Wq', 'bq', 'Wk', 'bk', 'Wv', 'bv', 'Wo', 'bo', 'rel_emb', 'ln_g', 'ln_b', 'Wpk', 'bpk', 'Wpq', 'bpq')}
    del _L0_attn_all

    def _L0_ffn_setup():
        import jax, jax.numpy as jnp
        import numpy as np
        LN_EPS = 1e-05
        NORM_EPS = 1e-12

        def _layernorm(x, gamma, beta):
            mu = x.mean(axis=-1, keepdims=True)
            var = ((x - mu) ** 2).mean(axis=-1, keepdims=True)
            return (x - mu) * jax.lax.rsqrt(var + LN_EPS) * gamma + beta

        def _l2norm(x, axis):
            n = jnp.sqrt((x ** 2).sum(axis=axis, keepdims=True))
            return x / jnp.maximum(n, NORM_EPS)
        key = jax.random.key(seed)
        ks = jax.random.split(key, 4)
        B, N, D, E, S, H = (64, 128, 512, 16, 16, 128)
        x = jax.random.normal(ks[0], (B, N, D), dtype=jnp.float32)
        mu = jax.random.normal(ks[1], (D, E, S), dtype=jnp.float32) / np.sqrt(D)
        w1 = jax.random.normal(ks[2], (E, D, H), dtype=jnp.float32) * np.sqrt(2.0 / D)
        w2 = jax.random.normal(ks[3], (E, H, D), dtype=jnp.float32) * np.sqrt(2.0 / (H + D))
        return {'x': x, 'ln_gamma': jnp.ones((D,), jnp.float32), 'ln_beta': jnp.zeros((D,), jnp.float32), 'mu': mu, 'scale': jnp.ones((1,), jnp.float32), 'w1': w1, 'b1': jnp.zeros((E, H), jnp.float32), 'w2': w2, 'b2': jnp.zeros((E, D), jnp.float32)}
    _L0_ffn_all = _L0_ffn_setup()
    _L0_ffn_in = {k: v for k, v in _L0_ffn_all.items() if k in ('ln_gamma', 'ln_beta', 'mu', 'scale', 'w1', 'b1', 'w2', 'b2')}
    del _L0_ffn_all
    return {'x': x, 'ctx_1024': ctx_1024, 'mask_BxS2_bk0': mask_BxS2_bk0, 'L0_xattn_Wq': _L0_xattn_in['Wq'], 'L0_xattn_bq': _L0_xattn_in['bq'], 'L0_xattn_Wk': _L0_xattn_in['Wk'], 'L0_xattn_bk': _L0_xattn_in['bk'], 'L0_xattn_Wfc': _L0_xattn_in['Wfc'], 'L0_xattn_bfc': _L0_xattn_in['bfc'], 'L0_attn_Wq': _L0_attn_in['Wq'], 'L0_attn_bq': _L0_attn_in['bq'], 'L0_attn_Wk': _L0_attn_in['Wk'], 'L0_attn_bk': _L0_attn_in['bk'], 'L0_attn_Wv': _L0_attn_in['Wv'], 'L0_attn_bv': _L0_attn_in['bv'], 'L0_attn_Wo': _L0_attn_in['Wo'], 'L0_attn_bo': _L0_attn_in['bo'], 'L0_attn_rel_emb': _L0_attn_in['rel_emb'], 'L0_attn_ln_g': _L0_attn_in['ln_g'], 'L0_attn_ln_b': _L0_attn_in['ln_b'], 'L0_attn_Wpk': _L0_attn_in['Wpk'], 'L0_attn_bpk': _L0_attn_in['bpk'], 'L0_attn_Wpq': _L0_attn_in['Wpq'], 'L0_attn_bpq': _L0_attn_in['bpq'], 'L0_ffn_ln_gamma': _L0_ffn_in['ln_gamma'], 'L0_ffn_ln_beta': _L0_ffn_in['ln_beta'], 'L0_ffn_mu': _L0_ffn_in['mu'], 'L0_ffn_scale': _L0_ffn_in['scale'], 'L0_ffn_w1': _L0_ffn_in['w1'], 'L0_ffn_b1': _L0_ffn_in['b1'], 'L0_ffn_w2': _L0_ffn_in['w2'], 'L0_ffn_b2': _L0_ffn_in['b2']}

def reference(x, ctx_1024, mask_BxS2_bk0, L0_xattn_Wq, L0_xattn_bq, L0_xattn_Wk, L0_xattn_bk, L0_xattn_Wfc, L0_xattn_bfc, L0_attn_Wq, L0_attn_bq, L0_attn_Wk, L0_attn_bk, L0_attn_Wv, L0_attn_bv, L0_attn_Wo, L0_attn_bo, L0_attn_rel_emb, L0_attn_ln_g, L0_attn_ln_b, L0_attn_Wpk, L0_attn_bpk, L0_attn_Wpq, L0_attn_bpq, L0_ffn_ln_gamma, L0_ffn_ln_beta, L0_ffn_mu, L0_ffn_scale, L0_ffn_w1, L0_ffn_b1, L0_ffn_w2, L0_ffn_b2):
    import jax
    import jax.numpy as jnp

    def _L0_xattn_ref(query, key, key_mask, Wq, bq, Wk, bk, Wfc, bfc):
        import jax, jax.numpy as jnp
        import numpy as np
        B, LQ, LK = (4, 1024, 1024)
        DQ = DK = DV = DH = 512

        def _xavier(key, shape):
            fan_out, fan_in = shape
            bound = float(np.sqrt(6.0 / (fan_in + fan_out)))
            return jax.random.uniform(key, shape, jnp.float32, -bound, bound)
        bs, timesteps, _ = key.shape
        dim = DH
        q = query @ Wq.T + bq
        c = (key @ Wk.T + bk).reshape(bs, timesteps, 2, dim)
        k = c[:, :, 0]
        v = c[:, :, 1]
        scores = jnp.einsum('bqd,bkd->bqk', q, k)
        scores = jnp.where(key_mask[:, None, :], -jnp.inf, scores)
        attn = jax.nn.softmax(scores, axis=-1)
        out = jnp.einsum('bqk,bkd->bqd', attn, v)
        out = out @ Wfc.T + bfc
        return out

    def _L0_attn_ref(hidden_states, Wq, bq, Wk, bk, Wv, bv, Wo, bo, rel_emb, ln_g, ln_b, Wpk, bpk, Wpq, bpq):
        import jax, jax.numpy as jnp
        import numpy as np
        H = 16
        BUCKETS = 128
        MAX_REL = 256

        def _log_bucket(rel, bucket_size, max_position):
            mid = bucket_size // 2
            sign = jnp.sign(rel).astype(jnp.float32)
            abs_pos = jnp.where((rel < mid) & (rel > -mid), mid - 1, jnp.abs(rel)).astype(jnp.float32)
            log_pos = jnp.ceil(jnp.log(abs_pos / mid) / np.log((max_position - 1) / mid) * (mid - 1)) + mid
            bucket = jnp.where(abs_pos <= mid, rel.astype(jnp.float32), log_pos * sign)
            return bucket.astype(jnp.int32)

        def _rel_pos(seq_len):
            ids = jnp.arange(seq_len)
            rel = ids[:, None] - ids[None, :]
            return _log_bucket(rel, BUCKETS, MAX_REL)
        B, S, D = hidden_states.shape
        hd = D // H
        span = BUCKETS

        def shape_heads(x):
            return x.reshape(*x.shape[:-1], H, hd).swapaxes(-2, -3)
        q = shape_heads(hidden_states @ Wq + bq)
        k = shape_heads(hidden_states @ Wk + bk)
        v = shape_heads(hidden_states @ Wv + bv)
        scale_factor = 3
        scores = jnp.einsum('bhsd,bhkd->bhsk', q, k) / jnp.sqrt(jnp.float32(hd * scale_factor))
        mu = rel_emb.mean(-1, keepdims=True)
        var = rel_emb.var(-1, keepdims=True)
        re = (rel_emb - mu) / jnp.sqrt(var + 1e-05) * ln_g + ln_b
        pos_k = shape_heads(re @ Wpk + bpk)
        pos_q = shape_heads(re @ Wpq + bpq)
        rel = _rel_pos(S)
        bias_scale = jnp.sqrt(jnp.float32(hd * 2))
        c2p = jnp.einsum('bhsd,hkd->bhsk', q, pos_k)
        c2p_idx = jnp.clip(rel + span, 0, 2 * span - 1)
        c2p = jnp.take_along_axis(c2p, jnp.broadcast_to(c2p_idx[None, None], (B, H, S, S)), axis=-1)
        scores = scores + c2p / bias_scale
        p2c = jnp.einsum('bhsd,hkd->bhsk', k, pos_q)
        p2c_idx = jnp.clip(-rel + span, 0, 2 * span - 1)
        p2c = jnp.take_along_axis(p2c, jnp.broadcast_to(p2c_idx[None, None], (B, H, S, S)), axis=-1)
        scores = scores + p2c.swapaxes(-1, -2) / bias_scale
        probs = jax.nn.softmax(scores.astype(jnp.float32), axis=-1).astype(q.dtype)
        ctx = jnp.einsum('bhsk,bhkd->bhsd', probs, v)
        ctx = ctx.swapaxes(1, 2).reshape(B, S, D)
        return ctx @ Wo + bo

    def _L0_ffn_ref(x, ln_gamma, ln_beta, mu, scale, w1, b1, w2, b2):
        import jax, jax.numpy as jnp
        import numpy as np
        LN_EPS = 1e-05
        NORM_EPS = 1e-12

        def _layernorm(x, gamma, beta):
            mu = x.mean(axis=-1, keepdims=True)
            var = ((x - mu) ** 2).mean(axis=-1, keepdims=True)
            return (x - mu) * jax.lax.rsqrt(var + LN_EPS) * gamma + beta

        def _l2norm(x, axis):
            n = jnp.sqrt((x ** 2).sum(axis=axis, keepdims=True))
            return x / jnp.maximum(n, NORM_EPS)
        B, N, D = x.shape
        _, E, S = mu.shape
        xn = _layernorm(x, ln_gamma, ln_beta)
        x_unit = _l2norm(xn, axis=-1)
        mu_unit = _l2norm(mu, axis=0)
        logits = jnp.einsum('bnd,des->bnes', x_unit * scale, mu_unit)
        dispatch = jax.nn.softmax(logits, axis=1)
        combine = jax.nn.softmax(logits.reshape(B, N, E * S), axis=-1).reshape(B, N, E, S)
        slot_in = jnp.einsum('bnd,bnes->besd', xn, dispatch)
        h = jax.nn.gelu(jnp.einsum('besd,edh->besh', slot_in, w1) + b1[None, :, None, :], approximate=False)
        slot_out = jnp.einsum('besh,ehd->besd', h, w2) + b2[None, :, None, :]
        out = jnp.einsum('besd,bnes->bnd', slot_out, combine)
        return out
    x = x + _L0_xattn_ref(_layernorm(x, axis=-1), ctx_1024, mask_BxS2_bk0, L0_xattn_Wq, L0_xattn_bq, L0_xattn_Wk, L0_xattn_bk, L0_xattn_Wfc, L0_xattn_bfc)
    x = x + _L0_attn_ref(_layernorm(x, axis=-1), L0_attn_Wq, L0_attn_bq, L0_attn_Wk, L0_attn_bk, L0_attn_Wv, L0_attn_bv, L0_attn_Wo, L0_attn_bo, L0_attn_rel_emb, L0_attn_ln_g, L0_attn_ln_b, L0_attn_Wpk, L0_attn_bpk, L0_attn_Wpq, L0_attn_bpq)
    x = x + _L0_ffn_ref(_layernorm(x, axis=-1), L0_ffn_ln_gamma, L0_ffn_ln_beta, L0_ffn_mu, L0_ffn_scale, L0_ffn_w1, L0_ffn_b1, L0_ffn_w2, L0_ffn_b2)
    return x

_drawn_inputs = setup_inputs


def setup_inputs(seed=0):
    import zlib

    import numpy as np

    out = dict(_drawn_inputs(seed))
    spreads = {'L0_xattn_bq': (0.0, 0.1),
     'L0_xattn_bk': (0.0, 0.1),
     'L0_xattn_bfc': (0.0, 0.1),
     'L0_attn_bq': (0.0, 0.8),
     'L0_attn_bk': (0.0, 0.8),
     'L0_attn_bv': (0.0, 0.1),
     'L0_attn_bo': (0.0, 0.1),
     'L0_attn_ln_g': (1.0, 0.6),
     'L0_attn_ln_b': (0.0, 0.8),
     'L0_attn_bpk': (0.0, 0.8),
     'L0_attn_bpq': (0.0, 0.8),
     'L0_ffn_ln_gamma': (1.0, 0.6),
     'L0_ffn_ln_beta': (0.0, 0.8),
     'L0_ffn_b1': (0.0, 0.8),
     'L0_ffn_b2': (0.0, 0.474)}
    factors = {'L0_attn_Wq': 8.0,
     'L0_attn_Wk': 8.0,
     'L0_attn_rel_emb': 8.0,
     'L0_attn_Wpk': 8.0,
     'L0_attn_Wpq': 8.0,
     'L0_ffn_mu': 8.0}
    for name, (base, spread) in spreads.items():
        noise = np.random.default_rng([zlib.crc32(name.encode()), seed]).standard_normal(out[name].shape)
        drawn = base * np.exp(spread * noise) if base else spread * noise
        out[name] = jnp.asarray(drawn.astype(out[name].dtype))
    for name, factor in factors.items():
        out[name] = (out[name] * factor).astype(out[name].dtype)
    return out
```

```python
from contextlib import ExitStack

import concourse.bass as bass
from concourse import mybir

ALU = mybir.AluOpType
ACT = mybir.ActivationFunctionType
F32 = mybir.dt.float32
U8 = mybir.dt.uint8
U32 = mybir.dt.uint32
AX_X = mybir.AxisListType.X

P = 128
B = 16
S = 64
D = 512
NC = D // P
TOK = B * S
T = TOK // P
KEYS = 512
KB = KEYS // P
H = 16
HD = D // H
G = H // 4
SPAN = 128
R = 2 * S
IB = 16
W = 80
NI = S // IB
E = 16
SL = 16
ES = E * SL
HID = 128
EG = E // 4
LN_EPS = 1e-5
MASKED = -3e38
NORM_EPS = 1e-12
ATT_SCALE = float((HD * 3) ** -0.5)
POS_SCALE = float((HD * 3) ** 0.5 / (HD * 2) ** 0.5)


def build(nc, a, out):
    with ExitStack() as whole:
        def sem(name):
            return whole.enter_context(nc.semaphore(name))

        def buffers(stack):
            return lambda name, shape, dt=F32: stack.enter_context(nc.sbuf_tensor(name, shape, dt))

        keep = buffers(whole)
        bank = [whole.enter_context(nc.psum_tensor(f"bank{i}", [P, 512], F32)) for i in range(8)]
        X = keep("X", [P, T, D])
        ident = keep("ident", [P, P])
        ones = keep("ones", [P, P])
        eps = keep("eps", [P, 1])

        ident_ready = sem("ident_ready")
        scr_c2p = nc.dram_tensor("scr_c2p", [TOK, W * H], F32, kind="Internal").ap()
        scr_p2c = nc.dram_tensor("scr_p2c", [TOK, W * H], F32, kind="Internal").ap()

        def transposes(pe, dst, src, n):
            for c in range(n):
                last = pe.transpose(dst[:, c * P:(c + 1) * P], src[:, c * P:(c + 1) * P], ident[:, :])
            return last

        ab = ExitStack()
        with ab:
            sb = buffers(ab)
            M2 = sb("M2", [P, NC, D])
            out_bias = sb("out_bias", [P, D])
            AT = sb("AT", [P, NC, TOK])
            a01 = ExitStack()
            with a01:
                sb01 = buffers(a01)
                QT = sb01("QT", [P, NC, TOK])
                ctx = [sb01(f"ctx{u}", [P, 2, KB, D]) for u in range(2)]
                mask = sb01("mask", [P, T, KEYS // 4], U32)
                s_q = sb01("s_q", [P, T])
                ctx_loaded = [sem(f"ctx_loaded{u}") for u in range(2)]
                mask_loaded = sem("mask_loaded")

                def load_ctx(sp, t):
                    for b in range(2):
                        sp.dma_start(ctx[t % 2][:, b, :, :],
                                     a["ctx"][2 * t + b].rearrange("(p k) d -> p k d", k=KB)
                                     ).then_inc(ctx_loaded[t % 2], 16)

                with ExitStack() as st:
                    phase_queries(nc, a, st, sem, buffers(st), bank, X, ident, ones, eps, ident_ready,
                                  transposes, M2, out_bias, QT, mask, s_q, load_ctx, mask_loaded)
                with ExitStack() as st:
                    phase_context(nc, a, st, sem, buffers(st), bank, ident, transposes, QT, ctx, mask, s_q,
                                  AT, load_ctx, ctx_loaded, mask_loaded)
            bc = ExitStack()
            sbc = buffers(bc)
            with bc:
                XT = sbc("XT", [P, NC, TOK])
                QTh = sbc("QTh", [P, G, 2, NI, 8, IB])
                KTh = sbc("KTh", [P, G, 2, NI, 8, IB])
                with ExitStack() as st:
                    phase_projections(nc, a, st, sem, buffers(st), bank, X, ident, eps, transposes,
                                      M2, out_bias, AT, XT, QTh, KTh, scr_c2p, scr_p2c)
                with ExitStack() as st:
                    phase_attention(nc, a, st, sem, buffers(st), bank, ident, transposes,
                                    XT, QTh, KTh, AT, scr_c2p, scr_p2c)
            with ExitStack() as de:
                sde = buffers(de)
                XN = sde("XN", [P, T, D])
                XUT = sde("XUT", [P, NC, TOK])
                MU = sde("MU", [P, NC, ES])
                with ExitStack() as st:
                    phase_norms(nc, a, st, sem, buffers(st), bank, X, ident, ones, eps, transposes,
                                AT, XN, XUT, MU)
                with ExitStack() as st:
                    phase_routing_and_experts(nc, a, st, sem, buffers(st), bank, X, ident, transposes,
                                              XN, XUT, MU, AT, M2, out)


def phase_queries(nc, a, st, sem, sb, bank, X, ident, ones, eps, ident_ready, transposes,
                  M2, out_bias, QT, mask, s_q, load_ctx, mask_loaded):
    Wq = sb("Wq", [P, NC, D])
    Wk = sb("Wk", [P, NC, D])
    Wv = sb("Wv", [P, NC, D])
    WfcT = sb("WfcT", [P, NC, D])
    cols = sb("xattn_bias_cols", [P, 3, NC])
    spread = sb("xattn_bias_spread", [P, 3, NC, P])
    bfc = sb("bfc", [P, D])
    M1 = sb("M1", [P, NC, D])
    xn = [sb(f"xn{u}", [P, D]) for u in range(2)]
    XNT = sb("XNT", [P, NC, TOK])
    U = sb("U", [P, D])
    prod = sb("prod_q", [P, D])
    prod2 = sb("prod_q2", [P, P])
    qcol = sb("qcol", [P, NC])
    const = sb("const", [P, 1])
    stats = sb("stats", [P, T, 6])
    mv = sb("mv", [P, T, 2])
    std = sb("std", [P, T])
    rstd = sb("rstd", [P, T])

    x_loaded = sem("x_loaded")
    qk_loaded = sem("qk_loaded")
    vo_loaded = sem("vo_loaded")
    bias_loaded = sem("bias_loaded")
    spread_ready = sem("spread_ready")
    fold_done = sem("fold_done")
    m1_ready = sem("m1_ready")
    u_ready = sem("u_ready")
    qcol_ready = sem("qcol_ready")
    c_ready = sem("c_ready")
    stats_ready = sem("stats_ready")
    mv_ready = sem("mv_ready")
    std_ready = sem("std_ready")
    rstd_ready = sem("rstd_ready")
    xn_ready = sem("xn_ready")
    sq_ready = sem("sq_ready")
    xnT_turned = sem("xnT_turned")
    xnT_ready = sem("xnT_ready")
    qt_done = sem("qt_done")
    qt_read = [sem("qt_read_dve"), sem("qt_read_act")]
    m2_done = sem("m2_done")
    m2_ready = sem("m2_ready")
    out_bias_ready = sem("out_bias_ready")

    with nc.Block() as block:
        @block.sync
        def _(sp):
            sp.dma_start(X[:, :, :], a["x"].rearrange("(t p) d -> p t d", p=P)).then_inc(x_loaded, 16)
            sp.dma_start(Wq[:, :, :], a["xWq"].rearrange("(c p) n -> p c n", p=P)).then_inc(qk_loaded, 16)
            sp.dma_start(Wk[:, :, :], a["xWk"][0:D].rearrange("(c p) n -> p c n", p=P)).then_inc(qk_loaded, 16)
            sp.dma_start(cols[:, :, :], a["xcols"]).then_inc(bias_loaded, 16)
            sp.dma_start(bfc[:, :], a["xbfc"].broadcast_to([P, D])).then_inc(bias_loaded, 16)
            sp.dma_start(Wv[:, :, :], a["xWk"][D:2 * D].rearrange("(c p) n -> p c n", p=P)).then_inc(vo_loaded, 16)
            sp.dma_start(WfcT[:, :, :], a["xWfcT"].rearrange("(c p) n -> p c n", p=P)).then_inc(vo_loaded, 16)
            for b in range(2):
                sp.dma_start(mask[64 * b:64 * b + 64, :, :],
                             bass.AP(a["mask"].tensor, b * KEYS // 4, [[0, 64], [2 * KEYS // 4, T], [1, KEYS // 4]])
                             ).then_inc(mask_loaded, 16)
            load_ctx(sp, 0)
            load_ctx(sp, 1)

        @block.gpsimd
        def _(pool):
            pool.memset(ident[:, :], 0.0).then_inc(ident_ready, 1)
            pool.memset(ones[:, :], 1.0).then_inc(ident_ready, 1)
            pool.memset(eps[:, :], LN_EPS).then_inc(ident_ready, 1)
            pool.wait_ge(ident_ready, 3)
            pool.affine_select(out=ident[:, :], in_=ident[:, :], compare_op=ALU.not_equal, fill=1.0,
                               base=0, pattern=[[-1, P]], channel_multiplier=1).then_inc(ident_ready, 1)

        @block.tensor
        def _(pe):
            pe.wait_ge(spread_ready, 3 * NC)
            pe.wait_ge(qk_loaded, 32)
            for c in range(NC):
                last = pe.matmul(bank[2][:, :], spread[:, 1, c, :], Wq[:, c, :], start=(c == 0), stop=(c == NC - 1))
            last.then_inc(fold_done, 1)
            for c in range(NC):
                last = pe.matmul(bank[3][:, :], spread[:, 0, c, :], Wk[:, c, :], start=(c == 0), stop=(c == NC - 1))
            last.then_inc(fold_done, 1)
            for c in range(NC):
                last = pe.matmul(bank[4][:, 0:2], spread[:, 1, c, :], spread[:, 0, c, 0:2],
                                 start=(c == 0), stop=(c == NC - 1))
            last.then_inc(fold_done, 1)
            for i in range(NC):
                if i >= 2:
                    pe.wait_ge(m1_ready, i - 1)
                for c in range(NC):
                    last = pe.matmul(bank[i % 2][:, :], Wq[:, c, i * P:(i + 1) * P], Wk[:, c, :],
                                     start=(c == 0), stop=(c == NC - 1))
                last.then_inc(fold_done, 1)
            pe.wait_ge(ident_ready, 4)
            for t in range(T):
                pe.wait_ge(xn_ready, t + 1)
                if t >= 2:
                    pe.wait_ge(xnT_ready, t - 1)
                transposes(pe, bank[6 + t % 2], xn[t % 2], NC).then_inc(xnT_turned, 1)
            pe.wait_ge(m1_ready, NC)
            pe.wait_ge(u_ready, 1)
            pe.wait_ge(qcol_ready, NC)
            for half in range(2):
                pe.wait_ge(xnT_ready, 4 * (half + 1))
                for m in range(NC):
                    if half:
                        pe.wait_ge(qt_read[m % 2], m // 2 + 1)
                    for c in range(NC):
                        last = pe.matmul(bank[m][:, :], M1[:, c, m * P:(m + 1) * P],
                                         XNT[:, c, 512 * half:512 * half + 512],
                                         start=(c == 0), stop=(c == NC - 1))
                    last.then_inc(qt_done, 1)
            pe.wait_ge(vo_loaded, 32)
            for c in range(NC):
                last = pe.matmul(bank[5][:, :], spread[:, 2, c, :], WfcT[:, c, :], start=(c == 0), stop=(c == NC - 1))
            last.then_inc(m2_done, 1)
            for i in range(NC):
                if i < 2:
                    pe.wait_ge(xnT_ready, T)
                else:
                    pe.wait_ge(m2_ready, i - 1)
                for c in range(NC):
                    last = pe.matmul(bank[6 + i % 2][:, :], Wv[:, c, i * P:(i + 1) * P], WfcT[:, c, :],
                                     start=(c == 0), stop=(c == NC - 1))
                last.then_inc(m2_done, 1)

        @block.scalar
        def _(act):
            act.wait_ge(mv_ready, T)
            act.wait_ge(ident_ready, 3)
            act.activation(std[:, :], mv[:, :, 1], ACT.Sqrt, bias=eps[:, :]).then_inc(std_ready, 1)
            for i in range(NC):
                act.wait_ge(fold_done, 4 + i)
                act.activation(M1[:, i, :], bank[i % 2][:, :], ACT.Copy).then_inc(m1_ready, 1)
            for t in range(T):
                act.wait_ge(xnT_turned, t + 1)
                act.activation(XNT[:, :, t * P:(t + 1) * P], bank[6 + t % 2][:, :].rearrange("p (c n) -> p c n", c=NC),
                               ACT.Copy).then_inc(xnT_ready, 1)
            act.wait_ge(qcol_ready, NC)
            for half in range(2):
                for m in (1, 3):
                    act.wait_ge(qt_done, 4 * half + m + 1)
                    act.activation(QT[:, m, 512 * half:512 * half + 512], bank[m][:, :], ACT.Identity,
                                   bias=qcol[:, m:m + 1]).then_inc(qt_read[1], 1)
            for i in range(NC):
                act.wait_ge(m2_done, 2 + i)
                act.activation(M2[:, i, :], bank[6 + i % 2][:, :], ACT.Copy).then_inc(m2_ready, 1)

        @block.vector
        def _(dve):
            dve.wait_ge(bias_loaded, 32)
            dve.wait_ge(ident_ready, 4)
            for k in range(3):
                for c in range(NC):
                    dve.tensor_scalar(spread[:, k, c, :], ones[:, :], cols[:, k, c:c + 1], None,
                                      ALU.mult).then_inc(spread_ready, 1)
            dve.wait_ge(x_loaded, 16)
            for t in range(T):
                dve.bn_stats(stats[:, t, :], X[:, t, :]).then_inc(stats_ready, 1)
            for t in range(T):
                dve.wait_ge(stats_ready, t + 1)
                dve.bn_aggr(mv[:, t, :], stats[:, t, :]).then_inc(mv_ready, 1)
            dve.wait_ge(std_ready, 1)
            dve.reciprocal(rstd[:, :], std[:, :]).then_inc(rstd_ready, 1)
            dve.wait_ge(fold_done, 1)
            dve.tensor_copy(U[:, :], bank[2][:, :]).then_inc(u_ready, 1)
            dve.wait_ge(fold_done, 2)
            for m in range(NC):
                if m:
                    dve.wait_ge(qcol_ready, m)
                dve.tensor_tensor_reduce(out=prod2[:, :], in0=bank[3][:, m * P:(m + 1) * P], in1=ident[:, :],
                                         scale=1.0, scalar=0.0, op0=ALU.mult, op1=ALU.add,
                                         accum_out=qcol[:, m:m + 1]).then_inc(qcol_ready, 1)
            dve.wait_ge(fold_done, 3)
            dve.tensor_copy(const[:, :], bank[4][:, 0:1]).then_inc(c_ready, 1)
            dve.wait_ge(rstd_ready, 1)
            dve.wait_ge(u_ready, 1)
            for t in range(T):
                if t >= 2:
                    dve.wait_ge(xnT_turned, t - 1)
                dve.tensor_scalar(xn[t % 2][:, :], X[:, t, :], mv[:, t, 0:1], rstd[:, t:t + 1],
                                  ALU.subtract, ALU.mult).then_inc(xn_ready, 1)
                dve.wait_ge(xn_ready, t + 1)
                if t:
                    dve.wait_ge(sq_ready, t)
                dve.tensor_tensor_reduce(out=prod[:, :], in0=xn[t % 2][:, :], in1=U[:, :],
                                         scale=1.0, scalar=0.0, op0=ALU.mult, op1=ALU.add,
                                         accum_out=s_q[:, t:t + 1]).then_inc(sq_ready, 1)
            dve.wait_ge(sq_ready, T)
            dve.wait_ge(c_ready, 1)
            dve.tensor_scalar(s_q[:, :], s_q[:, :], const[:, :], None, ALU.add).then_inc(sq_ready, 1)
            for half in range(2):
                for m in (0, 2):
                    dve.wait_ge(qt_done, 4 * half + m + 1)
                    dve.tensor_scalar(QT[:, m, 512 * half:512 * half + 512], bank[m][:, :], qcol[:, m:m + 1], None,
                                      ALU.add).then_inc(qt_read[0], 1)
            dve.wait_ge(m2_done, 1)
            dve.tensor_tensor(out_bias[:, :], bank[5][:, :], bfc[:, :], ALU.add).then_inc(out_bias_ready, 1)


def phase_context(nc, a, st, sem, sb, bank, ident, transposes, QT, ctx, mask, s_q,
                  AT, load_ctx, ctx_loaded, mask_loaded):
    ctxT = [sb(f"ctxT{u}", [P, 2, NC, KEYS]) for u in range(2)]
    mask_bias = [sb(f"mask_bias{u}", [P, KEYS]) for u in range(2)]
    sm = [sb(f"sm{u}", [P, KEYS]) for u in range(2)]
    prob = [sb(f"prob{u}", [P, KEYS]) for u in range(2)]
    probT = [sb(f"probT{u}", [P, KB, P]) for u in range(2)]
    att = [sb(f"att{u}", [P, D]) for u in range(2)]
    smax = sb("smax", [P, T])
    smax2 = sb("smax2", [P, T])
    nbias = sb("nbias", [P, T])
    rsum = sb("rsum", [P, T])
    rrec = sb("rrec", [P, T])

    turn_banks, s_bank, p_bank, o_bank, at_bank = bank[0:4], bank[4], bank[5], bank[6], bank[7]

    turned = sem("ctx_turned")
    turned_read = [sem("ctx_turned_read_dve"), sem("ctx_turned_read_act")]
    mask_ready = sem("mask_ready")
    scores_done = sem("scores_done")
    sm_ready = sem("sm_ready")
    smax_ready = sem("smax_ready")
    smax2_ready = sem("smax2_ready")
    nbias_ready = sem("nbias_ready")
    prob_ready = sem("prob_ready")
    rrec_ready = sem("rrec_ready")
    prob_turned = sem("prob_turned")
    probT_ready = sem("probT_ready")
    pv_done = sem("pv_done")
    att_ready = sem("att_ready")
    att_turned = sem("att_turned")
    AT_ready = sem("AT_ready")
    NB = 2 * NC

    with nc.Block() as block:
        @block.sync
        def _(sp):
            for t in range(2, T):
                sp.wait_ge(pv_done, t - 1)
                load_ctx(sp, t)

        @block.gpsimd
        def _(pool):
            pool.wait_ge(mask_loaded, 32)
            for t in range(T):
                if t >= 2:
                    pool.wait_ge(sm_ready, t - 1)
                pool.tensor_scalar(mask_bias[t % 2][:, :], mask[:, t, :].bitcast(U8), MASKED, None,
                                   ALU.mult).then_inc(mask_ready, 1)

        @block.tensor
        def _(pe):
            def turn_context(t):
                pe.wait_ge(ctx_loaded[t % 2], 32 * (t // 2 + 1))
                for i in range(NB):
                    b, c = i // NC, i % NC
                    n = (NB * t + i - 4) // 2 + 1
                    if NB * t + i >= 4:
                        pe.wait_ge(turned_read[i % 2], n)
                    for k in range(KB):
                        last = pe.transpose(turn_banks[i % 4][:, k * P:(k + 1) * P],
                                            ctx[t % 2][:, b, k, c * P:(c + 1) * P], ident[:, :])
                    last.then_inc(turned, 1)

            def scores(t):
                if t:
                    pe.wait_ge(sm_ready, t)
                for e in range(2):
                    pe.wait_ge(turned_read[e], 4 * (t + 1))
                for c in range(NC):
                    for b in range(2):
                        last = pe.matmul(s_bank[64 * b:64 * b + 64, :],
                                         QT[:, c, t * P + 64 * b:t * P + 64 * b + 64],
                                         ctxT[t % 2][:, b, c, :], start=(c == 0), stop=(c == NC - 1))
                last.then_inc(scores_done, 1)

            def turn_probs(t):
                pe.wait_ge(prob_ready, t + 1)
                if t:
                    pe.wait_ge(probT_ready, t)
                transposes(pe, p_bank, prob[t % 2], KB).then_inc(prob_turned, 1)

            def attend(t):
                pe.wait_ge(probT_ready, t + 1)
                if t:
                    pe.wait_ge(att_ready, t)
                for k in range(KB):
                    for b in range(2):
                        last = pe.matmul(o_bank[64 * b:64 * b + 64, :],
                                         probT[t % 2][:, k, 64 * b:64 * b + 64],
                                         ctx[t % 2][:, b, k, :], start=(k == 0), stop=(k == KB - 1))
                last.then_inc(pv_done, 1)

            def turn_attended(t):
                pe.wait_ge(att_ready, t + 1)
                if t:
                    pe.wait_ge(AT_ready, t)
                transposes(pe, at_bank, att[t % 2], NC).then_inc(att_turned, 1)

            for t in range(T + 2):
                if t < T:
                    turn_context(t)
                if t >= 2:
                    turn_attended(t - 2)
                if 1 <= t <= T:
                    turn_probs(t - 1)
                if t < T:
                    scores(t)
                if 1 <= t <= T:
                    attend(t - 1)

        @block.vector
        def _(dve):
            for t in range(T + 1):
                if t < T:
                    if t >= 2:
                        dve.wait_ge(scores_done, t - 1)
                    for i in range(0, NB, 2):
                        dve.wait_ge(turned, NB * t + i + 1)
                        dve.tensor_copy(ctxT[t % 2][:, i // NC, i % NC, :], turn_banks[i % 4][:, :]
                                        ).then_inc(turned_read[0], 1)
                    dve.wait_ge(scores_done, t + 1)
                    dve.wait_ge(mask_ready, t + 1)
                    if t >= 2:
                        dve.wait_ge(prob_ready, t - 1)
                    dve.tensor_tensor(sm[t % 2][:, :], s_bank[:, :], mask_bias[t % 2][:, :], ALU.add
                                      ).then_inc(sm_ready, 1)
                    dve.wait_ge(sm_ready, t + 1)
                    dve.tensor_reduce(smax[:, t:t + 1], sm[t % 2][:, :], AX_X, ALU.max).then_inc(smax_ready, 1)
                    dve.wait_ge(smax_ready, t + 1)
                    dve.tensor_tensor(smax2[:, t:t + 1], smax[:, t:t + 1], s_q[:, t:t + 1], ALU.add
                                      ).then_inc(smax2_ready, 1)
                    dve.wait_ge(smax2_ready, t + 1)
                    dve.tensor_tensor(nbias[:, t:t + 1], s_q[:, t:t + 1], smax2[:, t:t + 1], ALU.subtract
                                      ).then_inc(nbias_ready, 1)
                if t >= 1:
                    dve.wait_ge(prob_ready, t)
                    dve.reciprocal(rrec[:, t - 1:t], rsum[:, t - 1:t]).then_inc(rrec_ready, 1)
                    dve.wait_ge(rrec_ready, t)
                    dve.wait_ge(pv_done, t)
                    if t >= 3:
                        dve.wait_ge(att_turned, t - 2)
                    dve.tensor_scalar(att[(t - 1) % 2][:, :], o_bank[:, :], rrec[:, t - 1:t], None, ALU.mult
                                      ).then_inc(att_ready, 1)

        @block.scalar
        def _(act):
            for t in range(T + 2):
                if t < T:
                    if t >= 2:
                        act.wait_ge(scores_done, t - 1)
                    for i in range(1, NB, 2):
                        act.wait_ge(turned, NB * t + i + 1)
                        act.activation(ctxT[t % 2][:, i // NC, i % NC, :], turn_banks[i % 4][:, :], ACT.Copy
                                       ).then_inc(turned_read[1], 1)
                if t >= 2:
                    act.wait_ge(att_turned, t - 1)
                    act.activation(AT[:, :, (t - 2) * P:(t - 1) * P],
                                   at_bank[:, :].rearrange("p (c n) -> p c n", c=NC), ACT.Copy).then_inc(AT_ready, 1)
                if 1 <= t <= T:
                    act.wait_ge(prob_turned, t)
                    if t >= 3:
                        act.wait_ge(pv_done, t - 2)
                    act.activation(probT[(t - 1) % 2][:, :, :], p_bank[:, :].rearrange("p (k n) -> p k n", k=KB),
                                   ACT.Copy).then_inc(probT_ready, 1)
                if t < T:
                    act.wait_ge(nbias_ready, t + 1)
                    if t >= 2:
                        act.wait_ge(prob_turned, t - 1)
                    act.activation(prob[t % 2][:, :], sm[t % 2][:, :], ACT.Exp, bias=nbias[:, t:t + 1],
                                   accum_out=rsum[:, t:t + 1]).then_inc(prob_ready, 1)


def phase_projections(nc, a, st, sem, sb, bank, X, ident, eps, transposes,
                      M2, out_bias, AT, XT, QTh, KTh, scr_c2p, scr_p2c):
    Wq = sb("hWq", [P, NC, D])
    Wk = sb("hWk", [P, NC, D])
    Wpk = sb("Wpk", [P, NC, D])
    Wpq = sb("Wpq", [P, NC, D])
    hcols = sb("hcols", [P, 4, G])
    rel = sb("rel", [P, D])
    reln = sb("reln", [P, D])
    ln_g = sb("ln_g", [P, D])
    ln_b = sb("ln_b", [P, D])
    relT = sb("relT", [P, NC, P])
    pos = [sb(f"pos{k}", [P, G, R]) for k in range(2)]
    pos_bd = [sb(f"pos_bd{k}", [P, G, R, 4]) for k in range(2)]
    xn = [sb(f"hxn{u}", [P, D]) for u in range(2)]
    qp = [sb(f"qp{u}", [P, W * H]) for u in range(3)]
    stats = sb("hstats", [P, T + 1, 6])
    mv = sb("hmv", [P, T + 1, 2])
    std = sb("hstd", [P, T + 1])
    rstd = sb("hrstd", [P, T + 1])

    pos_loaded = sem("pos_loaded")
    posw_loaded = sem("posw_loaded")
    hw_loaded = sem("hw_loaded")
    x_biased = sem("x_biased")
    bd_zero = sem("bd_zero")
    x1_done = sem("x1_done")
    x1_ready = sem("x1_ready")
    stats_ready = sem("hstats_ready")
    mv_ready = sem("hmv_ready")
    std_ready = sem("hstd_ready")
    rstd_ready = sem("hrstd_ready")
    rel_step = sem("rel_step")
    rel_turned = sem("rel_turned")
    relT_ready = sem("relT_ready")
    pos_done = sem("pos_done")
    pos_ready = sem("pos_ready")
    bd_ready = sem("bd_ready")
    xn_ready = sem("hxn_ready")
    xn_turned = sem("hxn_turned")
    XT_ready = sem("XT_ready")
    qk_done = sem("qk_done")
    qk_read = [sem("qk_read_dve"), sem("qk_read_act")]
    qp_done = sem("qp_done")
    qp_read = [sem("qp_read_dve"), sem("qp_read_act")]
    qp_stored = [sem(f"qp_stored{u}") for u in range(3)]
    NT = 2 * NI
    NQ = 2 * NT

    def tile_tokens(M, g, n):
        return M[:, g, (n % NT) // NI, n % NI, :, :]

    with nc.Block() as block:
        @block.sync
        def _(sp):
            sp.dma_start(rel[:, :], a["rel"][SPAN - S:SPAN + S]).then_inc(pos_loaded, 16)
            sp.dma_start(ln_g[:, :], a["ln_g"].broadcast_to([P, D])).then_inc(pos_loaded, 16)
            sp.dma_start(ln_b[:, :], a["ln_b"].broadcast_to([P, D])).then_inc(pos_loaded, 16)
            sp.dma_start(hcols[:, :, :], a["hcols"]).then_inc(pos_loaded, 16)
            sp.dma_start(Wpk[:, :, :], a["Wpk"].rearrange("(c p) n -> p c n", p=P)).then_inc(posw_loaded, 16)
            sp.dma_start(Wpq[:, :, :], a["Wpq"].rearrange("(c p) n -> p c n", p=P)).then_inc(posw_loaded, 16)
            sp.dma_start(Wq[:, :, :], a["hWq"].rearrange("(c p) n -> p c n", p=P)).then_inc(hw_loaded, 16)
            sp.dma_start(Wk[:, :, :], a["hWk"].rearrange("(c p) n -> p c n", p=P)).then_inc(hw_loaded, 16)
            for n in range(NQ):
                for e in range(2):
                    sp.wait_ge(qp_read[e], 2 * (n + 1))
                half, i = (n % NT) // NI, n % NI
                scr = scr_c2p if n < NT else scr_p2c
                dst = scr.rearrange("(b i) w -> b i w", b=B)[8 * half:8 * half + 8, IB * i:IB * i + IB, :]
                sp.dma_start(dst, qp[n % 3][:, :]).then_inc(qp_stored[n % 3], 16)
            for u in range(3):
                sp.wait_ge(qp_stored[u], 16 * len(range(u, NQ, 3)))

        @block.gpsimd
        def _(pool):
            for t in range(T):
                pool.tensor_tensor(X[:, t, :], X[:, t, :], out_bias[:, :], ALU.add).then_inc(x_biased, 1)
            for k in range(2):
                pool.memset(pos_bd[k][:, :, :, :], 0.0).then_inc(bd_zero, 1)

        @block.tensor
        def _(pe):
            pe.wait_ge(rel_step, 4)
            transposes(pe, bank[7], reln, NC).then_inc(rel_turned, 1)
            pe.wait_ge(relT_ready, 1)
            pe.wait_ge(posw_loaded, 32)
            for k, Wp in enumerate((Wpk, Wpq)):
                for g in range(G):
                    for c in range(NC):
                        last = pe.matmul(bank[5 + k][:, g * R:(g + 1) * R], Wp[:, c, g * P:(g + 1) * P], relT[:, c, :],
                                         start=(c == 0), stop=(c == NC - 1))
                last.then_inc(pos_done, 1)

            def project(t):
                if t >= 2:
                    pe.wait_ge(x1_ready, t - 1)
                for c in range(NC):
                    last = pe.matmul(bank[t % 2][:, :], AT[:, c, t * P:(t + 1) * P], M2[:, c, :],
                                     start=(c == 0), stop=(c == NC - 1))
                last.then_inc(x1_done, 1)

            def turn(t):
                pe.wait_ge(xn_ready, t + 1)
                if t >= 2:
                    pe.wait_ge(XT_ready, t - 1)
                transposes(pe, bank[2 + t % 2], xn[t % 2], NC).then_inc(xn_turned, 1)

            for t in range(T + 1):
                if t < T:
                    project(t)
                if t:
                    turn(t - 1)
            pe.wait_ge(pos_ready, 2 * G)
            pe.wait_ge(relT_ready, 1)
            pe.wait_ge(hw_loaded, 32)

            def heads(k, Wh):
                for half in range(2):
                    pe.wait_ge(XT_ready, 4 * (half + 1))
                    for g in range(G):
                        n = 8 * k + 4 * half + g
                        if n >= 4:
                            pe.wait_ge(qk_read[g % 2], (n - 4) // 2 + 1)
                        for c in range(NC):
                            last = pe.matmul(bank[4 + g][:, :], Wh[:, c, g * P:(g + 1) * P],
                                             XT[:, c, 512 * half:512 * half + 512],
                                             start=(c == 0), stop=(c == NC - 1))
                        last.then_inc(qk_done, 1)

            def positions(k, M):
                for e in range(2):
                    pe.wait_ge(qk_read[e], 4 * (k + 1))
                pe.wait_ge(bd_ready, 8)
                if k == 0:
                    pe.wait_ge(x1_ready, T)
                    pe.wait_ge(XT_ready, T)
                for n in range(NT * k, NT * k + NT):
                    lo = S - IB - IB * (n % NI)
                    for g in range(G):
                        if n:
                            pe.wait_ge(qp_read[g % 2], 2 * (n - 1) + g // 2 + 1)
                        pe.matmul(bank[g][:, 0:4 * W], tile_tokens(M, g, n),
                                  pos_bd[k][:, g, lo:lo + W, :], start=True, stop=True).then_inc(qp_done, 1)

            heads(0, Wq)
            positions(0, QTh)
            heads(1, Wk)
            positions(1, KTh)

        def read_heads(eng, k, e, write):
            M = (QTh, KTh)[k]
            for half in range(2):
                for g in range(e, G, 2):
                    eng.wait_ge(qk_done, 8 * k + 4 * half + g + 1)
                    write(M[:, g, half, :, :, :].rearrange("p i b w -> p b i w"),
                          bank[4 + g][:, :].rearrange("p (b i w) -> p b i w", b=8, i=NI), hcols[:, k, g:g + 1]
                          ).then_inc(qk_read[e], 1)

        def read_positions(eng, k, e, write):
            for n in range(NT * k, NT * k + NT):
                if n >= 3:
                    eng.wait_ge(qp_stored[n % 3], 16 * (n // 3))
                for g in range(e, G, 2):
                    eng.wait_ge(qp_done, G * n + g + 1)
                    if k == 0:
                        dst = qp[n % 3][:, :].rearrange("p (w h) -> p w h", h=H)[:, :, 4 * g:4 * g + 4]
                    else:
                        dst = qp[n % 3][:, (g // 2) * W * 8:(g // 2 + 1) * W * 8].rearrange(
                            "p (w h) -> p w h", h=8)[:, :, 4 * (g % 2):4 * (g % 2) + 4]
                    write(dst, bank[g][:, 0:4 * W].rearrange("p (w h) -> p w h", h=4)).then_inc(qp_read[e], 1)

        @block.vector
        def _(dve):
            dve.wait_ge(pos_loaded, 64)
            dve.bn_stats(stats[:, T, :], rel[:, :]).then_inc(stats_ready, 1)
            dve.wait_ge(stats_ready, 1)
            dve.bn_aggr(mv[:, T, :], stats[:, T, :]).then_inc(mv_ready, 1)
            dve.wait_ge(std_ready, 1)
            dve.reciprocal(rstd[:, T:T + 1], std[:, T:T + 1]).then_inc(rstd_ready, 1)
            dve.wait_ge(rstd_ready, 1)
            dve.tensor_scalar(rel[:, :], rel[:, :], mv[:, T, 0:1], rstd[:, T:T + 1], ALU.subtract, ALU.mult
                              ).then_inc(rel_step, 1)
            dve.wait_ge(rel_step, 1)
            dve.tensor_tensor(reln[:, :], rel[:, :], ln_g[:, :], ALU.mult).then_inc(rel_step, 1)
            dve.wait_ge(rel_step, 2)
            dve.tensor_tensor(reln[:, :], reln[:, :], ln_b[:, :], ALU.add).then_inc(rel_step, 2)
            dve.wait_ge(rel_turned, 1)
            dve.tensor_copy(relT[:, :, :], bank[7][:, :].rearrange("p (c n) -> p c n", c=NC)).then_inc(relT_ready, 1)
            for k in range(2):
                dve.wait_ge(pos_done, k + 1)
                for g in range(G):
                    dve.tensor_scalar(pos[k][:, g, :], bank[5 + k][:, g * R:(g + 1) * R], hcols[:, 2 + k, g:g + 1],
                                      POS_SCALE, ALU.add, ALU.mult).then_inc(pos_ready, 1)
            dve.wait_ge(pos_ready, 2 * G)
            dve.wait_ge(bd_zero, 2)
            for k in range(2):
                for h in range(4):
                    src = pos[k][32 * h:32 * h + 32, :, :]
                    src = src[:, :, ::-1] if k == 0 else src
                    dve.tensor_copy(pos_bd[k][32 * h:32 * h + 32, :, :, h], src).then_inc(bd_ready, 1)
            for t in range(T):
                dve.wait_ge(x1_done, t + 1)
                dve.wait_ge(x_biased, t + 1)
                dve.tensor_tensor(X[:, t, :], bank[t % 2][:, :], X[:, t, :], ALU.add).then_inc(x1_ready, 1)
                dve.wait_ge(x1_ready, t + 1)
                dve.bn_stats(stats[:, t, :], X[:, t, :]).then_inc(stats_ready, 1)
                dve.wait_ge(stats_ready, t + 2)
                dve.bn_aggr(mv[:, t, :], stats[:, t, :]).then_inc(mv_ready, 1)
                dve.wait_ge(std_ready, t + 2)
                dve.reciprocal(rstd[:, t:t + 1], std[:, t:t + 1]).then_inc(rstd_ready, 1)
                dve.wait_ge(rstd_ready, t + 2)
                if t >= 2:
                    dve.wait_ge(xn_turned, t - 1)
                dve.tensor_scalar(xn[t % 2][:, :], X[:, t, :], mv[:, t, 0:1], rstd[:, t:t + 1],
                                  ALU.subtract, ALU.mult).then_inc(xn_ready, 1)
            for k in range(2):
                read_heads(dve, k, 0, lambda o, i, b: dve.tensor_scalar(o, i, b, None, ALU.add))
                read_positions(dve, k, 0, lambda o, i: dve.tensor_copy(o, i))

        @block.scalar
        def _(act):
            act.wait_ge(mv_ready, 1)
            act.activation(std[:, T:T + 1], mv[:, T, 1:2], ACT.Sqrt, bias=eps[:, :]).then_inc(std_ready, 1)
            for t in range(T):
                act.wait_ge(mv_ready, t + 2)
                act.activation(std[:, t:t + 1], mv[:, t, 1:2], ACT.Sqrt, bias=eps[:, :]).then_inc(std_ready, 1)
                act.wait_ge(xn_turned, t + 1)
                act.activation(XT[:, :, t * P:(t + 1) * P], bank[2 + t % 2][:, :].rearrange("p (c n) -> p c n", c=NC),
                               ACT.Copy).then_inc(XT_ready, 1)
            for k in range(2):
                read_heads(act, k, 1, lambda o, i, b: act.activation(o, i, ACT.Identity, bias=b))
                read_positions(act, k, 1, lambda o, i: act.activation(o, i, ACT.Copy))


def phase_attention(nc, a, st, sem, sb, bank, ident, transposes, XT, QTh, KTh, AT, scr_c2p, scr_p2c):
    Wv = sb("hWv", [P, NC, D])
    bv = sb("hbv", [P, D])
    c2p = [sb(f"c2p{u}", [P, S, H]) for u in range(3)]
    p2c = [sb(f"p2c{u}", [P, 2, S, 8]) for u in range(3)]
    k_bd = [sb(f"k_bd{u}", [P, G, 2, 4, S]) for u in range(2)]
    q_of = [sb(f"q_of{u}", [P, G, 2, S]) for u in range(2)]
    v_bd = [sb(f"v_bd{u}", [P, 2, 8, 2, HD]) for u in range(2)]
    sc = [sb(f"sc{u}", [P, 8, 2, S]) for u in range(2)]
    pr = [sb(f"pr{u}", [P, 8, 2, S]) for u in range(2)]
    prT = [sb(f"prT{u}", [P, 8, P]) for u in range(2)]
    att = [sb(f"hatt{u}", [P, 2, 8, HD]) for u in range(2)]
    smax = [sb(f"hsmax{u}", [P, H]) for u in range(2)]
    ssum = [sb(f"hssum{u}", [P, H]) for u in range(2)]
    srec = [sb(f"hsrec{u}", [P, H]) for u in range(2)]

    v_bank, s_banks, p_banks, o_bank, at_bank = bank[0], bank[1:3], bank[3:5], bank[5], bank[6]

    hv_loaded = sem("hv_loaded")
    rel_loaded = [sem(f"rel_loaded{u}") for u in range(3)]
    bd_zero = sem("kv_bd_zero")
    k_ready = sem("k_bd_ready")
    v_done = sem("v_done")
    v_ready = sem("v_ready")
    sc_done = sem("hsc_done")
    sc_ready = sem("hsc_ready")
    smax_ready = sem("hsmax_ready")
    shifted = sem("hshifted")
    pr_ready = sem("hpr_ready")
    ssum_ready = sem("hssum_ready")
    srec_ready = sem("hsrec_ready")
    pr_turned = sem("hpr_turned")
    prT_ready = sem("hprT_ready")
    pv_done = sem("hpv_done")
    att_ready = sem("hatt_ready")
    att_turned = sem("hatt_turned")
    AT_ready = sem("hAT_ready")
    NR = 6

    with nc.Block() as block:
        @block.sync
        def _(sp):
            sp.dma_start(Wv[:, :, :], a["hWv"].rearrange("(c p) n -> p c n", p=P)).then_inc(hv_loaded, 16)
            sp.dma_start(bv[:, :], a["hbv"].broadcast_to([P, D])).then_inc(hv_loaded, 16)
            row = W * H
            for t in range(T):
                if t >= 3:
                    sp.wait_ge(sc_ready, 2 * (t - 2))
                for b in range(2):
                    at = (2 * t + b) * S * row
                    sp.dma_start(c2p[t % 3][64 * b:64 * b + 64, :, :],
                                 bass.AP(scr_c2p.tensor, at + (IB - 1) * H,
                                         [[IB * row, NI], [row - H, IB], [1, S * H]])
                                 ).then_inc(rel_loaded[t % 3], 16)
                    for hh in range(2):
                        sp.dma_start(p2c[t % 3][64 * hh:64 * hh + 64, b, :, :],
                                     bass.AP(scr_p2c.tensor, at + hh * W * 8 + IB * 8,
                                             [[IB * row, NI], [row - 8, IB], [1, S * 8]])
                                     ).then_inc(rel_loaded[t % 3], 16)

        @block.gpsimd
        def _(pool):
            for u in range(2):
                pool.memset(k_bd[u][:, :, :, :, :], 0.0).then_inc(bd_zero, 1)
            for u in range(2):
                pool.memset(v_bd[u][:, :, :, :, :], 0.0).then_inc(bd_zero, 1)
            pool.wait_ge(bd_zero, 4)

            def keys(t):
                if t >= 2:
                    pool.wait_ge(sc_done, t - 1)
                for h in range(4):
                    for b in range(2):
                        if t or h or b:
                            pool.wait_ge(k_ready, 10 * t + 2 * h + b)
                        pool.tensor_copy(k_bd[t % 2][32 * h:32 * h + 32, :, b, h, :].rearrange("p g (i w) -> p g i w", i=NI),
                                         KTh[32 * h:32 * h + 32, :, t // 4, :, 2 * (t % 4) + b, :]
                                         ).then_inc(k_ready, 1)
                for b in range(2):
                    pool.wait_ge(k_ready, 10 * t + 8 + b)
                    pool.tensor_copy(q_of[t % 2][:, :, b, :].rearrange("p g (i w) -> p g i w", i=NI),
                                     QTh[:, :, t // 4, :, 2 * (t % 4) + b, :]).then_inc(k_ready, 1)

            def shift(t):
                pool.wait_ge(smax_ready, t + 1)
                pool.wait_ge(k_ready, 10 * min(t + 2, T))
                pool.tensor_tensor(sc[t % 2][:, :, :, :].rearrange("p a b j -> p (a b) j"),
                                   sc[t % 2][:, :, :, :].rearrange("p a b j -> p (a b) j"),
                                   smax[t % 2][:, :].unsqueeze(2).broadcast_to([P, H, S]), ALU.subtract
                                   ).then_inc(shifted, 1)

            keys(0)
            keys(1)
            for t in range(T):
                shift(t)
                if t + 2 < T:
                    pool.wait_ge(shifted, t + 1)
                    keys(t + 2)

        @block.tensor
        def _(pe):
            pe.wait_ge(hv_loaded, 32)

            def values(t):
                if t:
                    pe.wait_ge(v_ready, 4 * t)
                for c in range(NC):
                    last = pe.matmul(v_bank[:, :], XT[:, c, t * P:(t + 1) * P], Wv[:, c, :],
                                     start=(c == 0), stop=(c == NC - 1))
                last.then_inc(v_done, 1)

            def scores(t):
                pe.wait_ge(k_ready, 10 * (t + 1))
                if t:
                    pe.wait_ge(sc_ready, 2 * t)
                for g in range(G):
                    for b in range(2):
                        o = s_banks[g % 2][64 * b:64 * b + 64, :].rearrange("p (h x j) -> p h x j", h=4, x=2)
                        pe.matmul(o[:, :, g // 2, :], q_of[t % 2][:, g, b, :],
                                  k_bd[t % 2][:, g, b, :, :], start=(g < 2), stop=False, skip_group_check=True)
                pe.wait_ge(rel_loaded[t % 3], 16 * NR * (t // 3 + 1))
                for h in range(8):
                    last = pe.matmul(s_banks[h // 4][:, (h % 4) * P:(h % 4 + 1) * P], p2c[t % 3][:, :, :, h],
                                     ident[:, :], start=False, stop=(h % 4 == 3), is_transpose=True,
                                     skip_group_check=True)
                last.then_inc(sc_done, 1)

            def turn_probs(t):
                pe.wait_ge(pr_ready, t + 1)
                if t:
                    pe.wait_ge(prT_ready, 2 * t)
                for h in range(8):
                    last = pe.transpose(p_banks[h // 4][:, (h % 4) * P:(h % 4 + 1) * P], pr[t % 2][:, h, :, :],
                                        ident[:, :])
                last.then_inc(pr_turned, 1)

            def attend(t):
                pe.wait_ge(prT_ready, 2 * (t + 1))
                pe.wait_ge(v_ready, 4 * (t + 1))
                if t:
                    pe.wait_ge(att_ready, t)
                for h in range(8):
                    for b in range(2):
                        o = o_bank[64 * b:64 * b + 64, :].rearrange("p (x h d) -> p x h d", x=2, h=8)
                        last = pe.matmul(o[:, :, h, :], prT[t % 2][:, h, 64 * b:64 * b + 64],
                                         v_bd[t % 2][:, b, h, :, :], start=(h == 0), stop=(h == 7),
                                         skip_group_check=True)
                last.then_inc(pv_done, 1)

            def turn_attended(t):
                pe.wait_ge(att_ready, t + 1)
                if t:
                    pe.wait_ge(AT_ready, t)
                for c in range(NC):
                    last = pe.transpose(at_bank[:, c * P:(c + 1) * P], att[t % 2][:, c // 2, 4 * (c % 2):4 * (c % 2) + 4, :],
                                        ident[:, :])
                last.then_inc(att_turned, 1)

            for t in range(T + 2):
                if t < T:
                    scores(t)
                if t >= 2:
                    turn_attended(t - 2)
                if t < T:
                    values(t)
                if 1 <= t <= T:
                    turn_probs(t - 1)
                    attend(t - 1)

        @block.vector
        def _(dve):
            dve.wait_ge(bd_zero, 4)
            dve.wait_ge(hv_loaded, 32)
            for t in range(T + 1):
                if t < T:
                    dve.wait_ge(sc_done, t + 1)
                    if t >= 2:
                        dve.wait_ge(pr_ready, t - 1)
                    for k in range(2):
                        for x in range(2):
                            ins = dve.tensor_tensor(
                                sc[t % 2][:, 4 * k:4 * k + 4, x, :],
                                s_banks[k][:, :].rearrange("p (h x j) -> p h x j", h=4, x=2)[:, :, x, :],
                                c2p[t % 3][:, :, 8 * x + 4 * k:8 * x + 4 * k + 4].rearrange("p j h -> p h j"), ALU.add)
                        ins.then_inc(sc_ready, 1)
                    dve.wait_ge(sc_ready, 2 * (t + 1))
                    if t >= 2:
                        dve.wait_ge(shifted, t - 1)
                    dve.tensor_reduce(smax[t % 2][:, :], sc[t % 2][:, :, :, :].rearrange("p a b j -> p (a b) j"),
                                      AX_X, ALU.max).then_inc(smax_ready, 1)
                    dve.wait_ge(v_done, t + 1)
                    if t >= 2:
                        dve.wait_ge(pv_done, t - 1)
                    for b in range(2):
                        for x in range(2):
                            dve.tensor_tensor(
                                v_bd[t % 2][64 * x:64 * x + 64, b, :, x, :],
                                v_bank[64 * b:64 * b + 64, 256 * x:256 * x + 256].rearrange("p (h d) -> p h d", h=8),
                                bv[64 * b:64 * b + 64, 256 * x:256 * x + 256].rearrange("p (h d) -> p h d", h=8),
                                ALU.add).then_inc(v_ready, 1)
                if t >= 1:
                    u = (t - 1) % 2
                    dve.wait_ge(pr_ready, t)
                    if t >= 3:
                        dve.wait_ge(att_ready, t - 2)
                    dve.tensor_reduce(ssum[u][:, :], pr[u][:, :, :, :].rearrange("p a b j -> p (a b) j"),
                                      AX_X, ALU.add).then_inc(ssum_ready, 1)
                    dve.wait_ge(ssum_ready, t)
                    dve.reciprocal(srec[u][:, :], ssum[u][:, :]).then_inc(srec_ready, 1)
                    dve.wait_ge(srec_ready, t)
                    dve.wait_ge(pv_done, t)
                    if t >= 3:
                        dve.wait_ge(att_turned, t - 2)
                    dve.tensor_tensor(att[u][:, :, :, :], o_bank[:, :].rearrange("p (x h d) -> p x h d", x=2, h=8),
                                      srec[u][:, :].rearrange("p (h x) -> p x h", x=2).unsqueeze(3)
                                      .broadcast_to([P, 2, 8, HD]), ALU.mult).then_inc(att_ready, 1)

        @block.scalar
        def _(act):
            for t in range(T + 2):
                if t >= 2:
                    act.wait_ge(att_turned, t - 1)
                    act.activation(AT[:, :, (t - 2) * P:(t - 1) * P],
                                   at_bank[:, :].rearrange("p (c n) -> p c n", c=NC), ACT.Copy).then_inc(AT_ready, 1)
                if 1 <= t <= T:
                    act.wait_ge(pr_turned, t)
                    if t >= 3:
                        act.wait_ge(pv_done, t - 2)
                    for k in range(2):
                        act.activation(prT[(t - 1) % 2][:, 4 * k:4 * k + 4, :],
                                       p_banks[k][:, :].rearrange("p (h n) -> p h n", h=4), ACT.Copy
                                       ).then_inc(prT_ready, 1)
                if t < T:
                    act.wait_ge(shifted, t + 1)
                    if t >= 2:
                        act.wait_ge(pr_turned, t - 1)
                        act.wait_ge(ssum_ready, t - 1)
                    act.activation(pr[t % 2][:, :, :, :].rearrange("p a b j -> p (a b j)"),
                                   sc[t % 2][:, :, :, :].rearrange("p a b j -> p (a b j)"), ACT.Exp,
                                   scale=ATT_SCALE).then_inc(pr_ready, 1)


def phase_norms(nc, a, st, sem, sb, bank, X, ident, ones, eps, transposes, AT, XN, XUT, MU):
    Wo = sb("hWo", [P, NC, D])
    bo = sb("hbo", [P, D])
    ln_g = sb("fln_g", [P, D])
    ln_b = sb("fln_b", [P, D])
    scale = sb("fscale", [P, 1])
    musq = sb("musq", [P, NC, ES])
    munorm = sb("munorm", [P, ES])
    z = [sb(f"z{u}", [P, D]) for u in range(2)]
    zn = [sb(f"zn{u}", [P, D]) for u in range(2)]
    sq = sb("sq", [P, D])
    xu = [sb(f"xu{u}", [P, D]) for u in range(2)]
    stats = sb("fstats", [P, 2, T, 6])
    mv = sb("fmv", [P, 2, T, 2])
    std = sb("fstd", [P, 3, T])
    rec = sb("frec", [P, 3, T])
    ss = sb("fss", [P, T])

    wo_loaded = sem("wo_loaded")
    f_loaded = sem("f_loaded")
    mu_loaded = sem("mu_loaded")
    x_biased = sem("fx_biased")
    musq_ready = sem("musq_ready")
    mu_summed = sem("mu_summed")
    munorm_ready = sem("munorm_ready")
    mu_step = sem("mu_step")
    x2_done = sem("x2_done")
    x2_ready = sem("x2_ready")
    stats_ready = sem("fstats_ready")
    mv_ready = sem("fmv_ready")
    std_ready = sem("fstd_ready")
    rec_ready = sem("frec_ready")
    z_ready = sem("z_ready")
    zn_ready = sem("zn_ready")
    zg_ready = sem("zg_ready")
    XN_ready = sem("XN_ready")
    ss_ready = sem("ss_ready")
    norm_ready = sem("norm_ready")
    unit_step = sem("unit_step")
    xu_ready = sem("xu_ready")
    xu_turned = sem("xu_turned")
    XUT_ready = sem("XUT_ready")

    with nc.Block() as block:
        @block.sync
        def _(sp):
            sp.dma_start(Wo[:, :, :], a["hWo"].rearrange("(c p) n -> p c n", p=P)).then_inc(wo_loaded, 16)
            sp.dma_start(bo[:, :], a["hbo"].broadcast_to([P, D])).then_inc(wo_loaded, 16)
            sp.dma_start(MU[:, :, :], a["mu"].rearrange("(c p) n -> p c n", p=P)).then_inc(mu_loaded, 16)
            sp.dma_start(ln_g[:, :], a["fln_g"].broadcast_to([P, D])).then_inc(f_loaded, 16)
            sp.dma_start(ln_b[:, :], a["fln_b"].broadcast_to([P, D])).then_inc(f_loaded, 16)
            sp.dma_start(scale[:, :], a["fscale"].broadcast_to([P, 1])).then_inc(f_loaded, 16)

        @block.gpsimd
        def _(pool):
            pool.wait_ge(wo_loaded, 32)
            for t in range(T):
                pool.tensor_tensor(X[:, t, :], X[:, t, :], bo[:, :], ALU.add).then_inc(x_biased, 1)
            pool.wait_ge(f_loaded, 48)
            for t in range(T):
                pool.wait_ge(zn_ready, t + 1)
                pool.tensor_tensor(XN[:, t, :], zn[t % 2][:, :], ln_g[:, :], ALU.mult).then_inc(zg_ready, 1)
                pool.wait_ge(zg_ready, t + 1)
                pool.tensor_tensor(XN[:, t, :], XN[:, t, :], ln_b[:, :], ALU.add).then_inc(XN_ready, 1)

        @block.tensor
        def _(pe):
            pe.wait_ge(musq_ready, 1)
            for c in range(NC):
                last = pe.matmul(bank[7][:, 0:ES], ones[:, :], musq[:, c, :], start=(c == 0), stop=(c == NC - 1))
            last.then_inc(mu_summed, 1)
            pe.wait_ge(wo_loaded, 32)

            def project(t):
                if t >= 2:
                    pe.wait_ge(x2_ready, t - 1)
                for c in range(NC):
                    last = pe.matmul(bank[t % 2][:, :], AT[:, c, t * P:(t + 1) * P], Wo[:, c, :],
                                     start=(c == 0), stop=(c == NC - 1))
                last.then_inc(x2_done, 1)

            def turn(t):
                pe.wait_ge(xu_ready, t + 1)
                if t >= 2:
                    pe.wait_ge(XUT_ready, t - 1)
                transposes(pe, bank[2 + t % 2], xu[t % 2], NC).then_inc(xu_turned, 1)

            for t in range(T + 2):
                if t < T:
                    project(t)
                if t >= 2:
                    turn(t - 2)

        @block.scalar
        def _(act):
            act.wait_ge(mu_summed, 1)
            act.activation(munorm[:, :], bank[7][:, 0:ES], ACT.Sqrt).then_inc(munorm_ready, 1)
            n = 0

            def norm_of(t):
                act.wait_ge(ss_ready, t + 1)
                act.activation(std[:, 2, t:t + 1], ss[:, t:t + 1], ACT.Sqrt).then_inc(norm_ready, 1)

            def turned(t):
                act.wait_ge(xu_turned, t + 1)
                act.activation(XUT[:, :, t * P:(t + 1) * P], bank[2 + t % 2][:, :].rearrange("p (c n) -> p c n", c=NC),
                               ACT.Copy).then_inc(XUT_ready, 1)

            for t in range(T + 2):
                if t < T:
                    for k in range(2):
                        act.wait_ge(mv_ready, 2 * t + k + 1)
                        act.activation(std[:, k, t:t + 1], mv[:, k, t, 1:2], ACT.Sqrt, bias=eps[:, :]
                                       ).then_inc(std_ready, 1)
                if 1 <= t <= T:
                    norm_of(t - 1)
                if t >= 2:
                    turned(t - 2)

        @block.vector
        def _(dve):
            dve.wait_ge(mu_loaded, 16)
            dve.tensor_tensor(musq[:, :, :], MU[:, :, :], MU[:, :, :], ALU.mult).then_inc(musq_ready, 1)
            dve.wait_ge(munorm_ready, 1)
            dve.tensor_scalar(munorm[:, :], munorm[:, :], NORM_EPS, None, ALU.max).then_inc(mu_step, 1)
            dve.wait_ge(mu_step, 1)
            dve.reciprocal(munorm[:, :], munorm[:, :]).then_inc(mu_step, 1)
            dve.wait_ge(mu_step, 2)
            for c in range(NC):
                dve.tensor_tensor(MU[:, c, :], MU[:, c, :], munorm[:, :], ALU.mult).then_inc(mu_step, 1)
            dve.wait_ge(f_loaded, 48)
            for t in range(T + 1):
                if t < T:
                    dve.wait_ge(x2_done, t + 1)
                    dve.wait_ge(x_biased, t + 1)
                    dve.tensor_tensor(X[:, t, :], bank[t % 2][:, :], X[:, t, :], ALU.add).then_inc(x2_ready, 1)
                    dve.wait_ge(x2_ready, t + 1)
                    src = X[:, t, :]
                    for k in range(2):
                        dve.bn_stats(stats[:, k, t, :], src).then_inc(stats_ready, 1)
                        dve.wait_ge(stats_ready, 2 * t + k + 1)
                        dve.bn_aggr(mv[:, k, t, :], stats[:, k, t, :]).then_inc(mv_ready, 1)
                        dve.wait_ge(std_ready, 2 * t + k + 1)
                        dve.reciprocal(rec[:, k, t:t + 1], std[:, k, t:t + 1]).then_inc(rec_ready, 1)
                        dve.wait_ge(rec_ready, 2 * t + k + 1)
                        if k == 0:
                            dve.tensor_scalar(z[t % 2][:, :], src, mv[:, k, t, 0:1], rec[:, k, t:t + 1],
                                              ALU.subtract, ALU.mult).then_inc(z_ready, 1)
                            dve.wait_ge(z_ready, t + 1)
                            src = z[t % 2][:, :]
                        else:
                            if t >= 2:
                                dve.wait_ge(zg_ready, t - 1)
                            dve.tensor_scalar(zn[t % 2][:, :], src, mv[:, k, t, 0:1], rec[:, k, t:t + 1],
                                              ALU.subtract, ALU.mult).then_inc(zn_ready, 1)
                if t >= 1:
                    v = t - 1
                    dve.wait_ge(XN_ready, t)
                    if t >= 2:
                        dve.wait_ge(ss_ready, t - 1)
                    dve.tensor_tensor_reduce(out=sq[:, :], in0=XN[:, v, :], in1=XN[:, v, :], scale=1.0, scalar=0.0,
                                             op0=ALU.mult, op1=ALU.add, accum_out=ss[:, v:v + 1]
                                             ).then_inc(ss_ready, 1)
                    dve.wait_ge(norm_ready, t)
                    dve.tensor_scalar(std[:, 2, v:v + 1], std[:, 2, v:v + 1], NORM_EPS, None, ALU.max
                                      ).then_inc(unit_step, 1)
                    dve.wait_ge(unit_step, 3 * v + 1)
                    dve.reciprocal(rec[:, 2, v:v + 1], std[:, 2, v:v + 1]).then_inc(unit_step, 1)
                    dve.wait_ge(unit_step, 3 * v + 2)
                    dve.tensor_scalar(rec[:, 2, v:v + 1], rec[:, 2, v:v + 1], scale[:, :], None, ALU.mult
                                      ).then_inc(unit_step, 1)
                    dve.wait_ge(unit_step, 3 * v + 3)
                    if v >= 2:
                        dve.wait_ge(xu_turned, v - 1)
                    dve.tensor_scalar(xu[v % 2][:, :], XN[:, v, :], rec[:, 2, v:v + 1], None, ALU.mult
                                      ).then_inc(xu_ready, 1)


def phase_routing_and_experts(nc, a, st, sem, sb, bank, X, ident, transposes, XN, XUT, MU, AT, M2, out):
    SI = sb("SI", [P, NC, E, B, SL])
    W1 = sb("W1", [P, E, NC, HID])
    combT = sb("combT", [P, T, EG, P])
    w1_loaded = sem("w1_loaded")

    with ExitStack() as rt:
        def rb(name, shape, dt=F32):
            return rt.enter_context(nc.sbuf_tensor(name, shape, dt))
        lg = [rb(f"lg{u}", [P, ES]) for u in range(2)]
        ce = [rb(f"ce{u}", [P, EG, 4, SL]) for u in range(2)]
        c_bd = [rb(f"c_bd{u}", [P, EG, 4, 2, SL]) for u in range(2)]
        d_bd = [rb(f"d_bd{u}", [P, 2, ES]) for u in range(2)]
        le = [rb(f"le{u}", [P, 4, S]) for u in range(2)]
        cmax = rb("cmax", [P, T])
        csum = rb("csum", [P, T])
        crec = rb("crec", [P, T])
        dmax = [rb(f"dmax{u}", [P, 4]) for u in range(2)]
        dsum = [rb(f"dsum{u}", [P, 4]) for u in range(2)]
        drec = [rb(f"drec{u}", [P, 4]) for u in range(2)]
        l_bank, lt_bank, d_bank, c_bank, si_banks = bank[0], bank[1], bank[2], bank[3], bank[4:8]
        bd_zero = sem("r_bd_zero")
        l_done = sem("l_done")
        lg_ready = sem("lg_ready")
        cmax_ready = sem("cmax_ready")
        ce_ready = sem("ce_ready")
        crec_ready = sem("crec_ready")
        cbd_ready = sem("cbd_ready")
        comb_turned = sem("comb_turned")
        combT_ready = sem("combT_ready")
        l_turned = sem("l_turned")
        dmax_ready = sem("dmax_ready")
        dsub_ready = sem("dsub_ready")
        de_ready = sem("de_ready")
        dsum_ready = sem("dsum_ready")
        drec_ready = sem("drec_ready")
        disp_ready = sem("disp_ready")
        disp_turned = sem("disp_turned")
        dbd_ready = sem("dbd_ready")
        si_done = sem("si_done")
        si_read = [sem("si_read_dve"), sem("si_read_act")]

        with nc.Block() as block:
            @block.sync
            def _(sp):
                sp.dma_start(W1[:, :, :, :], a["w1"]).then_inc(w1_loaded, 16)

            @block.gpsimd
            def _(pool):
                for u in range(2):
                    pool.memset(c_bd[u][:, :, :, :, :], 0.0).then_inc(bd_zero, 1)
                    pool.memset(d_bd[u][:, :, :], 0.0).then_inc(bd_zero, 1)
                pool.wait_ge(bd_zero, 4)
                for t in range(T):
                    pool.wait_ge(crec_ready, t + 1)
                    if t >= 2:
                        pool.wait_ge(comb_turned, t - 1)
                    for b in range(2):
                        q = slice(64 * b, 64 * b + 64)
                        if t or b:
                            pool.wait_ge(cbd_ready, 2 * t + b)
                        pool.tensor_scalar(c_bd[t % 2][q, :, :, b, :].rearrange("p g e s -> p (g e) s"),
                                           ce[t % 2][q, :, :, :].rearrange("p g e s -> p (g e) s"),
                                           crec[q, t:t + 1], None, ALU.mult).then_inc(cbd_ready, 1)

            @block.tensor
            def _(pe):
                def logits(t):
                    if t:
                        pe.wait_ge(lg_ready, t)
                        pe.wait_ge(cmax_ready, t)
                        pe.wait_ge(ce_ready, t)
                    for c in range(NC):
                        last = pe.matmul(l_bank[:, 0:ES], XUT[:, c, t * P:(t + 1) * P], MU[:, c, :],
                                         start=(c == 0), stop=(c == NC - 1))
                    last.then_inc(l_done, 1)

                def turn_logits(t):
                    pe.wait_ge(lg_ready, t + 1)
                    if t:
                        pe.wait_ge(dsub_ready, t)
                    transposes(pe, lt_bank, lg[t % 2], 2).then_inc(l_turned, 1)

                def turn_dispatch(t):
                    pe.wait_ge(disp_ready, t + 1)
                    if t:
                        pe.wait_ge(dbd_ready, 2 * t)
                    for k in range(2):
                        last = pe.transpose(d_bank[:, k * P:(k + 1) * P], le[t % 2][:, 2 * k:2 * k + 2, :], ident[:, :])
                    last.then_inc(disp_turned, 1)

                def turn_combine(t):
                    pe.wait_ge(cbd_ready, 2 * (t + 1))
                    if t:
                        pe.wait_ge(combT_ready, t)
                    for g in range(EG):
                        last = pe.transpose(c_bank[:, g * P:(g + 1) * P], c_bd[t % 2][:, g, :, :, :], ident[:, :])
                    last.then_inc(comb_turned, 1)

                def slot_inputs(t):
                    pe.wait_ge(dbd_ready, 2 * (t + 1))
                    for c in range(NC):
                        if t:
                            pe.wait_ge(si_read[c % 2], 2 * (t - 1) + c // 2 + 1)
                        pe.matmul(si_banks[c][:, :], XN[:, t, c * P:(c + 1) * P], d_bd[t % 2][:, :, :],
                                  start=True, stop=True).then_inc(si_done, 1)

                for t in range(T + 2):
                    if t < T:
                        logits(t)
                    if 1 <= t <= T:
                        turn_dispatch(t - 1)
                        turn_combine(t - 1)
                    if t < T:
                        turn_logits(t)
                    if 1 <= t <= T:
                        slot_inputs(t - 1)

            def read_slots(eng, e, t, copy):
                for c in (e, e + 2):
                    eng.wait_ge(si_done, NC * t + c + 1)
                    for b in range(2):
                        ins = copy(SI[:, c, :, 2 * t + b, :],
                                   si_banks[c][:, b * ES:(b + 1) * ES].rearrange("p (e s) -> p e s", e=E))
                    ins.then_inc(si_read[e], 1)

            @block.vector
            def _(dve):
                dve.wait_ge(bd_zero, 4)
                for t in range(T + 1):
                    if t < T:
                        dve.wait_ge(l_done, t + 1)
                        if t >= 2:
                            dve.wait_ge(l_turned, t - 1)
                        dve.tensor_copy(lg[t % 2][:, :], l_bank[:, 0:ES]).then_inc(lg_ready, 1)
                        dve.tensor_reduce(cmax[:, t:t + 1], l_bank[:, 0:ES], AX_X, ALU.max, negate=True
                                          ).then_inc(cmax_ready, 1)
                    if t >= 1:
                        v = t - 1
                        dve.wait_ge(disp_turned, t)
                        if v >= 2:
                            dve.wait_ge(si_done, NC * (v - 1))
                        for b in range(2):
                            q = slice(64 * b, 64 * b + 64)
                            dve.tensor_copy(d_bd[v % 2][q, b, :], d_bank[q, 0:ES]).then_inc(dbd_ready, 1)
                    if t < T:
                        u = t % 2
                        lt = lt_bank[:, 0:ES].rearrange("p (k n) -> p k n", k=4)
                        dve.wait_ge(l_turned, t + 1)
                        dve.tensor_reduce(dmax[u][:, :], lt, AX_X, ALU.max).then_inc(dmax_ready, 1)
                        dve.wait_ge(dmax_ready, t + 1)
                        if t >= 2:
                            dve.wait_ge(disp_turned, t - 1)
                        dve.tensor_tensor(le[u][:, :, :], lt, dmax[u][:, :].unsqueeze(2).broadcast_to([P, 4, S]),
                                          ALU.subtract).then_inc(dsub_ready, 1)
                        dve.wait_ge(ce_ready, t + 1)
                        dve.reciprocal(crec[:, t:t + 1], csum[:, t:t + 1]).then_inc(crec_ready, 1)
                        dve.wait_ge(de_ready, t + 1)
                        dve.tensor_reduce(dsum[u][:, :], le[u][:, :, :], AX_X, ALU.add).then_inc(dsum_ready, 1)
                        dve.wait_ge(dsum_ready, t + 1)
                        dve.reciprocal(drec[u][:, :], dsum[u][:, :]).then_inc(drec_ready, 1)
                        dve.wait_ge(drec_ready, t + 1)
                        dve.tensor_tensor(le[u][:, :, :], le[u][:, :, :],
                                          drec[u][:, :].unsqueeze(2).broadcast_to([P, 4, S]), ALU.mult
                                          ).then_inc(disp_ready, 1)
                    if t >= 1:
                        read_slots(dve, 0, t - 1, lambda o, i: dve.tensor_copy(o, i))

            @block.scalar
            def _(act):
                for t in range(T + 1):
                    if t < T:
                        act.wait_ge(cmax_ready, t + 1)
                        if t >= 2:
                            act.wait_ge(cbd_ready, 2 * (t - 1))
                        act.activation(ce[t % 2][:, :, :, :].rearrange("p g e s -> p (g e s)"), l_bank[:, 0:ES],
                                       ACT.Exp, bias=cmax[:, t:t + 1], accum_out=csum[:, t:t + 1]
                                       ).then_inc(ce_ready, 1)
                    if t >= 1:
                        act.wait_ge(comb_turned, t)
                        act.activation(combT[:, t - 1, :, :], c_bank[:, :].rearrange("p (g n) -> p g n", g=EG),
                                       ACT.Copy).then_inc(combT_ready, 1)
                    if t < T:
                        act.wait_ge(dsub_ready, t + 1)
                        act.activation(le[t % 2][:, :, :], le[t % 2][:, :, :], ACT.Exp).then_inc(de_ready, 1)
                    if t >= 1:
                        read_slots(act, 1, t - 1, lambda o, i: act.activation(o, i, ACT.Copy))

    NSO = 4
    Hs = XUT[:, :, :].rearrange("p c n -> p (c n)").rearrange("p (e n) -> p e n", e=E)
    W2 = [XN[:, :, :], AT[:, :, :].rearrange("p c n -> p (c n)").rearrange("p (e n) -> p e n", e=8)]
    b2x = M2
    b1c = sb("b1c", [P, E])
    so = [sb(f"so{i}", [P, D]) for i in range(NSO)]
    fin = [sb(f"fin{u}", [P, D]) for u in range(2)]
    w2_loaded = sem("w2_loaded")
    eb_loaded = sem("eb_loaded")
    h_done = sem("h_done")
    h_ready = sem("h_ready")
    so_done = sem("so_done")
    so_ready = sem("so_ready")
    y_done = sem("y_done")
    fin_ready = sem("fin_ready")
    stored = [sem(f"stored{u}") for u in range(2)]

    with nc.Block() as block:
        @block.sync
        def _(sp):
            sp.dma_start(b1c[:, :], a["b1c"]).then_inc(eb_loaded, 16)
            for g in range(EG):
                sp.dma_start(b2x[:, g, :], bass.AP(a["b2"].tensor, 4 * g * D, [[D, 4], [0, 32], [1, D]])
                             ).then_inc(eb_loaded, 16)
            w2 = a["w2"].rearrange("e h d -> h e d")
            for k in range(2):
                sp.dma_start(W2[k], w2[:, 8 * k:8 * k + 8, :]).then_inc(w2_loaded, 16)
            for t in range(T):
                sp.wait_ge(fin_ready, t + 1)
                sp.dma_start(out[t * P:(t + 1) * P, :], fin[t % 2][:, :]).then_inc(stored[t % 2], 16)
            for u in range(2):
                sp.wait_ge(stored[u], 16 * T // 2)

        @block.tensor
        def _(pe):
            pe.wait_ge(w1_loaded, 16)
            for e in range(E):
                if e >= 4:
                    pe.wait_ge(h_ready, e - 3)
                for c in range(NC):
                    last = pe.matmul(bank[e % 4][:, 0:B * SL], W1[:, e, c, :], SI[:, c, e, :, :],
                                     start=(c == 0), stop=(c == NC - 1))
                last.then_inc(h_done, 1)
            pe.wait_ge(w2_loaded, 32)
            pe.wait_ge(h_ready, E)

            def slot_outputs(t):
                for g in range(EG):
                    if t:
                        pe.wait_ge(so_ready, EG * (t - 1) + g + 1)
                    for k in range(4):
                        e = 4 * g + k
                        last = pe.matmul(bank[g][32 * k:32 * k + 32, :], Hs[:, e, 32 * t:32 * t + 32], W2[e // 8][:, e % 8, :],
                                         start=True, stop=True)
                    last.then_inc(so_done, 1)

            def combine(t):
                if t >= 2:
                    pe.wait_ge(fin_ready, t - 1)
                for g in range(EG):
                    pe.wait_ge(so_ready, EG * t + g + 1)
                    last = pe.matmul(bank[4 + t % 2][:, :], combT[:, t, g, :], so[(EG * t + g) % NSO][:, :],
                                     start=(g == 0), stop=(g == EG - 1))
                    last.then_inc(y_done, 1)

            for t in range(T + 1):
                if t < T:
                    slot_outputs(t)
                if t:
                    combine(t - 1)

        @block.scalar
        def _(act):
            act.wait_ge(eb_loaded, 80)
            for e in range(E):
                act.wait_ge(h_done, e + 1)
                act.activation(Hs[:, e, :], bank[e % 4][:, 0:B * SL], ACT.Gelu, bias=b1c[:, e:e + 1]
                               ).then_inc(h_ready, 1)

        @block.vector
        def _(dve):
            dve.wait_ge(eb_loaded, 80)
            for t in range(T + 1):
                for g in range(EG):
                    n = EG * t + g
                    if t < T:
                        dve.wait_ge(so_done, n + 1)
                        if n >= NSO:
                            dve.wait_ge(y_done, n - NSO + 1)
                        dve.tensor_tensor(so[n % NSO][:, :], bank[g][:, :], b2x[:, g, :], ALU.add
                                          ).then_inc(so_ready, 1)
                if t:
                    v = t - 1
                    dve.wait_ge(y_done, EG * t)
                    if v >= 2:
                        dve.wait_ge(stored[v % 2], 16 * (v // 2))
                    dve.tensor_tensor(fin[v % 2][:, :], bank[4 + v % 2][:, :], X[:, v, :], ALU.add
                                      ).then_inc(fin_ready, 1)


def kernel(**inputs):
    import numpy as _np
    import concourse.bacc as _bacc
    from concourse import mybir as _mybir
    from concourse.bass_utils import run_bass_kernel_spmd as _run

    def arr(name):
        return _np.asarray(inputs[name])

    def cols(*names):
        return _np.stack([arr(n).reshape(-1, P).T for n in names], axis=1)

    xbk, xbv = arr("L0_xattn_bk")[:D], arr("L0_xattn_bk")[D:]
    mask = arr("mask_BxS2_bk0").view(_np.uint8)
    data = {
        "x": arr("x").reshape(TOK, D),
        "ctx": arr("ctx_1024"),
        "mask": mask.reshape(B, P, KB).transpose(0, 2, 1).reshape(B, KEYS).copy().view(_np.uint32),
        "xWq": arr("L0_xattn_Wq"),
        "xWk": arr("L0_xattn_Wk"),
        "xWfcT": arr("L0_xattn_Wfc").T,
        "xcols": _np.stack([v.reshape(-1, P).T for v in (arr("L0_xattn_bq"), xbk, xbv)], axis=1),
        "xbfc": arr("L0_xattn_bfc").reshape(1, D),
        "hWq": arr("L0_attn_Wq"), "hWk": arr("L0_attn_Wk"), "hWv": arr("L0_attn_Wv"), "hWo": arr("L0_attn_Wo"),
        "Wpk": arr("L0_attn_Wpk"), "Wpq": arr("L0_attn_Wpq"),
        "hcols": cols("L0_attn_bq", "L0_attn_bk", "L0_attn_bpk", "L0_attn_bpq"),
        "hbv": arr("L0_attn_bv").reshape(1, D), "hbo": arr("L0_attn_bo").reshape(1, D),
        "rel": arr("L0_attn_rel_emb"),
        "ln_g": arr("L0_attn_ln_g").reshape(1, D), "ln_b": arr("L0_attn_ln_b").reshape(1, D),
        "fln_g": arr("L0_ffn_ln_gamma").reshape(1, D), "fln_b": arr("L0_ffn_ln_beta").reshape(1, D),
        "mu": arr("L0_ffn_mu").reshape(D, ES),
        "fscale": arr("L0_ffn_scale").reshape(1, 1),
        "w1": arr("L0_ffn_w1").reshape(E, NC, P, HID).transpose(2, 0, 1, 3),
        "b1c": arr("L0_ffn_b1").T,
        "w2": arr("L0_ffn_w2"),
        "b2": arr("L0_ffn_b2"),
    }
    nc = _bacc.Bacc("TRN2", target_bir_lowering=False, num_devices=1)
    arrays, aps = {}, {}
    for name, v in data.items():
        v = _np.ascontiguousarray(v)
        arrays[f"in_{name}"] = v
        aps[name] = nc.dram_tensor(f"in_{name}", v.shape, _mybir.dt.from_np(v.dtype), kind="ExternalInput").ap()
    out = nc.dram_tensor("out", (TOK, D), F32, kind="ExternalOutput").ap()
    build(nc, aps, out)
    r = _run(nc, [arrays], core_ids=[0])
    return r.results[0]["out"].reshape(B, S, D)
```

```python
from contextlib import ExitStack

import concourse.bass as bass
from concourse import mybir

ALU = mybir.AluOpType
ACT = mybir.ActivationFunctionType
F32 = mybir.dt.float32
U8 = mybir.dt.uint8
U32 = mybir.dt.uint32
AX_X = mybir.AxisListType.X

P = 128
B = 16
S = 64
D = 512
NC = D // P
TOK = B * S
T = TOK // P
KEYS = 512
KB = KEYS // P
H = 16
HD = D // H
G = H // 4
SPAN = 128
R = 2 * S
IB = 16
W = 80
NI = S // IB
E = 16
SL = 16
ES = E * SL
HID = 128
EG = E // 4
LN_EPS = 1e-5
MASKED = -3e38
NORM_EPS = 1e-12
ATT_SCALE = float((HD * 3) ** -0.5)
POS_SCALE = float((HD * 3) ** 0.5 / (HD * 2) ** 0.5)


def build(nc, a, out):
    with ExitStack() as whole:
        def sem(name):
            return whole.enter_context(nc.semaphore(name))

        def buffers(stack):
            return lambda name, shape, dt=F32: stack.enter_context(nc.sbuf_tensor(name, shape, dt))

        keep = buffers(whole)
        bank = [whole.enter_context(nc.psum_tensor(f"bank{i}", [P, 512], F32)) for i in range(8)]
        X = keep("X", [P, T, D])
        ident = keep("ident", [P, P])
        ones = keep("ones", [P, P])
        eps = keep("eps", [P, 1])

        ident_ready = sem("ident_ready")
        scr_c2p = nc.dram_tensor("scr_c2p", [TOK, W * H], F32, kind="Internal").ap()
        scr_p2c = nc.dram_tensor("scr_p2c", [TOK, W * H], F32, kind="Internal").ap()

        def transposes(pe, dst, src, n):
            for c in range(n):
                last = pe.transpose(dst[:, c * P:(c + 1) * P], src[:, c * P:(c + 1) * P], ident[:, :])
            return last

        ab = ExitStack()
        with ab:
            sb = buffers(ab)
            M2 = sb("M2", [P, NC, D])
            out_bias = sb("out_bias", [P, D])
            AT = sb("AT", [P, NC, TOK])
            WR = sb("WR", [P, 4, NC, D])
            proj_loaded = sem("proj_loaded")
            wo_loaded = sem("wo_loaded")
            w1_loaded = sem("w1_loaded")

            def load_projection_weights(sp):
                for k, name in enumerate(("Wpk", "Wpq", "hWq", "hWk")):
                    sp.dma_start(WR[:, k, :, :], a[name].rearrange("(c p) n -> p c n", p=P)
                                 ).then_inc(proj_loaded, 16)

            a01 = ExitStack()
            with a01:
                sb01 = buffers(a01)
                QT = sb01("QT", [P, NC, TOK])
                ctx = [sb01(f"ctx{u}", [P, 2, KB, D]) for u in range(3)]
                mask = sb01("mask", [P, T, KEYS // 4], U32)
                s_q = sb01("s_q", [P, T])
                ctx_loaded = [sem(f"ctx_loaded{u}") for u in range(3)]
                mask_loaded = sem("mask_loaded")

                def load_ctx(sp, t):
                    for b in range(2):
                        sp.dma_start(ctx[t % 3][:, b, :, :],
                                     a["ctx"][2 * t + b].rearrange("(p k) d -> p k d", k=KB)
                                     ).then_inc(ctx_loaded[t % 3], 16)

                with ExitStack() as st:
                    phase_queries(nc, a, st, sem, buffers(st), bank, X, ident, ones, eps, ident_ready,
                                  transposes, M2, out_bias, WR, QT, mask, s_q, load_ctx, mask_loaded)
                with ExitStack() as st:
                    phase_context(nc, a, st, sem, buffers(st), bank, ident, transposes, QT, ctx, mask, s_q,
                                  AT, load_ctx, ctx_loaded, mask_loaded, load_projection_weights)
            bc = ExitStack()
            sbc = buffers(bc)
            with bc:
                XT = sbc("XT", [P, NC, TOK])
                QTh = sbc("QTh", [P, G, 2, NI, 8, IB])
                KTh = sbc("KTh", [P, G, 2, NI, 8, IB])
                Wv = sbc("hWv", [P, NC, D])
                bv = sbc("hbv", [P, D])
                c2p = [sbc(f"c2p{u}", [P, S, H]) for u in range(2)]
                p2c = [sbc(f"p2c{u}", [P, 2, S, 8]) for u in range(2)]
                rel_loaded = [sem(f"rel_loaded{u}") for u in range(2)]

                def load_relative(sp, t):
                    row = W * H
                    for b in range(2):
                        at = (2 * t + b) * S * row
                        sp.dma_start(c2p[t % 2][64 * b:64 * b + 64, :, :],
                                     bass.AP(scr_c2p.tensor, at + (IB - 1) * H,
                                             [[IB * row, NI], [row - H, IB], [1, S * H]])
                                     ).then_inc(rel_loaded[t % 2], 16)
                        for hh in range(2):
                            sp.dma_start(p2c[t % 2][64 * hh:64 * hh + 64, b, :, :],
                                         bass.AP(scr_p2c.tensor, at + hh * W * 8 + IB * 8,
                                                 [[IB * row, NI], [row - 8, IB], [1, S * 8]])
                                         ).then_inc(rel_loaded[t % 2], 16)

                with ExitStack() as st:
                    phase_projections(nc, a, st, sem, buffers(st), bank, X, ident, eps, transposes,
                                      M2, out_bias, AT, WR, proj_loaded, XT, QTh, KTh, Wv, bv,
                                      scr_c2p, scr_p2c, load_relative)
                with ExitStack() as st:
                    phase_attention(nc, a, st, sem, buffers(st), bank, ident, transposes,
                                    XT, QTh, KTh, c2p, p2c, AT, rel_loaded, load_relative,
                                    M2, out_bias, WR, wo_loaded, w1_loaded)
            with ExitStack() as de:
                sde = buffers(de)
                XN = sde("XN", [P, T, D])
                XUT = sde("XUT", [P, NC, TOK])
                MU = sde("MU", [P, NC, ES])
                with ExitStack() as st:
                    phase_norms(nc, a, st, sem, buffers(st), bank, X, ident, ones, eps, transposes,
                                AT, M2, out_bias, wo_loaded, XN, XUT, MU)
                with ExitStack() as st:
                    phase_routing_and_experts(nc, a, st, sem, buffers(st), bank, X, ident, transposes,
                                              XN, XUT, MU, AT, M2, WR, w1_loaded, out)


def phase_queries(nc, a, st, sem, sb, bank, X, ident, ones, eps, ident_ready, transposes,
                  M2, out_bias, WR, QT, mask, s_q, load_ctx, mask_loaded):
    Wq, Wk, Wv, WfcT = (WR[:, k, :, :] for k in range(4))
    cols = sb("xattn_bias_cols", [P, 3, NC])
    spread = sb("xattn_bias_spread", [P, 3, NC, P])
    bfc = sb("bfc", [P, D])
    M1 = sb("M1", [P, NC, D])
    xn = [sb(f"xn{u}", [P, D]) for u in range(2)]
    XNT = sb("XNT", [P, NC, TOK])
    U = sb("U", [P, D])
    prod = sb("prod_q", [P, D])
    prod2 = sb("prod_q2", [P, P])
    qcol = sb("qcol", [P, NC])
    const = sb("const", [P, 1])
    stats = sb("stats", [P, T, 6])
    mv = sb("mv", [P, T, 2])
    std = sb("std", [P, T])
    rstd = sb("rstd", [P, T])

    x_loaded = sem("x_loaded")
    qk_loaded = sem("qk_loaded")
    vo_loaded = sem("vo_loaded")
    bias_loaded = sem("bias_loaded")
    spread_ready = sem("spread_ready")
    fold_done = sem("fold_done")
    m1_ready = sem("m1_ready")
    u_ready = sem("u_ready")
    qcol_ready = sem("qcol_ready")
    c_ready = sem("c_ready")
    stats_ready = sem("stats_ready")
    mv_ready = sem("mv_ready")
    std_ready = sem("std_ready")
    rstd_ready = sem("rstd_ready")
    xn_ready = sem("xn_ready")
    sq_ready = sem("sq_ready")
    xnT_turned = sem("xnT_turned")
    xnT_ready = sem("xnT_ready")
    qt_done = sem("qt_done")
    qt_read = [sem("qt_read_dve"), sem("qt_read_act")]
    m2_done = sem("m2_done")
    m2_ready = sem("m2_ready")
    out_bias_ready = sem("out_bias_ready")

    with nc.Block() as block:
        @block.sync
        def _(sp):
            sp.dma_start(Wq[:, :, :], a["xWq"].rearrange("(c p) n -> p c n", p=P)).then_inc(qk_loaded, 16)
            sp.dma_start(Wk[:, :, :], a["xWk"][0:D].rearrange("(c p) n -> p c n", p=P)).then_inc(qk_loaded, 16)
            sp.dma_start(X[:, :, :], a["x"].rearrange("(t p) d -> p t d", p=P)).then_inc(x_loaded, 16)
            sp.dma_start(cols[:, :, :], a["xcols"]).then_inc(bias_loaded, 16)
            sp.dma_start(bfc[:, :], a["xbfc"].broadcast_to([P, D])).then_inc(bias_loaded, 16)
            sp.dma_start(Wv[:, :, :], a["xWk"][D:2 * D].rearrange("(c p) n -> p c n", p=P)).then_inc(vo_loaded, 16)
            sp.dma_start(WfcT[:, :, :], a["xWfcT"].rearrange("(c p) n -> p c n", p=P)).then_inc(vo_loaded, 16)
            for b in range(2):
                sp.dma_start(mask[64 * b:64 * b + 64, :, :],
                             bass.AP(a["mask"].tensor, b * KEYS // 4, [[0, 64], [2 * KEYS // 4, T], [1, KEYS // 4]])
                             ).then_inc(mask_loaded, 16)
            for t in range(3):
                load_ctx(sp, t)

        @block.gpsimd
        def _(pool):
            pool.memset(ident[:, :], 0.0).then_inc(ident_ready, 1)
            pool.memset(ones[:, :], 1.0).then_inc(ident_ready, 1)
            pool.memset(eps[:, :], LN_EPS).then_inc(ident_ready, 1)
            pool.wait_ge(ident_ready, 3)
            pool.affine_select(out=ident[:, :], in_=ident[:, :], compare_op=ALU.not_equal, fill=1.0,
                               base=0, pattern=[[-1, P]], channel_multiplier=1).then_inc(ident_ready, 1)

        @block.tensor
        def _(pe):
            pe.wait_ge(qk_loaded, 32)
            for i in range(NC):
                if i >= 2:
                    pe.wait_ge(m1_ready, i - 1)
                for c in range(NC):
                    last = pe.matmul(bank[i % 2][:, :], Wq[:, c, i * P:(i + 1) * P], Wk[:, c, :],
                                     start=(c == 0), stop=(c == NC - 1))
                last.then_inc(fold_done, 1)
            pe.wait_ge(spread_ready, 3 * NC)
            for c in range(NC):
                last = pe.matmul(bank[2][:, :], spread[:, 1, c, :], Wq[:, c, :], start=(c == 0), stop=(c == NC - 1))
            last.then_inc(fold_done, 1)
            for c in range(NC):
                last = pe.matmul(bank[3][:, :], spread[:, 0, c, :], Wk[:, c, :], start=(c == 0), stop=(c == NC - 1))
            last.then_inc(fold_done, 1)
            for c in range(NC):
                last = pe.matmul(bank[4][:, 0:2], spread[:, 1, c, :], spread[:, 0, c, 0:2],
                                 start=(c == 0), stop=(c == NC - 1))
            last.then_inc(fold_done, 1)
            pe.wait_ge(ident_ready, 4)
            for t in range(T):
                pe.wait_ge(xn_ready, t + 1)
                if t >= 2:
                    pe.wait_ge(xnT_ready, t - 1)
                transposes(pe, bank[6 + t % 2], xn[t % 2], NC).then_inc(xnT_turned, 1)
            pe.wait_ge(m1_ready, NC)
            pe.wait_ge(u_ready, 1)
            pe.wait_ge(qcol_ready, NC)
            for half in range(2):
                pe.wait_ge(xnT_ready, 4 * (half + 1))
                for m in range(NC):
                    if half:
                        pe.wait_ge(qt_read[m % 2], m // 2 + 1)
                    for c in range(NC):
                        last = pe.matmul(bank[m][:, :], M1[:, c, m * P:(m + 1) * P],
                                         XNT[:, c, 512 * half:512 * half + 512],
                                         start=(c == 0), stop=(c == NC - 1))
                    last.then_inc(qt_done, 1)
            pe.wait_ge(vo_loaded, 32)
            for c in range(NC):
                last = pe.matmul(bank[5][:, :], spread[:, 2, c, :], WfcT[:, c, :], start=(c == 0), stop=(c == NC - 1))
            last.then_inc(m2_done, 1)
            for i in range(NC):
                if i < 2:
                    pe.wait_ge(xnT_ready, T)
                else:
                    pe.wait_ge(m2_ready, i - 1)
                for c in range(NC):
                    last = pe.matmul(bank[6 + i % 2][:, :], Wv[:, c, i * P:(i + 1) * P], WfcT[:, c, :],
                                     start=(c == 0), stop=(c == NC - 1))
                last.then_inc(m2_done, 1)

        @block.scalar
        def _(act):
            for i in range(NC):
                if i == 2:
                    act.wait_ge(mv_ready, T)
                    act.wait_ge(ident_ready, 3)
                    act.activation(std[:, :], mv[:, :, 1], ACT.Sqrt, bias=eps[:, :]).then_inc(std_ready, 1)
                act.wait_ge(fold_done, 1 + i)
                act.activation(M1[:, i, :], bank[i % 2][:, :], ACT.Copy).then_inc(m1_ready, 1)
            for t in range(T):
                act.wait_ge(xnT_turned, t + 1)
                act.activation(XNT[:, :, t * P:(t + 1) * P], bank[6 + t % 2][:, :].rearrange("p (c n) -> p c n", c=NC),
                               ACT.Copy).then_inc(xnT_ready, 1)
            act.wait_ge(qcol_ready, NC)
            for half in range(2):
                for m in (1, 3):
                    act.wait_ge(qt_done, 4 * half + m + 1)
                    act.activation(QT[:, m, 512 * half:512 * half + 512], bank[m][:, :], ACT.Identity,
                                   bias=qcol[:, m:m + 1]).then_inc(qt_read[1], 1)
            for i in range(NC):
                act.wait_ge(m2_done, 2 + i)
                act.activation(M2[:, i, :], bank[6 + i % 2][:, :], ACT.Copy).then_inc(m2_ready, 1)

        @block.vector
        def _(dve):
            dve.wait_ge(bias_loaded, 32)
            dve.wait_ge(ident_ready, 4)
            for k in range(3):
                for c in range(NC):
                    dve.tensor_scalar(spread[:, k, c, :], ones[:, :], cols[:, k, c:c + 1], None,
                                      ALU.mult).then_inc(spread_ready, 1)
            dve.wait_ge(x_loaded, 16)
            for t in range(T):
                dve.bn_stats(stats[:, t, :], X[:, t, :]).then_inc(stats_ready, 1)
            for t in range(T):
                dve.wait_ge(stats_ready, t + 1)
                dve.bn_aggr(mv[:, t, :], stats[:, t, :]).then_inc(mv_ready, 1)
            dve.wait_ge(std_ready, 1)
            dve.reciprocal(rstd[:, :], std[:, :]).then_inc(rstd_ready, 1)
            dve.wait_ge(fold_done, NC + 1)
            dve.tensor_copy(U[:, :], bank[2][:, :]).then_inc(u_ready, 1)
            dve.wait_ge(fold_done, NC + 2)
            for m in range(NC):
                if m:
                    dve.wait_ge(qcol_ready, m)
                dve.tensor_tensor_reduce(out=prod2[:, :], in0=bank[3][:, m * P:(m + 1) * P], in1=ident[:, :],
                                         scale=1.0, scalar=0.0, op0=ALU.mult, op1=ALU.add,
                                         accum_out=qcol[:, m:m + 1]).then_inc(qcol_ready, 1)
            dve.wait_ge(fold_done, NC + 3)
            dve.tensor_copy(const[:, :], bank[4][:, 0:1]).then_inc(c_ready, 1)
            dve.wait_ge(rstd_ready, 1)
            dve.wait_ge(u_ready, 1)
            for t in range(T):
                if t >= 2:
                    dve.wait_ge(xnT_turned, t - 1)
                dve.tensor_scalar(xn[t % 2][:, :], X[:, t, :], mv[:, t, 0:1], rstd[:, t:t + 1],
                                  ALU.subtract, ALU.mult).then_inc(xn_ready, 1)
                dve.wait_ge(xn_ready, t + 1)
                if t:
                    dve.wait_ge(sq_ready, t)
                dve.tensor_tensor_reduce(out=prod[:, :], in0=xn[t % 2][:, :], in1=U[:, :],
                                         scale=1.0, scalar=0.0, op0=ALU.mult, op1=ALU.add,
                                         accum_out=s_q[:, t:t + 1]).then_inc(sq_ready, 1)
            dve.wait_ge(sq_ready, T)
            dve.wait_ge(c_ready, 1)
            dve.tensor_scalar(s_q[:, :], s_q[:, :], const[:, :], None, ALU.add).then_inc(sq_ready, 1)
            for half in range(2):
                for m in (0, 2):
                    dve.wait_ge(qt_done, 4 * half + m + 1)
                    dve.tensor_scalar(QT[:, m, 512 * half:512 * half + 512], bank[m][:, :], qcol[:, m:m + 1], None,
                                      ALU.add).then_inc(qt_read[0], 1)
            dve.wait_ge(m2_done, 1)
            dve.tensor_tensor(out_bias[:, :], bank[5][:, :], bfc[:, :], ALU.add).then_inc(out_bias_ready, 1)


def phase_context(nc, a, st, sem, sb, bank, ident, transposes, QT, ctx, mask, s_q,
                  AT, load_ctx, ctx_loaded, mask_loaded, load_projection_weights):
    ctxT = [sb(f"ctxT{u}", [P, 2, NC, KEYS]) for u in range(2)]
    mask_bias = [sb(f"mask_bias{u}", [P, KEYS]) for u in range(2)]
    sm = [sb(f"sm{u}", [P, KEYS]) for u in range(2)]
    prob = [sb(f"prob{u}", [P, KEYS]) for u in range(2)]
    probT = [sb(f"probT{u}", [P, KB, P]) for u in range(2)]
    att = [sb(f"att{u}", [P, D]) for u in range(2)]
    smax = sb("smax", [P, T])
    smax2 = sb("smax2", [P, T])
    nbias = sb("nbias", [P, T])
    rsum = sb("rsum", [P, T])
    rrec = sb("rrec", [P, T])

    turn_banks, s_bank, p_bank, o_bank, at_bank = bank[0:4], bank[4], bank[5], bank[6], bank[7]

    turned = sem("ctx_turned")
    turned_read = [sem("ctx_turned_read_dve"), sem("ctx_turned_read_act")]
    mask_ready = sem("mask_ready")
    scores_done = sem("scores_done")
    sm_ready = sem("sm_ready")
    smax_ready = sem("smax_ready")
    smax2_ready = sem("smax2_ready")
    nbias_ready = sem("nbias_ready")
    prob_ready = sem("prob_ready")
    rrec_ready = sem("rrec_ready")
    prob_turned = sem("prob_turned")
    probT_ready = sem("probT_ready")
    pv_done = sem("pv_done")
    att_ready = sem("att_ready")
    att_turned = sem("att_turned")
    AT_ready = sem("AT_ready")
    NB = 2 * NC

    with nc.Block() as block:
        @block.sync
        def _(sp):
            for t in range(3, T):
                sp.wait_ge(pv_done, t - 2)
                load_ctx(sp, t)
            load_projection_weights(sp)

        @block.gpsimd
        def _(pool):
            pool.wait_ge(mask_loaded, 32)
            for t in range(T):
                if t >= 2:
                    pool.wait_ge(sm_ready, t - 1)
                pool.tensor_scalar(mask_bias[t % 2][:, :], mask[:, t, :].bitcast(U8), MASKED, None,
                                   ALU.mult).then_inc(mask_ready, 1)

        @block.tensor
        def _(pe):
            def turn_context(t):
                pe.wait_ge(ctx_loaded[t % 3], 32 * (t // 3 + 1))
                for i in range(NB):
                    b, c = i // NC, i % NC
                    n = (NB * t + i - 4) // 2 + 1
                    if NB * t + i >= 4:
                        pe.wait_ge(turned_read[i % 2], n)
                    for k in range(KB):
                        last = pe.transpose(turn_banks[i % 4][:, k * P:(k + 1) * P],
                                            ctx[t % 3][:, b, k, c * P:(c + 1) * P], ident[:, :])
                    last.then_inc(turned, 1)

            def scores(t):
                if t:
                    pe.wait_ge(sm_ready, t)
                for e in range(2):
                    pe.wait_ge(turned_read[e], 4 * (t + 1))
                for c in range(NC):
                    for b in range(2):
                        last = pe.matmul(s_bank[64 * b:64 * b + 64, :],
                                         QT[:, c, t * P + 64 * b:t * P + 64 * b + 64],
                                         ctxT[t % 2][:, b, c, :], start=(c == 0), stop=(c == NC - 1))
                last.then_inc(scores_done, 1)

            def turn_probs(t):
                pe.wait_ge(prob_ready, t + 1)
                if t:
                    pe.wait_ge(probT_ready, t)
                transposes(pe, p_bank, prob[t % 2], KB).then_inc(prob_turned, 1)

            def attend(t):
                pe.wait_ge(probT_ready, t + 1)
                if t:
                    pe.wait_ge(att_ready, t)
                for k in range(KB):
                    for b in range(2):
                        last = pe.matmul(o_bank[64 * b:64 * b + 64, :],
                                         probT[t % 2][:, k, 64 * b:64 * b + 64],
                                         ctx[t % 3][:, b, k, :], start=(k == 0), stop=(k == KB - 1))
                last.then_inc(pv_done, 1)

            def turn_attended(t):
                pe.wait_ge(att_ready, t + 1)
                if t:
                    pe.wait_ge(AT_ready, t)
                transposes(pe, at_bank, att[t % 2], NC).then_inc(att_turned, 1)

            for t in range(T + 2):
                if t < T:
                    turn_context(t)
                if t >= 2:
                    turn_attended(t - 2)
                if 1 <= t <= T:
                    turn_probs(t - 1)
                if t < T:
                    scores(t)
                if 1 <= t <= T:
                    attend(t - 1)

        @block.vector
        def _(dve):
            for t in range(T + 1):
                if t < T:
                    if t >= 2:
                        dve.wait_ge(scores_done, t - 1)
                    for i in range(0, NB, 2):
                        dve.wait_ge(turned, NB * t + i + 1)
                        dve.tensor_copy(ctxT[t % 2][:, i // NC, i % NC, :], turn_banks[i % 4][:, :]
                                        ).then_inc(turned_read[0], 1)
                    dve.wait_ge(scores_done, t + 1)
                    dve.wait_ge(mask_ready, t + 1)
                    if t >= 2:
                        dve.wait_ge(prob_ready, t - 1)
                    dve.tensor_tensor(sm[t % 2][:, :], s_bank[:, :], mask_bias[t % 2][:, :], ALU.add
                                      ).then_inc(sm_ready, 1)
                    dve.wait_ge(sm_ready, t + 1)
                    dve.tensor_reduce(smax[:, t:t + 1], sm[t % 2][:, :], AX_X, ALU.max).then_inc(smax_ready, 1)
                    dve.wait_ge(smax_ready, t + 1)
                    dve.tensor_tensor(smax2[:, t:t + 1], smax[:, t:t + 1], s_q[:, t:t + 1], ALU.add
                                      ).then_inc(smax2_ready, 1)
                    dve.wait_ge(smax2_ready, t + 1)
                    dve.tensor_tensor(nbias[:, t:t + 1], s_q[:, t:t + 1], smax2[:, t:t + 1], ALU.subtract
                                      ).then_inc(nbias_ready, 1)
                if t >= 1:
                    dve.wait_ge(prob_ready, t)
                    dve.reciprocal(rrec[:, t - 1:t], rsum[:, t - 1:t]).then_inc(rrec_ready, 1)
                    dve.wait_ge(rrec_ready, t)
                    dve.wait_ge(pv_done, t)
                    if t >= 3:
                        dve.wait_ge(att_turned, t - 2)
                    dve.tensor_scalar(att[(t - 1) % 2][:, :], o_bank[:, :], rrec[:, t - 1:t], None, ALU.mult
                                      ).then_inc(att_ready, 1)

        @block.scalar
        def _(act):
            for t in range(T + 2):
                if t < T:
                    if t >= 2:
                        act.wait_ge(scores_done, t - 1)
                    for i in range(1, NB, 2):
                        act.wait_ge(turned, NB * t + i + 1)
                        act.activation(ctxT[t % 2][:, i // NC, i % NC, :], turn_banks[i % 4][:, :], ACT.Copy
                                       ).then_inc(turned_read[1], 1)
                if t >= 2:
                    act.wait_ge(att_turned, t - 1)
                    act.activation(AT[:, :, (t - 2) * P:(t - 1) * P],
                                   at_bank[:, :].rearrange("p (c n) -> p c n", c=NC), ACT.Copy).then_inc(AT_ready, 1)
                if 1 <= t <= T:
                    act.wait_ge(prob_turned, t)
                    if t >= 3:
                        act.wait_ge(pv_done, t - 2)
                    act.activation(probT[(t - 1) % 2][:, :, :], p_bank[:, :].rearrange("p (k n) -> p k n", k=KB),
                                   ACT.Copy).then_inc(probT_ready, 1)
                if t < T:
                    act.wait_ge(nbias_ready, t + 1)
                    if t >= 2:
                        act.wait_ge(prob_turned, t - 1)
                    act.activation(prob[t % 2][:, :], sm[t % 2][:, :], ACT.Exp, bias=nbias[:, t:t + 1],
                                   accum_out=rsum[:, t:t + 1]).then_inc(prob_ready, 1)


def phase_projections(nc, a, st, sem, sb, bank, X, ident, eps, transposes,
                      M2, out_bias, AT, WR, proj_loaded, XT, QTh, KTh, Wv, bv,
                      scr_c2p, scr_p2c, load_relative):
    Wpk, Wpq, Wq, Wk = (WR[:, k, :, :] for k in range(4))
    hcols = sb("hcols", [P, 4, G])
    rel = sb("rel", [P, D])
    reln = sb("reln", [P, D])
    ln_g = sb("ln_g", [P, D])
    ln_b = sb("ln_b", [P, D])
    relT = sb("relT", [P, NC, P])
    pos = [sb(f"pos{k}", [P, G, R]) for k in range(2)]
    pos_bd = [sb(f"pos_bd{k}", [P, G, R, 4]) for k in range(2)]
    xn = [sb(f"hxn{u}", [P, D]) for u in range(2)]
    qp = [sb(f"qp{u}", [P, W * H]) for u in range(2)]
    stats = sb("hstats", [P, T + 1, 6])
    mv = sb("hmv", [P, T + 1, 2])
    std = sb("hstd", [P, T + 1])
    rstd = sb("hrstd", [P, T + 1])

    pos_loaded = sem("pos_loaded")
    x_biased = sem("x_biased")
    bd_zero = sem("bd_zero")
    x1_done = sem("x1_done")
    x1_ready = sem("x1_ready")
    stats_ready = sem("hstats_ready")
    mv_ready = sem("hmv_ready")
    std_ready = sem("hstd_ready")
    rstd_ready = sem("hrstd_ready")
    rel_step = sem("rel_step")
    rel_turned = sem("rel_turned")
    relT_ready = sem("relT_ready")
    pos_done = sem("pos_done")
    pos_ready = sem("pos_ready")
    bd_ready = sem("bd_ready")
    xn_ready = sem("hxn_ready")
    xn_turned = sem("hxn_turned")
    XT_ready = sem("XT_ready")
    qk_done = sem("qk_done")
    qk_read = [sem("qk_read_dve"), sem("qk_read_act")]
    qp_done = sem("qp_done")
    qp_read = [sem("qp_read_dve"), sem("qp_read_act")]
    qp_stored = [sem(f"qp_stored{u}") for u in range(2)]
    v_done = sem("v_done")
    v_ready = sem("v_ready")
    hv_loaded = sem("hv_loaded")
    NT = 2 * NI
    NQ = 2 * NT

    def tile_tokens(M, g, n):
        return M[:, g, (n % NT) // NI, n % NI, :, :]

    with nc.Block() as block:
        @block.sync
        def _(sp):
            sp.dma_start(rel[:, :], a["rel"][SPAN - S:SPAN + S]).then_inc(pos_loaded, 16)
            sp.dma_start(ln_g[:, :], a["ln_g"].broadcast_to([P, D])).then_inc(pos_loaded, 16)
            sp.dma_start(ln_b[:, :], a["ln_b"].broadcast_to([P, D])).then_inc(pos_loaded, 16)
            sp.dma_start(hcols[:, :, :], a["hcols"]).then_inc(pos_loaded, 16)
            sp.dma_start(Wv[:, :, :], a["hWv"].rearrange("(c p) n -> p c n", p=P)).then_inc(hv_loaded, 16)
            sp.dma_start(bv[:, :], a["hbv"].broadcast_to([P, D])).then_inc(hv_loaded, 16)
            for n in range(NQ):
                for e in range(2):
                    sp.wait_ge(qp_read[e], 2 * (n + 1))
                half, i = (n % NT) // NI, n % NI
                scr = scr_c2p if n < NT else scr_p2c
                dst = scr.rearrange("(b i) w -> b i w", b=B)[8 * half:8 * half + 8, IB * i:IB * i + IB, :]
                sp.dma_start(dst, qp[n % 2][:, :]).then_inc(qp_stored[n % 2], 16)
            for u in range(2):
                sp.wait_ge(qp_stored[u], 16 * NQ // 2)
            for t in range(2):
                load_relative(sp, t)

        @block.gpsimd
        def _(pool):
            for t in range(T):
                pool.tensor_tensor(X[:, t, :], X[:, t, :], out_bias[:, :], ALU.add).then_inc(x_biased, 1)
            for k in range(2):
                pool.memset(pos_bd[k][:, :, :, :], 0.0).then_inc(bd_zero, 1)

        @block.tensor
        def _(pe):
            def project(t):
                if t >= 2:
                    pe.wait_ge(x1_ready, t - 1)
                for c in range(NC):
                    last = pe.matmul(bank[t % 2][:, :], AT[:, c, t * P:(t + 1) * P], M2[:, c, :],
                                     start=(c == 0), stop=(c == NC - 1))
                last.then_inc(x1_done, 1)

            def turn(t):
                pe.wait_ge(xn_ready, t + 1)
                if t >= 2:
                    pe.wait_ge(XT_ready, t - 1)
                transposes(pe, bank[2 + t % 2], xn[t % 2], NC).then_inc(xn_turned, 1)

            pe.wait_ge(proj_loaded, 64)
            for t in range(T + 1):
                if t < T:
                    project(t)
                if t == 1:
                    pe.wait_ge(rel_step, 4)
                    transposes(pe, bank[7], reln, NC).then_inc(rel_turned, 1)
                if t:
                    turn(t - 1)
            pe.wait_ge(relT_ready, 1)
            for k, Wp in enumerate((Wpk, Wpq)):
                for g in range(G):
                    for c in range(NC):
                        last = pe.matmul(bank[5 + k][:, g * R:(g + 1) * R], Wp[:, c, g * P:(g + 1) * P], relT[:, c, :],
                                         start=(c == 0), stop=(c == NC - 1))
                last.then_inc(pos_done, 1)

            def heads(k, Wh):
                for half in range(2):
                    pe.wait_ge(XT_ready, 4 * (half + 1))
                    for g in range(G):
                        n = 8 * k + 4 * half + g
                        if n >= 4:
                            pe.wait_ge(qk_read[g % 2], (n - 4) // 2 + 1)
                        if n in (1, 2):
                            pe.wait_ge(pos_ready, G * n)
                        for c in range(NC):
                            last = pe.matmul(bank[4 + g][:, :], Wh[:, c, g * P:(g + 1) * P],
                                             XT[:, c, 512 * half:512 * half + 512],
                                             start=(c == 0), stop=(c == NC - 1))
                        last.then_inc(qk_done, 1)

            def positions(k, M):
                for e in range(2):
                    pe.wait_ge(qk_read[e], 4 * (k + 1))
                pe.wait_ge(bd_ready, 8)
                if k == 0:
                    pe.wait_ge(x1_ready, T)
                    pe.wait_ge(XT_ready, T)
                for n in range(NT * k, NT * k + NT):
                    lo = S - IB - IB * (n % NI)
                    for g in range(G):
                        if n:
                            pe.wait_ge(qp_read[g % 2], 2 * (n - 1) + g // 2 + 1)
                        pe.matmul(bank[g][:, 0:4 * W], tile_tokens(M, g, n),
                                  pos_bd[k][:, g, lo:lo + W, :], start=True, stop=True).then_inc(qp_done, 1)

            heads(0, Wq)
            positions(0, QTh)
            heads(1, Wk)
            positions(1, KTh)
            for e in range(2):
                pe.wait_ge(qk_read[e], 8)
            pe.wait_ge(hv_loaded, 32)
            for t in range(T):
                if t >= 4:
                    pe.wait_ge(v_ready, t - 3)
                for c in range(NC):
                    last = pe.matmul(bank[4 + t % 4][:, :], XT[:, c, t * P:(t + 1) * P], Wv[:, c, :],
                                     start=(c == 0), stop=(c == NC - 1))
                last.then_inc(v_done, 1)

        def read_heads(eng, k, e, write):
            M = (QTh, KTh)[k]
            for half in range(2):
                for g in range(e, G, 2):
                    eng.wait_ge(qk_done, 8 * k + 4 * half + g + 1)
                    write(M[:, g, half, :, :, :].rearrange("p i b w -> p b i w"),
                          bank[4 + g][:, :].rearrange("p (b i w) -> p b i w", b=8, i=NI), hcols[:, k, g:g + 1]
                          ).then_inc(qk_read[e], 1)

        def read_positions(eng, k, e, write):
            for n in range(NT * k, NT * k + NT):
                if n >= 2:
                    eng.wait_ge(qp_stored[n % 2], 16 * (n // 2))
                for g in range(e, G, 2):
                    eng.wait_ge(qp_done, G * n + g + 1)
                    if k == 0:
                        dst = qp[n % 2][:, :].rearrange("p (w h) -> p w h", h=H)[:, :, 4 * g:4 * g + 4]
                    else:
                        dst = qp[n % 2][:, (g // 2) * W * 8:(g // 2 + 1) * W * 8].rearrange(
                            "p (w h) -> p w h", h=8)[:, :, 4 * (g % 2):4 * (g % 2) + 4]
                    write(dst, bank[g][:, 0:4 * W].rearrange("p (w h) -> p w h", h=4)).then_inc(qp_read[e], 1)

        @block.vector
        def _(dve):
            dve.wait_ge(pos_loaded, 64)
            dve.bn_stats(stats[:, T, :], rel[:, :]).then_inc(stats_ready, 1)
            dve.wait_ge(stats_ready, 1)
            dve.bn_aggr(mv[:, T, :], stats[:, T, :]).then_inc(mv_ready, 1)
            dve.wait_ge(std_ready, 1)
            dve.reciprocal(rstd[:, T:T + 1], std[:, T:T + 1]).then_inc(rstd_ready, 1)
            dve.wait_ge(rstd_ready, 1)
            dve.tensor_scalar(rel[:, :], rel[:, :], mv[:, T, 0:1], rstd[:, T:T + 1], ALU.subtract, ALU.mult
                              ).then_inc(rel_step, 1)
            dve.wait_ge(rel_step, 1)
            dve.tensor_tensor(reln[:, :], rel[:, :], ln_g[:, :], ALU.mult).then_inc(rel_step, 1)
            dve.wait_ge(rel_step, 2)
            dve.tensor_tensor(reln[:, :], reln[:, :], ln_b[:, :], ALU.add).then_inc(rel_step, 2)
            for t in range(T):
                dve.wait_ge(x1_done, t + 1)
                dve.wait_ge(x_biased, t + 1)
                dve.tensor_tensor(X[:, t, :], bank[t % 2][:, :], X[:, t, :], ALU.add).then_inc(x1_ready, 1)
                dve.wait_ge(x1_ready, t + 1)
                dve.bn_stats(stats[:, t, :], X[:, t, :]).then_inc(stats_ready, 1)
                dve.wait_ge(stats_ready, t + 2)
                dve.bn_aggr(mv[:, t, :], stats[:, t, :]).then_inc(mv_ready, 1)
                dve.wait_ge(std_ready, t + 2)
                dve.reciprocal(rstd[:, t:t + 1], std[:, t:t + 1]).then_inc(rstd_ready, 1)
                dve.wait_ge(rstd_ready, t + 2)
                if t >= 2:
                    dve.wait_ge(xn_turned, t - 1)
                dve.tensor_scalar(xn[t % 2][:, :], X[:, t, :], mv[:, t, 0:1], rstd[:, t:t + 1],
                                  ALU.subtract, ALU.mult).then_inc(xn_ready, 1)
            for k in range(2):
                dve.wait_ge(pos_done, k + 1)
                for g in range(G):
                    dve.tensor_scalar(pos[k][:, g, :], bank[5 + k][:, g * R:(g + 1) * R], hcols[:, 2 + k, g:g + 1],
                                      POS_SCALE, ALU.add, ALU.mult).then_inc(pos_ready, 1)
            dve.wait_ge(pos_ready, 2 * G)
            dve.wait_ge(bd_zero, 2)
            for k in range(2):
                for h in range(4):
                    src = pos[k][32 * h:32 * h + 32, :, :]
                    src = src[:, :, ::-1] if k == 0 else src
                    dve.tensor_copy(pos_bd[k][32 * h:32 * h + 32, :, :, h], src).then_inc(bd_ready, 1)
            for k in range(2):
                read_heads(dve, k, 0, lambda o, i, b: dve.tensor_scalar(o, i, b, None, ALU.add))
                read_positions(dve, k, 0, lambda o, i: dve.tensor_copy(o, i))
            dve.wait_ge(hv_loaded, 32)
            for t in range(T):
                dve.wait_ge(v_done, t + 1)
                dve.tensor_tensor(XT[:, :, t * P:(t + 1) * P], bank[4 + t % 4][:, :].rearrange("p (c n) -> p c n", c=NC),
                                  bv[:, :].rearrange("p (c n) -> p c n", c=NC), ALU.add).then_inc(v_ready, 1)

        @block.scalar
        def _(act):
            act.wait_ge(mv_ready, 1)
            act.activation(std[:, T:T + 1], mv[:, T, 1:2], ACT.Sqrt, bias=eps[:, :]).then_inc(std_ready, 1)
            for t in range(T + 1):
                if t < T:
                    act.wait_ge(mv_ready, t + 2)
                    act.activation(std[:, t:t + 1], mv[:, t, 1:2], ACT.Sqrt, bias=eps[:, :]).then_inc(std_ready, 1)
                if t == 1:
                    act.wait_ge(rel_turned, 1)
                    act.activation(relT[:, :, :], bank[7][:, :].rearrange("p (c n) -> p c n", c=NC), ACT.Copy
                                   ).then_inc(relT_ready, 1)
                if t:
                    act.wait_ge(xn_turned, t)
                    act.activation(XT[:, :, (t - 1) * P:t * P],
                                   bank[2 + (t - 1) % 2][:, :].rearrange("p (c n) -> p c n", c=NC),
                                   ACT.Copy).then_inc(XT_ready, 1)
            for k in range(2):
                read_heads(act, k, 1, lambda o, i, b: act.activation(o, i, ACT.Identity, bias=b))
                read_positions(act, k, 1, lambda o, i: act.activation(o, i, ACT.Copy))


def phase_attention(nc, a, st, sem, sb, bank, ident, transposes, V, QTh, KTh, c2p, p2c, AT,
                    rel_loaded, load_relative, Wo, bo, W1, wo_loaded, w1_loaded):
    k_bd = [sb(f"k_bd{u}", [P, G, 4, NI, 2, IB]) for u in range(2)]
    q_of = [sb(f"q_of{u}", [P, G, 2, S]) for u in range(2)]
    v_bd = [sb(f"v_bd{u}", [P, 2, 8, 2, HD]) for u in range(2)]
    sc = [sb(f"sc{u}", [P, 8, 2, S]) for u in range(2)]
    pr = [sb(f"pr{u}", [P, 8, 2, S]) for u in range(2)]
    prT = [sb(f"prT{u}", [P, 8, P]) for u in range(2)]
    att = [sb(f"hatt{u}", [P, 2, 8, HD]) for u in range(2)]
    smax = [sb(f"hsmax{u}", [P, H]) for u in range(2)]
    ssum = [sb(f"hssum{u}", [P, H]) for u in range(2)]
    srec = [sb(f"hsrec{u}", [P, H]) for u in range(2)]

    s_banks, p_banks, o_bank, at_bank = bank[0:2], bank[4:6], bank[6], bank[7]

    bd_zero = sem("kv_bd_zero")
    k_ready = sem("k_bd_ready")
    q_ready = sem("q_of_ready")
    vbd_ready = sem("v_bd_ready")
    sc_done = sem("hsc_done")
    sc_ready = sem("hsc_ready")
    smax_ready = sem("hsmax_ready")
    shifted = sem("hshifted")
    pr_ready = sem("hpr_ready")
    ssum_ready = sem("hssum_ready")
    srec_ready = sem("hsrec_ready")
    pr_turned = sem("hpr_turned")
    prT_ready = sem("hprT_ready")
    pv_done = sem("hpv_done")
    att_ready = sem("hatt_ready")
    att_turned = sem("hatt_turned")
    AT_ready = sem("hAT_ready")
    NR = 6

    with nc.Block() as block:
        @block.sync
        def _(sp):
            sp.dma_start(Wo[:, :, :], a["hWo"].rearrange("(c p) n -> p c n", p=P)).then_inc(wo_loaded, 16)
            sp.dma_start(bo[:, :], a["hbo"].broadcast_to([P, D])).then_inc(wo_loaded, 16)
            for t in range(2, T):
                sp.wait_ge(sc_ready, 2 * (t - 1))
                load_relative(sp, t)
            sp.dma_start(W1[:, :, :, :].rearrange("p a c n -> p (a c n)"),
                         a["w1"].rearrange("p e c n -> p (e c n)")).then_inc(w1_loaded, 16)

        @block.gpsimd
        def _(pool):
            def queries(t):
                if t >= 2:
                    pool.wait_ge(sc_done, t - 1)
                for b in range(2):
                    pool.tensor_copy(q_of[t % 2][:, :, b, :].rearrange("p g (i w) -> p g i w", i=NI),
                                     QTh[:, :, t // 4, :, 2 * (t % 4) + b, :]).then_inc(q_ready, 1)

            queries(0)
            pool.memset(v_bd[0][:, :, :, :, :], 0.0).then_inc(bd_zero, 1)
            queries(1)
            pool.memset(v_bd[1][:, :, :, :, :], 0.0).then_inc(bd_zero, 1)
            for t in range(T):
                pool.wait_ge(smax_ready, t + 1)
                pool.tensor_tensor(sc[t % 2][:, :, :, :].rearrange("p a b j -> p (a b) j"),
                                   sc[t % 2][:, :, :, :].rearrange("p a b j -> p (a b) j"),
                                   smax[t % 2][:, :].unsqueeze(2).broadcast_to([P, H, S]), ALU.subtract
                                   ).then_inc(shifted, 1)
                if t + 2 < T:
                    queries(t + 2)

        @block.tensor
        def _(pe):
            def scores(t):
                pe.wait_ge(k_ready, 4 * (t + 1))
                pe.wait_ge(q_ready, 2 * (t + 1))
                if t:
                    pe.wait_ge(sc_ready, 2 * t)
                for g in range(G):
                    for b in range(2):
                        o = s_banks[g % 2][64 * b:64 * b + 64, :].rearrange("p (h x j) -> p h x j", h=4, x=2)
                        pe.matmul(o[:, :, g // 2, :], q_of[t % 2][:, g, b, :],
                                  k_bd[t % 2][:, g, :, :, b, :], start=(g < 2), stop=False, skip_group_check=True)
                pe.wait_ge(rel_loaded[t % 2], 16 * NR * (t // 2 + 1))
                for h in range(8):
                    last = pe.matmul(s_banks[h // 4][:, (h % 4) * P:(h % 4 + 1) * P], p2c[t % 2][:, :, :, h],
                                     ident[:, :], start=False, stop=(h % 4 == 3), is_transpose=True,
                                     skip_group_check=True)
                last.then_inc(sc_done, 1)

            def turn_probs(t):
                pe.wait_ge(pr_ready, t + 1)
                if t:
                    pe.wait_ge(prT_ready, 2 * t)
                for h in range(8):
                    last = pe.transpose(p_banks[h // 4][:, (h % 4) * P:(h % 4 + 1) * P], pr[t % 2][:, h, :, :],
                                        ident[:, :])
                    if h % 4 == 3:
                        last.then_inc(pr_turned, 1)

            def attend(t):
                pe.wait_ge(vbd_ready, 4 * (t + 1))
                if t:
                    pe.wait_ge(att_ready, t)
                for h in range(8):
                    if h % 4 == 0:
                        pe.wait_ge(prT_ready, 2 * t + h // 4 + 1)
                    for b in range(2):
                        o = o_bank[64 * b:64 * b + 64, :].rearrange("p (x h d) -> p x h d", x=2, h=8)
                        last = pe.matmul(o[:, :, h, :], prT[t % 2][:, h, 64 * b:64 * b + 64],
                                         v_bd[t % 2][:, b, h, :, :], start=(h == 0), stop=(h == 7),
                                         skip_group_check=True)
                last.then_inc(pv_done, 1)

            def turn_attended(t):
                pe.wait_ge(att_ready, t + 1)
                if t:
                    pe.wait_ge(AT_ready, t)
                for c in range(NC):
                    last = pe.transpose(at_bank[:, c * P:(c + 1) * P], att[t % 2][:, c // 2, 4 * (c % 2):4 * (c % 2) + 4, :],
                                        ident[:, :])
                last.then_inc(att_turned, 1)

            for t in range(T + 3):
                if 2 <= t < T + 2:
                    turn_probs(t - 2)
                if t < T:
                    scores(t)
                if t >= 3:
                    turn_attended(t - 3)
                if 2 <= t < T + 2:
                    attend(t - 2)

        @block.vector
        def _(dve):
            for u in range(2):
                dve.memset(k_bd[u][:, :, :, :, :, :], 0.0).then_inc(bd_zero, 1)
            dve.wait_ge(bd_zero, 4)
            for t in range(T + 2):
                if t < T:
                    if t >= 2:
                        dve.wait_ge(pv_done, t - 1)
                    for b in range(2):
                        for x in range(2):
                            dve.tensor_copy(
                                v_bd[t % 2][64 * x:64 * x + 64, b, :, x, :].rearrange("p (c h) d -> p c h d", c=2),
                                V[64 * b:64 * b + 64, 2 * x:2 * x + 2, t * P:(t + 1) * P]
                                .rearrange("p c (h d) -> p c h d", h=4)).then_inc(vbd_ready, 1)
                    dve.wait_ge(sc_done, t + 1)
                    if t >= 2:
                        dve.wait_ge(pr_ready, t - 1)
                    for k in range(2):
                        dve.tensor_tensor(
                            sc[t % 2][:, 4 * k:4 * k + 4, :, :],
                            s_banks[k][:, :].rearrange("p (h x j) -> p h x j", h=4, x=2),
                            c2p[t % 2][:, :, :].rearrange("p j (x h) -> p h x j", x=2)[:, 4 * k:4 * k + 4, :, :],
                            ALU.add).then_inc(sc_ready, 1)
                    dve.wait_ge(sc_ready, 2 * (t + 1))
                    if t >= 2:
                        dve.wait_ge(shifted, t - 1)
                    dve.tensor_reduce(smax[t % 2][:, :], sc[t % 2][:, :, :, :].rearrange("p a b j -> p (a b) j"),
                                      AX_X, ALU.max).then_inc(smax_ready, 1)
                if 1 <= t <= T:
                    v = t - 1
                    dve.wait_ge(pr_ready, t)
                    if v >= 2:
                        dve.wait_ge(att_ready, v - 1)
                    dve.tensor_reduce(ssum[v % 2][:, :], pr[v % 2][:, :, :, :].rearrange("p a b j -> p (a b) j"),
                                      AX_X, ALU.add).then_inc(ssum_ready, 1)
                    dve.wait_ge(ssum_ready, t)
                    dve.reciprocal(srec[v % 2][:, :], ssum[v % 2][:, :]).then_inc(srec_ready, 1)
                if t >= 2:
                    v = t - 2
                    dve.wait_ge(srec_ready, v + 1)
                    dve.wait_ge(pv_done, v + 1)
                    if v >= 2:
                        dve.wait_ge(att_turned, v - 1)
                    dve.tensor_tensor(att[v % 2][:, :, :, :], o_bank[:, :].rearrange("p (x h d) -> p x h d", x=2, h=8),
                                      srec[v % 2][:, :].rearrange("p (h x) -> p x h", x=2).unsqueeze(3)
                                      .broadcast_to([P, 2, 8, HD]), ALU.mult).then_inc(att_ready, 1)

        @block.scalar
        def _(act):
            def keys(t):
                if t >= 2:
                    act.wait_ge(sc_done, t - 1)
                for h in range(4):
                    act.activation(k_bd[t % 2][32 * h:32 * h + 32, :, h, :, :, :].rearrange("p g i b w -> p g i (b w)"),
                                   KTh[32 * h:32 * h + 32, :, t // 4, :, 2 * (t % 4):2 * (t % 4) + 2, :]
                                   .rearrange("p g i b w -> p g i (b w)"), ACT.Copy).then_inc(k_ready, 1)

            act.wait_ge(bd_zero, 4)
            keys(0)
            keys(1)
            for t in range(T + 3):
                if 2 <= t < T + 2:
                    v = t - 2
                    if v >= 2:
                        act.wait_ge(pv_done, v - 1)
                    for k in range(2):
                        act.wait_ge(pr_turned, 2 * v + k + 1)
                        act.activation(prT[v % 2][:, 4 * k:4 * k + 4, :],
                                       p_banks[k][:, :].rearrange("p (h n) -> p h n", h=4), ACT.Copy
                                       ).then_inc(prT_ready, 1)
                if t >= 3:
                    act.wait_ge(att_turned, t - 2)
                    act.activation(AT[:, :, (t - 3) * P:(t - 2) * P],
                                   at_bank[:, :].rearrange("p (c n) -> p c n", c=NC), ACT.Copy).then_inc(AT_ready, 1)
                if t < T:
                    act.wait_ge(shifted, t + 1)
                    if t >= 2:
                        act.wait_ge(pr_turned, 2 * (t - 1))
                        act.wait_ge(ssum_ready, t - 1)
                    act.activation(pr[t % 2][:, :, :, :].rearrange("p a b j -> p (a b j)"),
                                   sc[t % 2][:, :, :, :].rearrange("p a b j -> p (a b j)"), ACT.Exp,
                                   scale=ATT_SCALE).then_inc(pr_ready, 1)
                if t + 2 < T:
                    keys(t + 2)


def phase_norms(nc, a, st, sem, sb, bank, X, ident, ones, eps, transposes, AT, Wo, bo, wo_loaded, XN, XUT, MU):
    ln_g = sb("fln_g", [P, D])
    ln_b = sb("fln_b", [P, D])
    scale = sb("fscale", [P, 1])
    musq = sb("musq", [P, NC, ES])
    munorm = sb("munorm", [P, ES])
    z = [sb(f"z{u}", [P, D]) for u in range(2)]
    zn = [sb(f"zn{u}", [P, D]) for u in range(2)]
    sq = [sb(f"sq{u}", [P, D]) for u in range(2)]
    xu = [sb(f"xu{u}", [P, D]) for u in range(2)]
    stats = sb("fstats", [P, 2, T, 6])
    mv = sb("fmv", [P, 2, T, 2])
    std = sb("fstd", [P, 3, T])
    rec = sb("frec", [P, 3, T])
    ss = sb("fss", [P, T])

    f_loaded = sem("f_loaded")
    mu_loaded = sem("mu_loaded")
    x_biased = sem("fx_biased")
    musq_ready = sem("musq_ready")
    mu_summed = sem("mu_summed")
    munorm_ready = sem("munorm_ready")
    mu_step = sem("mu_step")
    x2_done = sem("x2_done")
    x2_ready = sem("x2_ready")
    stats_ready = [sem(f"fstats_ready{k}") for k in range(2)]
    mv_ready = [sem(f"fmv_ready{k}") for k in range(2)]
    std_ready = [sem(f"fstd_ready{k}") for k in range(2)]
    rec_ready = [sem(f"frec_ready{k}") for k in range(2)]
    z_ready = sem("z_ready")
    zn_ready = sem("zn_ready")
    zg_ready = sem("zg_ready")
    XN_ready = sem("XN_ready")
    ss_ready = sem("ss_ready")
    norm_ready = sem("norm_ready")
    unit_step = sem("unit_step")
    xu_ready = sem("xu_ready")
    xu_turned = sem("xu_turned")
    XUT_ready = sem("XUT_ready")

    with nc.Block() as block:
        @block.sync
        def _(sp):
            sp.dma_start(MU[:, :, :], a["mu"].rearrange("(c p) n -> p c n", p=P)).then_inc(mu_loaded, 16)
            sp.dma_start(ln_g[:, :], a["fln_g"].broadcast_to([P, D])).then_inc(f_loaded, 16)
            sp.dma_start(ln_b[:, :], a["fln_b"].broadcast_to([P, D])).then_inc(f_loaded, 16)
            sp.dma_start(scale[:, :], a["fscale"].broadcast_to([P, 1])).then_inc(f_loaded, 16)

        @block.gpsimd
        def _(pool):
            pool.wait_ge(wo_loaded, 32)
            for t in range(T):
                pool.tensor_tensor(X[:, t, :], X[:, t, :], bo[:, :], ALU.add).then_inc(x_biased, 1)
            pool.wait_ge(f_loaded, 48)
            for t in range(T):
                pool.wait_ge(zn_ready, t + 1)
                pool.tensor_tensor(XN[:, t, :], zn[t % 2][:, :], ln_g[:, :], ALU.mult).then_inc(zg_ready, 1)
                pool.wait_ge(zg_ready, t + 1)
                pool.tensor_tensor(XN[:, t, :], XN[:, t, :], ln_b[:, :], ALU.add).then_inc(XN_ready, 1)

        @block.tensor
        def _(pe):
            pe.wait_ge(wo_loaded, 32)

            def project(t):
                if t >= 2:
                    pe.wait_ge(x2_ready, t - 1)
                for c in range(NC):
                    last = pe.matmul(bank[t % 2][:, :], AT[:, c, t * P:(t + 1) * P], Wo[:, c, :],
                                     start=(c == 0), stop=(c == NC - 1))
                last.then_inc(x2_done, 1)

            def turn(t):
                pe.wait_ge(xu_ready, t + 1)
                if t >= 2:
                    pe.wait_ge(XUT_ready, t - 1)
                transposes(pe, bank[2 + t % 2], xu[t % 2], NC).then_inc(xu_turned, 1)

            for t in range(T + 5):
                if t < T:
                    project(t)
                if t == 2:
                    pe.wait_ge(musq_ready, 1)
                    for c in range(NC):
                        last = pe.matmul(bank[7][:, 0:ES], ones[:, :], musq[:, c, :],
                                         start=(c == 0), stop=(c == NC - 1))
                    last.then_inc(mu_summed, 1)
                if t >= 5:
                    turn(t - 5)

        @block.scalar
        def _(act):
            for t in range(T + 5):
                if t < T:
                    act.wait_ge(mv_ready[0], t + 1)
                    act.activation(std[:, 0, t:t + 1], mv[:, 0, t, 1:2], ACT.Sqrt, bias=eps[:, :]
                                   ).then_inc(std_ready[0], 1)
                if 1 <= t < T + 1:
                    v = t - 1
                    act.wait_ge(mv_ready[1], v + 1)
                    act.activation(std[:, 1, v:v + 1], mv[:, 1, v, 1:2], ACT.Sqrt, bias=eps[:, :]
                                   ).then_inc(std_ready[1], 1)
                if t == 3:
                    act.wait_ge(mu_summed, 1)
                    act.activation(munorm[:, :], bank[7][:, 0:ES], ACT.Sqrt).then_inc(munorm_ready, 1)
                if 3 <= t < T + 3:
                    v = t - 3
                    act.wait_ge(XN_ready, v + 1)
                    act.activation(sq[v % 2][:, :], XN[:, v, :], ACT.Square, accum_out=ss[:, v:v + 1]
                                   ).then_inc(ss_ready, 1)
                    act.wait_ge(ss_ready, v + 1)
                    act.activation(std[:, 2, v:v + 1], ss[:, v:v + 1], ACT.Sqrt).then_inc(norm_ready, 1)
                if t >= 5:
                    v = t - 5
                    act.wait_ge(xu_turned, v + 1)
                    act.activation(XUT[:, :, v * P:(v + 1) * P],
                                   bank[2 + v % 2][:, :].rearrange("p (c n) -> p c n", c=NC),
                                   ACT.Copy).then_inc(XUT_ready, 1)

        @block.vector
        def _(dve):
            def moments(k, t, src):
                dve.bn_stats(stats[:, k, t, :], src).then_inc(stats_ready[k], 1)
                dve.wait_ge(stats_ready[k], t + 1)
                dve.bn_aggr(mv[:, k, t, :], stats[:, k, t, :]).then_inc(mv_ready[k], 1)

            def normed(k, t, dst, src, ready):
                dve.wait_ge(std_ready[k], t + 1)
                dve.reciprocal(rec[:, k, t:t + 1], std[:, k, t:t + 1]).then_inc(rec_ready[k], 1)
                dve.wait_ge(rec_ready[k], t + 1)
                dve.tensor_scalar(dst, src, mv[:, k, t, 0:1], rec[:, k, t:t + 1],
                                  ALU.subtract, ALU.mult).then_inc(ready, 1)

            for t in range(T + 4):
                if t < T:
                    dve.wait_ge(x2_done, t + 1)
                    dve.wait_ge(x_biased, t + 1)
                    dve.tensor_tensor(X[:, t, :], bank[t % 2][:, :], X[:, t, :], ALU.add).then_inc(x2_ready, 1)
                    dve.wait_ge(x2_ready, t + 1)
                    moments(0, t, X[:, t, :])
                if t == 1:
                    dve.wait_ge(mu_loaded, 16)
                    dve.tensor_tensor(musq[:, :, :], MU[:, :, :], MU[:, :, :], ALU.mult).then_inc(musq_ready, 1)
                if 1 <= t < T + 1:
                    v = t - 1
                    normed(0, v, z[v % 2][:, :], X[:, v, :], z_ready)
                    dve.wait_ge(z_ready, v + 1)
                    moments(1, v, z[v % 2][:, :])
                if 2 <= t < T + 2:
                    v = t - 2
                    if v >= 2:
                        dve.wait_ge(zg_ready, v - 1)
                    normed(1, v, zn[v % 2][:, :], z[v % 2][:, :], zn_ready)
                if t >= 4:
                    v = t - 4
                    dve.wait_ge(norm_ready, v + 1)
                    dve.tensor_scalar(std[:, 2, v:v + 1], std[:, 2, v:v + 1], NORM_EPS, None, ALU.max
                                      ).then_inc(unit_step, 1)
                    dve.wait_ge(unit_step, 3 * v + 1)
                    dve.reciprocal(rec[:, 2, v:v + 1], std[:, 2, v:v + 1]).then_inc(unit_step, 1)
                    dve.wait_ge(unit_step, 3 * v + 2)
                    dve.tensor_scalar(rec[:, 2, v:v + 1], rec[:, 2, v:v + 1], scale[:, :], None, ALU.mult
                                      ).then_inc(unit_step, 1)
                    dve.wait_ge(unit_step, 3 * v + 3)
                    if v >= 2:
                        dve.wait_ge(xu_turned, v - 1)
                    dve.tensor_scalar(xu[v % 2][:, :], XN[:, v, :], rec[:, 2, v:v + 1], None, ALU.mult
                                      ).then_inc(xu_ready, 1)
                if t == 5:
                    dve.wait_ge(munorm_ready, 1)
                    dve.tensor_scalar(munorm[:, :], munorm[:, :], NORM_EPS, None, ALU.max).then_inc(mu_step, 1)
                    dve.wait_ge(mu_step, 1)
                    dve.reciprocal(munorm[:, :], munorm[:, :]).then_inc(mu_step, 1)
                    dve.wait_ge(mu_step, 2)
                    for c in range(NC):
                        dve.tensor_tensor(MU[:, c, :], MU[:, c, :], munorm[:, :], ALU.mult).then_inc(mu_step, 1)


def phase_routing_and_experts(nc, a, st, sem, sb, bank, X, ident, transposes, XN, XUT, MU, AT, M2, WR,
                              w1_loaded, out):
    SI = sb("SI", [P, NC, E, B, SL])
    W1 = WR[:, :, :, :].rearrange("p a c n -> p (a c n)").rearrange("p (e c n) -> p e c n", e=E, c=NC)
    combT = sb("combT", [P, T, EG, P])

    with ExitStack() as rt:
        def rb(name, shape, dt=F32):
            return rt.enter_context(nc.sbuf_tensor(name, shape, dt))
        lg = [rb(f"lg{u}", [P, ES]) for u in range(2)]
        ce = [rb(f"ce{u}", [P, EG, 4, SL]) for u in range(2)]
        c_bd = [rb(f"c_bd{u}", [P, EG, 4, 2, SL]) for u in range(2)]
        d_bd = [rb(f"d_bd{u}", [P, 2, ES]) for u in range(2)]
        le = [rb(f"le{u}", [P, 4, S]) for u in range(2)]
        cmax = rb("cmax", [P, T])
        csum = rb("csum", [P, T])
        crec = rb("crec", [P, T])
        dmax = [rb(f"dmax{u}", [P, 4]) for u in range(2)]
        dsum = [rb(f"dsum{u}", [P, 4]) for u in range(2)]
        drec = [rb(f"drec{u}", [P, 4]) for u in range(2)]
        l_bank, lt_bank, d_bank, c_bank, si_banks = bank[0], bank[1], bank[2], bank[3], bank[4:8]
        bd_zero = sem("r_bd_zero")
        l_done = sem("l_done")
        lg_ready = sem("lg_ready")
        cmax_ready = sem("cmax_ready")
        ce_ready = sem("ce_ready")
        crec_ready = sem("crec_ready")
        cbd_ready = sem("cbd_ready")
        comb_turned = sem("comb_turned")
        combT_ready = sem("combT_ready")
        l_turned = sem("l_turned")
        dmax_ready = sem("dmax_ready")
        dsub_ready = sem("dsub_ready")
        de_ready = sem("de_ready")
        dsum_ready = sem("dsum_ready")
        drec_ready = sem("drec_ready")
        disp_ready = sem("disp_ready")
        disp_turned = sem("disp_turned")
        dbd_ready = sem("dbd_ready")
        si_done = sem("si_done")
        si_read = [sem("si_read_dve"), sem("si_read_act")]

        with nc.Block() as block:
            @block.gpsimd
            def _(pool):
                for u in range(2):
                    pool.memset(c_bd[u][:, :, :, :, :], 0.0).then_inc(bd_zero, 1)
                    pool.memset(d_bd[u][:, :, :], 0.0).then_inc(bd_zero, 1)
                pool.wait_ge(bd_zero, 4)
                for t in range(T):
                    pool.wait_ge(crec_ready, t + 1)
                    if t >= 2:
                        pool.wait_ge(comb_turned, t - 1)
                    for b in range(2):
                        q = slice(64 * b, 64 * b + 64)
                        if t or b:
                            pool.wait_ge(cbd_ready, 2 * t + b)
                        pool.tensor_scalar(c_bd[t % 2][q, :, :, b, :].rearrange("p g e s -> p (g e) s"),
                                           ce[t % 2][q, :, :, :].rearrange("p g e s -> p (g e) s"),
                                           crec[q, t:t + 1], None, ALU.mult).then_inc(cbd_ready, 1)

            @block.tensor
            def _(pe):
                def logits(t):
                    if t:
                        pe.wait_ge(lg_ready, t)
                        pe.wait_ge(cmax_ready, t)
                        pe.wait_ge(ce_ready, t)
                    for c in range(NC):
                        last = pe.matmul(l_bank[:, 0:ES], XUT[:, c, t * P:(t + 1) * P], MU[:, c, :],
                                         start=(c == 0), stop=(c == NC - 1))
                    last.then_inc(l_done, 1)

                def turn_logits(t):
                    pe.wait_ge(lg_ready, t + 1)
                    if t:
                        pe.wait_ge(dsub_ready, t)
                    transposes(pe, lt_bank, lg[t % 2], 2).then_inc(l_turned, 1)

                def turn_dispatch(t):
                    pe.wait_ge(disp_ready, t + 1)
                    if t:
                        pe.wait_ge(dbd_ready, 2 * t)
                    for k in range(2):
                        last = pe.transpose(d_bank[:, k * P:(k + 1) * P], le[t % 2][:, 2 * k:2 * k + 2, :], ident[:, :])
                    last.then_inc(disp_turned, 1)

                def turn_combine(t):
                    pe.wait_ge(cbd_ready, 2 * (t + 1))
                    if t:
                        pe.wait_ge(combT_ready, t)
                    for g in range(EG):
                        last = pe.transpose(c_bank[:, g * P:(g + 1) * P], c_bd[t % 2][:, g, :, :, :], ident[:, :])
                    last.then_inc(comb_turned, 1)

                def slot_inputs(t):
                    pe.wait_ge(dbd_ready, 2 * (t + 1))
                    for c in range(NC):
                        if t:
                            pe.wait_ge(si_read[c % 2], 2 * (t - 1) + c // 2 + 1)
                        pe.matmul(si_banks[c][:, :], XN[:, t, c * P:(c + 1) * P], d_bd[t % 2][:, :, :],
                                  start=True, stop=True).then_inc(si_done, 1)

                for t in range(T + 2):
                    if t < T:
                        logits(t)
                    if 1 <= t <= T:
                        turn_dispatch(t - 1)
                        turn_combine(t - 1)
                    if t < T:
                        turn_logits(t)
                    if 1 <= t <= T:
                        slot_inputs(t - 1)

            def read_slots(eng, e, t, copy):
                for c in (e, e + 2):
                    eng.wait_ge(si_done, NC * t + c + 1)
                    for b in range(2):
                        ins = copy(SI[:, c, :, 2 * t + b, :],
                                   si_banks[c][:, b * ES:(b + 1) * ES].rearrange("p (e s) -> p e s", e=E))
                    ins.then_inc(si_read[e], 1)

            @block.vector
            def _(dve):
                dve.wait_ge(bd_zero, 4)
                for t in range(T + 1):
                    if t < T:
                        dve.wait_ge(l_done, t + 1)
                        if t >= 2:
                            dve.wait_ge(l_turned, t - 1)
                        dve.tensor_copy(lg[t % 2][:, :], l_bank[:, 0:ES]).then_inc(lg_ready, 1)
                        dve.tensor_reduce(cmax[:, t:t + 1], l_bank[:, 0:ES], AX_X, ALU.max, negate=True
                                          ).then_inc(cmax_ready, 1)
                    if t >= 1:
                        v = t - 1
                        dve.wait_ge(disp_turned, t)
                        if v >= 2:
                            dve.wait_ge(si_done, NC * (v - 1))
                        for b in range(2):
                            q = slice(64 * b, 64 * b + 64)
                            dve.tensor_copy(d_bd[v % 2][q, b, :], d_bank[q, 0:ES]).then_inc(dbd_ready, 1)
                    if t < T:
                        u = t % 2
                        lt = lt_bank[:, 0:ES].rearrange("p (k n) -> p k n", k=4)
                        dve.wait_ge(l_turned, t + 1)
                        dve.tensor_reduce(dmax[u][:, :], lt, AX_X, ALU.max).then_inc(dmax_ready, 1)
                        dve.wait_ge(dmax_ready, t + 1)
                        if t >= 2:
                            dve.wait_ge(disp_turned, t - 1)
                        dve.tensor_tensor(le[u][:, :, :], lt, dmax[u][:, :].unsqueeze(2).broadcast_to([P, 4, S]),
                                          ALU.subtract).then_inc(dsub_ready, 1)
                        dve.wait_ge(ce_ready, t + 1)
                        dve.reciprocal(crec[:, t:t + 1], csum[:, t:t + 1]).then_inc(crec_ready, 1)
                        dve.wait_ge(de_ready, t + 1)
                        dve.tensor_reduce(dsum[u][:, :], le[u][:, :, :], AX_X, ALU.add).then_inc(dsum_ready, 1)
                        dve.wait_ge(dsum_ready, t + 1)
                        dve.reciprocal(drec[u][:, :], dsum[u][:, :]).then_inc(drec_ready, 1)
                        dve.wait_ge(drec_ready, t + 1)
                        dve.tensor_tensor(le[u][:, :, :], le[u][:, :, :],
                                          drec[u][:, :].unsqueeze(2).broadcast_to([P, 4, S]), ALU.mult
                                          ).then_inc(disp_ready, 1)
                    if t >= 1:
                        read_slots(dve, 0, t - 1, lambda o, i: dve.tensor_copy(o, i))

            @block.scalar
            def _(act):
                for t in range(T + 1):
                    if t < T:
                        act.wait_ge(cmax_ready, t + 1)
                        if t >= 2:
                            act.wait_ge(cbd_ready, 2 * (t - 1))
                        act.activation(ce[t % 2][:, :, :, :].rearrange("p g e s -> p (g e s)"), l_bank[:, 0:ES],
                                       ACT.Exp, bias=cmax[:, t:t + 1], accum_out=csum[:, t:t + 1]
                                       ).then_inc(ce_ready, 1)
                    if t >= 1:
                        act.wait_ge(comb_turned, t)
                        act.activation(combT[:, t - 1, :, :], c_bank[:, :].rearrange("p (g n) -> p g n", g=EG),
                                       ACT.Copy).then_inc(combT_ready, 1)
                    if t < T:
                        act.wait_ge(dsub_ready, t + 1)
                        act.activation(le[t % 2][:, :, :], le[t % 2][:, :, :], ACT.Exp).then_inc(de_ready, 1)
                    if t >= 1:
                        read_slots(act, 1, t - 1, lambda o, i: act.activation(o, i, ACT.Copy))

    NSO = 4
    Hs = XUT[:, :, :].rearrange("p c n -> p (c n)").rearrange("p (e n) -> p e n", e=E)
    W2 = [XN[:, :, :], AT[:, :, :].rearrange("p c n -> p (c n)").rearrange("p (e n) -> p e n", e=8)]
    b2x = M2
    b1c = sb("b1c", [P, E])
    so = [sb(f"so{i}", [P, D]) for i in range(NSO)]
    fin = [sb(f"fin{u}", [P, D]) for u in range(2)]
    w2_loaded = sem("w2_loaded")
    eb_loaded = sem("eb_loaded")
    h_done = sem("h_done")
    h_ready = sem("h_ready")
    so_done = sem("so_done")
    so_ready = sem("so_ready")
    y_done = sem("y_done")
    fin_ready = sem("fin_ready")
    stored = [sem(f"stored{u}") for u in range(2)]

    with nc.Block() as block:
        @block.sync
        def _(sp):
            sp.dma_start(b1c[:, :], a["b1c"]).then_inc(eb_loaded, 16)
            for g in range(EG):
                sp.dma_start(b2x[:, g, :], bass.AP(a["b2"].tensor, 4 * g * D, [[D, 4], [0, 32], [1, D]])
                             ).then_inc(eb_loaded, 16)
            w2 = a["w2"].rearrange("e h d -> h e d")
            for k in range(2):
                sp.dma_start(W2[k], w2[:, 8 * k:8 * k + 8, :]).then_inc(w2_loaded, 16)
            for t in range(T):
                sp.wait_ge(fin_ready, t + 1)
                sp.dma_start(out[t * P:(t + 1) * P, :], fin[t % 2][:, :]).then_inc(stored[t % 2], 16)
            for u in range(2):
                sp.wait_ge(stored[u], 16 * T // 2)

        @block.tensor
        def _(pe):
            pe.wait_ge(w1_loaded, 16)
            for e in range(E):
                if e >= 4:
                    pe.wait_ge(h_ready, e - 3)
                for c in range(NC):
                    last = pe.matmul(bank[e % 4][:, 0:B * SL], W1[:, e, c, :], SI[:, c, e, :, :],
                                     start=(c == 0), stop=(c == NC - 1))
                last.then_inc(h_done, 1)
            pe.wait_ge(w2_loaded, 32)
            pe.wait_ge(h_ready, E)

            def slot_outputs(t):
                for g in range(EG):
                    if t:
                        pe.wait_ge(so_ready, EG * (t - 1) + g + 1)
                    for k in range(4):
                        e = 4 * g + k
                        last = pe.matmul(bank[g][32 * k:32 * k + 32, :], Hs[:, e, 32 * t:32 * t + 32], W2[e // 8][:, e % 8, :],
                                         start=True, stop=True)
                    last.then_inc(so_done, 1)

            def combine(t):
                if t >= 2:
                    pe.wait_ge(fin_ready, t - 1)
                for g in range(EG):
                    pe.wait_ge(so_ready, EG * t + g + 1)
                    last = pe.matmul(bank[4 + t % 2][:, :], combT[:, t, g, :], so[(EG * t + g) % NSO][:, :],
                                     start=(g == 0), stop=(g == EG - 1))
                    last.then_inc(y_done, 1)

            for t in range(T + 1):
                if t < T:
                    slot_outputs(t)
                if t:
                    combine(t - 1)

        @block.scalar
        def _(act):
            act.wait_ge(eb_loaded, 80)
            for e in range(E):
                act.wait_ge(h_done, e + 1)
                act.activation(Hs[:, e, :], bank[e % 4][:, 0:B * SL], ACT.Gelu, bias=b1c[:, e:e + 1]
                               ).then_inc(h_ready, 1)

        @block.vector
        def _(dve):
            dve.wait_ge(eb_loaded, 80)
            for t in range(T + 1):
                for g in range(EG):
                    n = EG * t + g
                    if t < T:
                        dve.wait_ge(so_done, n + 1)
                        if n >= NSO:
                            dve.wait_ge(y_done, n - NSO + 1)
                        dve.tensor_tensor(so[n % NSO][:, :], bank[g][:, :], b2x[:, g, :], ALU.add
                                          ).then_inc(so_ready, 1)
                if t:
                    v = t - 1
                    dve.wait_ge(y_done, EG * t)
                    if v >= 2:
                        dve.wait_ge(stored[v % 2], 16 * (v // 2))
                    dve.tensor_tensor(fin[v % 2][:, :], bank[4 + v % 2][:, :], X[:, v, :], ALU.add
                                      ).then_inc(fin_ready, 1)


def kernel(**inputs):
    import numpy as _np
    import concourse.bacc as _bacc
    from concourse import mybir as _mybir
    from concourse.bass_utils import run_bass_kernel_spmd as _run

    def arr(name):
        return _np.asarray(inputs[name])

    def cols(*names):
        return _np.stack([arr(n).reshape(-1, P).T for n in names], axis=1)

    xbk, xbv = arr("L0_xattn_bk")[:D], arr("L0_xattn_bk")[D:]
    mask = arr("mask_BxS2_bk0").view(_np.uint8)
    data = {
        "x": arr("x").reshape(TOK, D),
        "ctx": arr("ctx_1024"),
        "mask": mask.reshape(B, P, KB).transpose(0, 2, 1).reshape(B, KEYS).copy().view(_np.uint32),
        "xWq": arr("L0_xattn_Wq"),
        "xWk": arr("L0_xattn_Wk"),
        "xWfcT": arr("L0_xattn_Wfc").T,
        "xcols": _np.stack([v.reshape(-1, P).T for v in (arr("L0_xattn_bq"), xbk, xbv)], axis=1),
        "xbfc": arr("L0_xattn_bfc").reshape(1, D),
        "hWq": arr("L0_attn_Wq"), "hWk": arr("L0_attn_Wk"), "hWv": arr("L0_attn_Wv"), "hWo": arr("L0_attn_Wo"),
        "Wpk": arr("L0_attn_Wpk"), "Wpq": arr("L0_attn_Wpq"),
        "hcols": cols("L0_attn_bq", "L0_attn_bk", "L0_attn_bpk", "L0_attn_bpq"),
        "hbv": arr("L0_attn_bv").reshape(1, D), "hbo": arr("L0_attn_bo").reshape(1, D),
        "rel": arr("L0_attn_rel_emb"),
        "ln_g": arr("L0_attn_ln_g").reshape(1, D), "ln_b": arr("L0_attn_ln_b").reshape(1, D),
        "fln_g": arr("L0_ffn_ln_gamma").reshape(1, D), "fln_b": arr("L0_ffn_ln_beta").reshape(1, D),
        "mu": arr("L0_ffn_mu").reshape(D, ES),
        "fscale": arr("L0_ffn_scale").reshape(1, 1),
        "w1": arr("L0_ffn_w1").reshape(E, NC, P, HID).transpose(2, 0, 1, 3),
        "b1c": arr("L0_ffn_b1").T,
        "w2": arr("L0_ffn_w2"),
        "b2": arr("L0_ffn_b2"),
    }
    nc = _bacc.Bacc("TRN2", target_bir_lowering=False, num_devices=1)
    arrays, aps = {}, {}
    for name, v in data.items():
        v = _np.ascontiguousarray(v)
        arrays[f"in_{name}"] = v
        aps[name] = nc.dram_tensor(f"in_{name}", v.shape, _mybir.dt.from_np(v.dtype), kind="ExternalInput").ap()
    out = nc.dram_tensor("out", (TOK, D), F32, kind="ExternalOutput").ap()
    build(nc, aps, out)
    r = _run(nc, [arrays], core_ids=[0])
    return r.results[0]["out"].reshape(B, S, D)
```

```python
from contextlib import ExitStack
from math import prod

import concourse.bass as bass
from concourse import mybir

ALU = mybir.AluOpType
ACT = mybir.ActivationFunctionType
F32R = mybir.dt.float32r
F32 = mybir.dt.float32
U8 = mybir.dt.uint8
U32 = mybir.dt.uint32
AX_X = mybir.AxisListType.X

P = 128
B = 16
S = 64
D = 512
NC = D // P
TOK = B * S
T = TOK // P
KEYS = 512
KB = KEYS // P
H = 16
HD = D // H
G = H // 4
SPAN = 128
R = 2 * S
IB = 16
W = 80
NI = S // IB
E = 16
SL = 16
ES = E * SL
HID = 128
EG = E // 4
LN_EPS = 1e-5
MASKED = -3e38
NORM_EPS = 1e-12
ATT_SCALE = float((HD * 3) ** -0.5)
POS_SCALE = float((HD * 3) ** 0.5 / (HD * 2) ** 0.5)


def products(pe, dst, lhs, rhs, first=False, last=False, chunk_ready=None):
    for c in range(NC):
        if chunk_ready is not None:
            pe.wait_ge(chunk_ready, c + 1)
        ins = pe.matmul(dst, lhs(c), rhs(c), start=(first and c == 0), stop=(last and c == NC - 1))
    return ins




def build(nc, a, out):
    with ExitStack() as whole:
        def sem(name):
            return whole.enter_context(nc.semaphore(name))

        used = []

        def begin_phase():
            if len(used) >= 2:
                used[-2][1].close()
            mine, scope = [], ExitStack()
            used.append((mine, scope))

            def phase_sem(name):
                mine.append(scope.enter_context(nc.semaphore(name)))
                return mine[-1]

            def retire(pool):
                for done in (used[-2][0] if len(used) >= 2 else []):
                    pool.sem_clear(done)
            return phase_sem, retire

        place = {}

        def buffers(stack):
            def sb(name, shape, dt=F32):
                t = stack.enter_context(nc.sbuf_tensor(name, shape, dt))
                place[name] = nc.sbuf_base - 4 * prod(shape[1:])
                return t
            return sb

        def over(name, shape, host, skip=0, dt=F32R):
            return nc.alloc_sbuf_tensor_at(name, shape, dt, offset=place[host] + skip * 4 * prod(shape[1:]))

        keep = buffers(whole)
        bank = [whole.enter_context(nc.psum_tensor(f"bank{i}", [P, 512], F32)) for i in range(8)]
        X = keep("X", [P, T, D])
        ident = keep("ident", [P, P])
        ones = keep("ones", [P, P])
        eps = keep("eps", [P, 1])

        ident_ready = sem("ident_ready")
        stored = [sem(f"stored{u}") for u in range(2)]
        scr_c2p = nc.dram_tensor("scr_c2p", [TOK, W * H], F32, kind="Internal").ap()
        scr_p2c = nc.dram_tensor("scr_p2c", [TOK, W * H], F32, kind="Internal").ap()

        def transposes(pe, dst, src, n):
            for c in range(n):
                last = pe.transpose(dst[:, c * P:(c + 1) * P], src[:, c * P:(c + 1) * P], ident[:, :])
            return last

        ab = ExitStack()
        with ab:
            sb = buffers(ab)
            M2 = sb("M2", [P, NC, D])
            out_bias = sb("out_bias", [P, D])
            AT = sb("AT", [P, NC, TOK])
            WR = sb("WR", [P, 4, NC, D])
            proj_loaded = sem("proj_loaded")
            wo_loaded = sem("wo_loaded")
            w1_loaded = sem("w1_loaded")

            def load_projection_weights(sp):
                for k, name in enumerate(("Wpk", "Wpq", "hWq", "hWk")):
                    sp.dma_start(WR[:, k, :, :], a[name].rearrange("(c p) n -> p c n", p=P)
                                 ).then_inc(proj_loaded, 16)

            a01 = ExitStack()
            with a01:
                sb01 = buffers(a01)
                QT = sb01("QT", [P, NC, TOK])
                ctx = [sb01(f"ctx{u}", [P, 2, KB, D]) for u in range(3)]
                mask = sb01("mask", [P, T, KEYS // 4], U32)
                s_q = sb01("s_q", [P, T])
                ctx_loaded = [sem(f"ctx_loaded{u}") for u in range(3)]
                mask_loaded = sem("mask_loaded")

                def load_ctx(sp, t):
                    for b in range(2):
                        sp.dma_start(ctx[t % 3][:, b, :, :],
                                     a["ctx"][2 * t + b].rearrange("(p k) d -> p k d", k=KB)
                                     ).then_inc(ctx_loaded[t % 3], 16)

                with ExitStack() as st:
                    phase_queries(nc, a, *begin_phase(), buffers(st), over, bank, X, ident, ones, eps, ident_ready,
                                  transposes, M2, out_bias, WR, QT, mask, s_q, load_ctx, mask_loaded)
                with ExitStack() as st:
                    phase_context(nc, a, *begin_phase(), buffers(st), bank, X, out_bias, ident, transposes,
                                  QT, ctx, mask, s_q, AT, load_ctx, ctx_loaded, mask_loaded, load_projection_weights)
            bc = ExitStack()
            sbc = buffers(bc)
            with bc:
                XT = sbc("XT", [P, NC, TOK])
                QTh = sbc("QTh", [P, G, 2, NI, 8, IB])
                KTh = sbc("KTh", [P, G, 2, NI, 8, IB])
                Wv = sbc("hWv", [P, NC, D])
                bv = sbc("hbv", [P, D])
                NREL = 3
                c2p = [sbc(f"c2p{u}", [P, S, H]) for u in range(NREL)]
                p2c = [sbc(f"p2c{u}", [P, 2, S, 8]) for u in range(NREL)]
                rel_loaded = [sem(f"rel_loaded{u}") for u in range(NREL)]

                def load_relative(sp, t):
                    row = W * H
                    for b in range(2):
                        at = (2 * t + b) * S * row
                        sp.dma_start(c2p[t % NREL][64 * b:64 * b + 64, :, :],
                                     bass.AP(scr_c2p.tensor, at + (IB - 1) * H,
                                             [[IB * row, NI], [row - H, IB], [1, S * H]])
                                     ).then_inc(rel_loaded[t % NREL], 16)
                        for hh in range(2):
                            sp.dma_start(p2c[t % NREL][64 * hh:64 * hh + 64, b, :, :],
                                         bass.AP(scr_p2c.tensor, at + hh * W * 8 + IB * 8,
                                                 [[IB * row, NI], [row - 8, IB], [1, S * 8]])
                                         ).then_inc(rel_loaded[t % NREL], 16)

                with ExitStack() as st:
                    phase_projections(nc, a, *begin_phase(), buffers(st), over, bank, X, eps, transposes,
                                      M2, out_bias, AT, WR, proj_loaded, XT, QTh, KTh, Wv, bv,
                                      len(c2p), scr_c2p, scr_p2c, load_relative)
                with ExitStack() as st:
                    phase_attention(nc, a, *begin_phase(), buffers(st), over, bank, ident,
                                    XT, QTh, KTh, c2p, p2c, AT, rel_loaded, load_relative,
                                    M2, WR, wo_loaded, w1_loaded)
            with ExitStack() as de:
                sde = buffers(de)
                XN = sde("XN", [P, T, D])
                LG = sde("LG", [P, T, ES])
                cmax = sde("cmax", [P, T])
                MU = sde("MU", [P, NC, ES])
                with ExitStack() as st:
                    phase_norms(nc, a, *begin_phase(), buffers(st), over, bank, X, ones, transposes,
                                AT, M2, wo_loaded, XN, LG, cmax, MU)
                with ExitStack() as st:
                    phase_routing_and_experts(nc, a, *begin_phase(), buffers(st), over, bank, X, ident, transposes,
                                              XN, LG, cmax, AT, M2, WR, w1_loaded, stored, out)


def phase_queries(nc, a, sem, retire, sb, over, bank, X, ident, ones, eps, ident_ready, transposes,
                  M2, out_bias, WR, QT, mask, s_q, load_ctx, mask_loaded):
    Wq, Wk, Wv, WfcT = (WR[:, k, :, :] for k in range(4))
    cols = sb("xattn_bias_cols", [P, 3, NC])
    spread = sb("xattn_bias_spread", [P, 3, NC, P])
    bfc = sb("bfc", [P, D])
    xn = sb("xn", [P, T, D])
    M1_hi, M1_lo = sb("M1_hi", [P, NC, D], F32R), sb("M1_lo", [P, NC, D], F32R)
    XNT_hi, XNT_lo = sb("XNT_hi", [P, NC, TOK], F32R), over("XNT_lo", [P, NC, TOK], "AT")
    Wv_hi, Wv_lo = over("xWv_hi", [P, NC, D], "WR", 0), over("xWv_lo", [P, NC, D], "WR", 2)
    Wfc_hi, Wfc_lo = over("xWfc_hi", [P, NC, D], "WR", 1), over("xWfc_lo", [P, NC, D], "WR", 3)
    U = sb("U", [P, D])
    prod = sb("prod_q", [P, D])
    part_sum = sb("part_sum", [P, P])
    qcol = sb("qcol", [P, NC])
    const = sb("const", [P, 1])
    stats = sb("stats", [P, T, 6])
    mv = sb("mv", [P, T, 2])
    std = sb("std", [P, T])
    rstd = sb("rstd", [P, T])

    x_loaded = sem("x_loaded")
    qk_loaded = [sem(f"qk_loaded{c}") for c in range(NC)]
    vo_loaded = sem("vo_loaded")
    bias_loaded = sem("bias_loaded")
    spread_ready = sem("spread_ready")
    fold_done = sem("fold_done")
    m1_hi_ready = sem("m1_hi_ready")
    m1_ready = sem("m1_ready")
    xnT_hi_ready = sem("xnT_hi_ready")
    vo_hi_ready = sem("vo_hi_ready")
    vo_lo_ready = sem("vo_lo_ready")
    shares_read = sem("shares_read")
    qcol_done = sem("qcol_done")
    u_done = sem("u_done")
    bias_done = sem("bias_done")
    u_ready = sem("u_ready")
    qcol_ready = sem("qcol_ready")
    c_ready = sem("c_ready")
    stats_ready = sem("stats_ready")
    mv_ready = sem("mv_ready")
    std_ready = sem("std_ready")
    rstd_ready = sem("rstd_ready")
    xn_ready = sem("xn_ready")
    sq_ready = sem("sq_ready")
    xnT_turned = sem("xnT_turned")
    xnT_ready = sem("xnT_ready")
    qt_done = sem("qt_done")
    qt_read = [sem("qt_read_dve"), sem("qt_read_act")]
    m2_done = sem("m2_done")
    m2_ready = sem("m2_ready")
    out_bias_ready = sem("out_bias_ready")

    m1_banks = bank[0], bank[1], bank[4], bank[5]

    with nc.Block() as block:
        @block.sync
        def _(sp):
            for c in range(NC):
                rows = slice(c * P, (c + 1) * P)
                sp.dma_start(Wq[:, c, :], a["xWq"][rows]).then_inc(qk_loaded[c], 16)
                sp.dma_start(Wk[:, c, :], a["xWk"][rows]).then_inc(qk_loaded[c], 16)
                if c == 0:
                    sp.dma_start(cols[:, :, :], a["xcols"]).then_inc(bias_loaded, 16)
                    sp.dma_start(bfc[:, :], a["xbfc"].broadcast_to([P, D])).then_inc(bias_loaded, 16)
            sp.dma_start(X[:, :, :], a["x"].rearrange("(t p) d -> p t d", p=P)).then_inc(x_loaded, 16)
            sp.dma_start(Wv[:, :, :], a["xWk"][D:2 * D].rearrange("(c p) n -> p c n", p=P)).then_inc(vo_loaded, 16)
            sp.dma_start(WfcT[:, :, :], a["xWfcT"].rearrange("(c p) n -> p c n", p=P)).then_inc(vo_loaded, 16)
            for b in range(2):
                sp.dma_start(mask[64 * b:64 * b + 64, :, :],
                             bass.AP(a["mask"].tensor, b * KEYS // 4, [[0, 64], [2 * KEYS // 4, T], [1, KEYS // 4]])
                             ).then_inc(mask_loaded, 16)
            for t in range(3):
                load_ctx(sp, t)

        @block.gpsimd
        def _(pool):
            pool.memset(ident[:, :], 0.0).then_inc(ident_ready, 1)
            pool.memset(ones[:, :], 1.0).then_inc(ident_ready, 1)
            pool.memset(eps[:, :], LN_EPS).then_inc(ident_ready, 1)
            pool.memset(part_sum[:, :], 1 / 32).then_inc(ident_ready, 1)
            pool.wait_ge(ident_ready, 4)
            pool.affine_select(out=ident[:, :], in_=ident[:, :], compare_op=ALU.not_equal, fill=1.0,
                               base=0, pattern=[[-1, P]], channel_multiplier=1).then_inc(ident_ready, 1)
            pool.wait_ge(m2_done, 1)
            for k, (M, M_hi, M_lo) in enumerate(((WfcT, Wfc_hi, Wfc_lo), (Wv, Wv_hi, Wv_lo))):
                for c in range(NC):
                    pool.wait_ge(vo_hi_ready, NC * k + c + 1)
                    pool.tensor_tensor(M_lo[:, c, :], M[:, c, :], M_hi[:, c, :].bitcast(F32), ALU.subtract
                                       ).then_inc(vo_lo_ready, 1)
            retire(pool)

        @block.tensor
        def _(pe):
            for c in range(NC):
                pe.wait_ge(qk_loaded[c], 32)
                for i in range(NC):
                    last = pe.matmul(m1_banks[i][:, :], Wq[:, c, i * P:(i + 1) * P], Wk[:, c, :],
                                     start=(c == 0), stop=(c == NC - 1))
                    if c == NC - 1:
                        last.then_inc(fold_done, 1)
            def shares(dst, k, M):
                for c in range(NC):
                    last = pe.matmul(dst[32 * c:32 * c + 32, :], spread[:, k, c, 0:32], M[:, c, :],
                                     start=True, stop=True)
                return last

            pe.wait_ge(spread_ready, 3 * NC)
            shares(bank[2], 1, Wq).then_inc(fold_done, 1)
            shares(bank[3], 0, Wk).then_inc(fold_done, 1)
            for c in range(NC):
                last = pe.matmul(bank[7][:, 0:2], spread[:, 1, c, :], spread[:, 0, c, 0:2],
                                 start=(c == 0), stop=(c == NC - 1))
            last.then_inc(fold_done, 1)
            pe.wait_ge(ident_ready, 5)
            pe.wait_ge(m1_ready, NC)

            def turn(t):
                pe.wait_ge(xn_ready, t + 1)
                if t == 3:
                    pe.wait_ge(c_ready, 1)
                if t >= 4:
                    pe.wait_ge(xnT_ready, t - 3)
                transposes(pe, bank[4 + t % 4], xn[:, t, :], NC).then_inc(xnT_turned, 1)

            for t in range(4):
                turn(t)
            pe.wait_ge(shares_read, 2)
            for m in range(NC):
                last = pe.matmul(bank[3][:, m:m + 1], U[:, m * P:(m + 1) * P], part_sum[:, 0:1], start=True, stop=True)
            last.then_inc(qcol_done, 1)
            pe.matmul(bank[2][:, :], part_sum[:, :], prod[:, :], start=True, stop=True).then_inc(u_done, 1)
            for t in range(4, T):
                turn(t)
            pe.wait_ge(u_ready, 1)
            pe.wait_ge(qcol_ready, 1)
            for half in range(2):
                pe.wait_ge(xnT_ready, 4 * (half + 1))
                there = slice(512 * half, 512 * half + 512)
                for m in range(NC):
                    if half:
                        pe.wait_ge(qt_read[m % 2], m // 2 + 1)
                    if half and m == 2:
                        pe.wait_ge(shares_read, 3)
                        pe.matmul(bank[4][:, :], part_sum[:, :], prod[:, :], start=True, stop=True
                                  ).then_inc(bias_done, 1)
                    rows = slice(m * P, (m + 1) * P)
                    products(pe, bank[m][:, :], lambda c: M1_hi[:, c, rows], lambda c: XNT_hi[:, c, there], first=True)
                    products(pe, bank[m][:, :], lambda c: M1_hi[:, c, rows], lambda c: XNT_lo[:, c, there])
                    products(pe, bank[m][:, :], lambda c: M1_lo[:, c, rows], lambda c: XNT_hi[:, c, there], last=True
                             ).then_inc(qt_done, 1)
                if half == 0:
                    pe.wait_ge(xnT_ready, T)
                    pe.wait_ge(vo_loaded, 32)
                    shares(bank[5], 2, WfcT).then_inc(m2_done, 1)
            pe.wait_ge(xnT_ready, T)
            pe.wait_ge(vo_lo_ready, 2 * NC)
            for i in range(NC):
                if i >= 2:
                    pe.wait_ge(m2_ready, i - 1)
                rows = slice(i * P, (i + 1) * P)
                products(pe, bank[6 + i % 2][:, :], lambda c: Wv_hi[:, c, rows], lambda c: Wfc_hi[:, c, :], first=True)
                products(pe, bank[6 + i % 2][:, :], lambda c: Wv_hi[:, c, rows], lambda c: Wfc_lo[:, c, :])
                products(pe, bank[6 + i % 2][:, :], lambda c: Wv_lo[:, c, rows], lambda c: Wfc_hi[:, c, :], last=True
                         ).then_inc(m2_done, 1)

        @block.scalar
        def _(act):
            act.wait_ge(mv_ready, T)
            act.wait_ge(ident_ready, 4)
            act.activation(std[:, :], mv[:, :, 1], ACT.Sqrt, bias=eps[:, :]).then_inc(std_ready, 1)
            for i in range(NC):
                act.wait_ge(fold_done, 1 + i)
                act.activation(M1_hi[:, i, :], m1_banks[i][:, :], ACT.Copy).then_inc(m1_hi_ready, 1)
            for t in range(T):
                act.wait_ge(xnT_turned, t + 1)
                act.activation(XNT_hi[:, :, t * P:(t + 1) * P],
                               bank[4 + t % 4][:, :].rearrange("p (c n) -> p c n", c=NC), ACT.Copy
                               ).then_inc(xnT_hi_ready, 1)
            act.wait_ge(fold_done, NC + 2)
            act.wait_ge(vo_loaded, 32)
            for M, M_hi in ((WfcT, Wfc_hi), (Wv, Wv_hi)):
                for c in range(NC):
                    act.activation(M_hi[:, c, :], M[:, c, :], ACT.Copy).then_inc(vo_hi_ready, 1)
            act.wait_ge(qcol_ready, 1)
            for half in range(2):
                for m in (1, 3):
                    act.wait_ge(qt_done, 4 * half + m + 1)
                    act.activation(QT[:, m, 512 * half:512 * half + 512], bank[m][:, :], ACT.Identity,
                                   bias=qcol[:, m:m + 1]).then_inc(qt_read[1], 1)
            for i in range(NC):
                act.wait_ge(m2_done, 2 + i)
                act.activation(M2[:, i, :], bank[6 + i % 2][:, :], ACT.Copy).then_inc(m2_ready, 1)

        @block.vector
        def _(dve):
            dve.wait_ge(bias_loaded, 32)
            dve.wait_ge(ident_ready, 5)
            for k in range(3):
                for c in range(NC):
                    dve.tensor_scalar(spread[:, k, c, :], ones[:, :], cols[:, k, c:c + 1], None,
                                      ALU.mult).then_inc(spread_ready, 1)
            dve.wait_ge(x_loaded, 16)
            for t in range(T):
                dve.bn_stats(stats[:, t, :], X[:, t, :]).then_inc(stats_ready, 1)
            for t in range(T):
                dve.wait_ge(stats_ready, t + 1)
                dve.bn_aggr(mv[:, t, :], stats[:, t, :]).then_inc(mv_ready, 1)
            dve.wait_ge(std_ready, 1)
            dve.reciprocal(rstd[:, :], std[:, :]).then_inc(rstd_ready, 1)
            dve.wait_ge(rstd_ready, 1)
            for t in range(T):
                dve.tensor_scalar(xn[:, t, :], X[:, t, :], mv[:, t, 0:1], rstd[:, t:t + 1],
                                  ALU.subtract, ALU.mult).then_inc(xn_ready, 1)
            for i in range(NC):
                dve.wait_ge(m1_hi_ready, i + 1)
                dve.tensor_tensor(M1_lo[:, i, :], m1_banks[i][:, :], M1_hi[:, i, :].bitcast(F32), ALU.subtract
                                  ).then_inc(m1_ready, 1)
            dve.wait_ge(fold_done, NC + 1)
            dve.tensor_copy(prod[:, :], bank[2][:, :]).then_inc(shares_read, 1)
            dve.wait_ge(fold_done, NC + 2)
            dve.tensor_copy(U[:, :], bank[3][:, :]).then_inc(shares_read, 1)
            dve.wait_ge(fold_done, NC + 3)
            dve.tensor_copy(const[:, :], bank[7][:, 0:1]).then_inc(c_ready, 1)
            for t in range(T):
                if t == 4:
                    dve.wait_ge(qcol_done, 1)
                    dve.tensor_copy(qcol[:, :], bank[3][:, 0:NC]).then_inc(qcol_ready, 1)
                    dve.wait_ge(u_done, 1)
                    dve.tensor_copy(U[:, :], bank[2][:, :]).then_inc(u_ready, 1)
                dve.wait_ge(xnT_hi_ready, t + 1)
                dve.tensor_tensor(XNT_lo[:, :, t * P:(t + 1) * P],
                                  bank[4 + t % 4][:, :].rearrange("p (c n) -> p c n", c=NC),
                                  XNT_hi[:, :, t * P:(t + 1) * P].bitcast(F32), ALU.subtract).then_inc(xnT_ready, 1)
            dve.wait_ge(u_ready, 1)
            dve.wait_ge(xn_ready, T)
            for t in range(T):
                if t:
                    dve.wait_ge(sq_ready, t)
                dve.tensor_tensor_reduce(out=prod[:, :], in0=xn[:, t, :], in1=U[:, :],
                                         scale=1.0, scalar=0.0, op0=ALU.mult, op1=ALU.add,
                                         accum_out=s_q[:, t:t + 1]).then_inc(sq_ready, 1)
            dve.wait_ge(sq_ready, T)
            dve.wait_ge(c_ready, 1)
            dve.tensor_scalar(s_q[:, :], s_q[:, :], const[:, :], None, ALU.add).then_inc(sq_ready, 1)
            dve.wait_ge(qcol_ready, 1)
            for half in range(2):
                if half:
                    dve.wait_ge(m2_done, 1)
                    dve.tensor_copy(prod[:, :], bank[5][:, :]).then_inc(shares_read, 1)
                for m in (0, 2):
                    dve.wait_ge(qt_done, 4 * half + m + 1)
                    dve.tensor_scalar(QT[:, m, 512 * half:512 * half + 512], bank[m][:, :], qcol[:, m:m + 1], None,
                                      ALU.add).then_inc(qt_read[0], 1)
            dve.wait_ge(bias_done, 1)
            dve.tensor_tensor(out_bias[:, :], bank[4][:, :], bfc[:, :], ALU.add).then_inc(out_bias_ready, 1)


def phase_context(nc, a, sem, retire, sb, bank, X, out_bias, ident, transposes, QT, ctx, mask, s_q,
                  AT, load_ctx, ctx_loaded, mask_loaded, load_projection_weights):
    ctxT = [sb(f"ctxT{u}", [P, 2, NC, KEYS]) for u in range(2)]
    mask_bias = [sb(f"mask_bias{u}", [P, KEYS]) for u in range(2)]
    sm = [sb(f"sm{u}", [P, KEYS]) for u in range(2)]
    prob = [sb(f"prob{u}", [P, KEYS]) for u in range(2)]
    probT = [sb(f"probT{u}", [P, KB, P]) for u in range(2)]
    att = [sb(f"att{u}", [P, D]) for u in range(2)]
    smax = sb("smax", [P, T])
    smax2 = sb("smax2", [P, T])
    nbias = sb("nbias", [P, T])
    rsum = sb("rsum", [P, T])
    rrec = sb("rrec", [P, T])

    turn_banks, s_bank, p_bank, o_bank, at_bank = bank[0:4], bank[4], bank[5], bank[6], bank[7]

    turned = sem("ctx_turned")
    turned_read = [sem("ctx_turned_read_dve"), sem("ctx_turned_read_act")]
    mask_ready = sem("mask_ready")
    x_biased = sem("x_biased")
    scores_done = sem("scores_done")
    sm_ready = sem("sm_ready")
    smax_ready = sem("smax_ready")
    smax2_ready = sem("smax2_ready")
    nbias_ready = sem("nbias_ready")
    prob_ready = sem("prob_ready")
    rrec_ready = sem("rrec_ready")
    prob_turned = sem("prob_turned")
    probT_ready = sem("probT_ready")
    pv_done = sem("pv_done")
    att_ready = sem("att_ready")
    att_turned = sem("att_turned")
    AT_ready = sem("AT_ready")
    NB = 2 * NC

    with nc.Block() as block:
        @block.sync
        def _(sp):
            for t in range(3, T):
                sp.wait_ge(pv_done, t - 2)
                load_ctx(sp, t)
            load_projection_weights(sp)

        @block.gpsimd
        def _(pool):
            pool.wait_ge(mask_loaded, 32)
            for t in range(T):
                if t >= 2:
                    pool.wait_ge(sm_ready, t - 1)
                pool.tensor_scalar(mask_bias[t % 2][:, :], mask[:, t, :].bitcast(U8), MASKED, None,
                                   ALU.mult).then_inc(mask_ready, 1)
                pool.tensor_tensor(X[:, t, :], X[:, t, :], out_bias[:, :], ALU.add).then_inc(x_biased, 1)
            retire(pool)

        @block.tensor
        def _(pe):
            def turn_context(t):
                pe.wait_ge(ctx_loaded[t % 3], 32 * (t // 3 + 1))
                for i in range(NB):
                    b, c = i // NC, i % NC
                    n = (NB * t + i - 4) // 2 + 1
                    if NB * t + i >= 4:
                        pe.wait_ge(turned_read[i % 2], n)
                    for k in range(KB):
                        last = pe.transpose(turn_banks[i % 4][:, k * P:(k + 1) * P],
                                            ctx[t % 3][:, b, k, c * P:(c + 1) * P], ident[:, :])
                    last.then_inc(turned, 1)

            def scores(t):
                if t:
                    pe.wait_ge(sm_ready, t)
                for e in range(2):
                    pe.wait_ge(turned_read[e], 4 * (t + 1))
                for c in range(NC):
                    for b in range(2):
                        last = pe.matmul(s_bank[64 * b:64 * b + 64, :],
                                         QT[:, c, t * P + 64 * b:t * P + 64 * b + 64],
                                         ctxT[t % 2][:, b, c, :], start=(c == 0), stop=(c == NC - 1))
                last.then_inc(scores_done, 1)

            def turn_probs(t):
                pe.wait_ge(prob_ready, t + 1)
                if t:
                    pe.wait_ge(probT_ready, t)
                transposes(pe, p_bank, prob[t % 2], KB).then_inc(prob_turned, 1)

            def attend(t):
                pe.wait_ge(probT_ready, t + 1)
                if t:
                    pe.wait_ge(att_ready, t)
                for k in range(KB):
                    for b in range(2):
                        last = pe.matmul(o_bank[64 * b:64 * b + 64, :],
                                         probT[t % 2][:, k, 64 * b:64 * b + 64],
                                         ctx[t % 3][:, b, k, :], start=(k == 0), stop=(k == KB - 1))
                last.then_inc(pv_done, 1)

            def turn_attended(t):
                pe.wait_ge(att_ready, t + 1)
                if t:
                    pe.wait_ge(AT_ready, t)
                transposes(pe, at_bank, att[t % 2], NC).then_inc(att_turned, 1)

            for t in range(T + 2):
                if t < T:
                    turn_context(t)
                if t >= 2:
                    turn_attended(t - 2)
                if 1 <= t <= T:
                    turn_probs(t - 1)
                if t < T:
                    scores(t)
                if 1 <= t <= T:
                    attend(t - 1)

        @block.vector
        def _(dve):
            for t in range(T + 1):
                if t < T:
                    if t >= 2:
                        dve.wait_ge(scores_done, t - 1)
                    for i in range(0, NB, 2):
                        dve.wait_ge(turned, NB * t + i + 1)
                        dve.tensor_copy(ctxT[t % 2][:, i // NC, i % NC, :], turn_banks[i % 4][:, :]
                                        ).then_inc(turned_read[0], 1)
                    dve.wait_ge(scores_done, t + 1)
                    dve.wait_ge(mask_ready, t + 1)
                    if t >= 2:
                        dve.wait_ge(prob_ready, t - 1)
                    dve.tensor_tensor(sm[t % 2][:, :], s_bank[:, :], mask_bias[t % 2][:, :], ALU.add
                                      ).then_inc(sm_ready, 1)
                    dve.wait_ge(sm_ready, t + 1)
                    dve.tensor_reduce(smax[:, t:t + 1], sm[t % 2][:, :], AX_X, ALU.max).then_inc(smax_ready, 1)
                    dve.wait_ge(smax_ready, t + 1)
                    dve.tensor_tensor(smax2[:, t:t + 1], smax[:, t:t + 1], s_q[:, t:t + 1], ALU.add
                                      ).then_inc(smax2_ready, 1)
                    dve.wait_ge(smax2_ready, t + 1)
                    dve.tensor_tensor(nbias[:, t:t + 1], s_q[:, t:t + 1], smax2[:, t:t + 1], ALU.subtract
                                      ).then_inc(nbias_ready, 1)
                if t >= 1:
                    dve.wait_ge(prob_ready, t)
                    dve.reciprocal(rrec[:, t - 1:t], rsum[:, t - 1:t]).then_inc(rrec_ready, 1)
                    dve.wait_ge(rrec_ready, t)
                    dve.wait_ge(pv_done, t)
                    if t >= 3:
                        dve.wait_ge(att_turned, t - 2)
                    dve.tensor_scalar(att[(t - 1) % 2][:, :], o_bank[:, :], rrec[:, t - 1:t], None, ALU.mult
                                      ).then_inc(att_ready, 1)

        @block.scalar
        def _(act):
            for t in range(T + 2):
                if t < T:
                    if t >= 2:
                        act.wait_ge(scores_done, t - 1)
                    for i in range(1, NB, 2):
                        act.wait_ge(turned, NB * t + i + 1)
                        act.activation(ctxT[t % 2][:, i // NC, i % NC, :], turn_banks[i % 4][:, :], ACT.Copy
                                       ).then_inc(turned_read[1], 1)
                if t >= 2:
                    act.wait_ge(att_turned, t - 1)
                    act.activation(AT[:, :, (t - 2) * P:(t - 1) * P],
                                   at_bank[:, :].rearrange("p (c n) -> p c n", c=NC), ACT.Copy).then_inc(AT_ready, 1)
                if 1 <= t <= T:
                    act.wait_ge(prob_turned, t)
                    if t >= 3:
                        act.wait_ge(pv_done, t - 2)
                    act.activation(probT[(t - 1) % 2][:, :, :], p_bank[:, :].rearrange("p (k n) -> p k n", k=KB),
                                   ACT.Copy).then_inc(probT_ready, 1)
                if t < T:
                    act.wait_ge(nbias_ready, t + 1)
                    if t >= 2:
                        act.wait_ge(prob_turned, t - 1)
                    act.activation(prob[t % 2][:, :], sm[t % 2][:, :], ACT.Exp, bias=nbias[:, t:t + 1],
                                   accum_out=rsum[:, t:t + 1]).then_inc(prob_ready, 1)


def phase_projections(nc, a, sem, retire, sb, over, bank, X, eps, transposes,
                      M2, bo, AT, WR, proj_loaded, XT, QTh, KTh, Wv, bv, NREL,
                      scr_c2p, scr_p2c, load_relative):
    Wpk, Wpq, Wq, Wk = (WR[:, k, :, :] for k in range(4))
    hcols = sb("hcols", [P, 4, G])
    rel = sb("rel", [P, D])
    reln = sb("reln", [P, D])
    ln_g = sb("ln_g", [P, D])
    ln_b = sb("ln_b", [P, D])
    relT = sb("relT", [P, NC, P])
    pos = [sb(f"pos{k}", [P, G, R]) for k in range(2)]
    pos_bd = [sb(f"pos_bd{k}", [P, G, R, 4]) for k in range(2)]
    xn = [sb(f"hxn{u}", [P, D]) for u in range(2)]
    NU = 3
    qp = [sb(f"qp{u}", [P, W * H]) for u in range(NU)]
    stats = sb("hstats", [P, T + 1, 6])
    mv = sb("hmv", [P, T + 1, 2])
    std = sb("hstd", [P, T + 1])
    rstd = sb("hrstd", [P, T + 1])

    A_hi, A_lo = over("xA_hi", [P, NC, TOK], "QTh"), over("xA_lo", [P, NC, TOK], "AT")
    XT_hi, XT_lo = over("XT_hi", [P, NC, TOK], "XT"), over("XT_lo", [P, NC, TOK], "AT")
    M2_hi, M2_lo = over("M2_hi", [P, NC, D], "KTh"), over("M2_lo", [P, NC, D], "M2")
    Wq_hi, Wq_lo = over("Wq_hi", [P, NC, D], "c2p0"), over("Wq_lo", [P, NC, D], "WR", 2)
    Wk_hi, Wk_lo = over("Wk_hi", [P, NC, D], "p2c0"), over("Wk_lo", [P, NC, D], "WR", 3)
    Wv_hi, Wv_lo = over("Wv_hi", [P, NC, D], "WR", 0), over("Wv_lo", [P, NC, D], "hWv")

    pos_loaded = sem("pos_loaded")
    a_hi_ready = sem("xa_hi_ready")
    a_lo_ready = sem("xa_lo_ready")
    m2_hi_ready = sem("m2_hi_ready")
    m2_lo_ready = sem("m2_lo_ready")
    wqk_hi_ready = sem("wqk_hi_ready")
    wqk_lo_ready = sem("wqk_lo_ready")
    wv_hi_ready = sem("wv_hi_ready")
    wv_lo_ready = sem("wv_lo_ready")
    XT_lo_ready = sem("XT_lo_ready")
    bd_zero = sem("bd_zero")
    x1_done = sem("x1_done")
    x1_ready = sem("x1_ready")
    stats_ready = sem("hstats_ready")
    mv_ready = sem("hmv_ready")
    std_ready = sem("hstd_ready")
    rstd_ready = sem("hrstd_ready")
    rel_step = sem("rel_step")
    rel_turned = sem("rel_turned")
    relT_ready = sem("relT_ready")
    pos_done = sem("pos_done")
    pos_ready = sem("pos_ready")
    bd_ready = sem("bd_ready")
    xn_ready = sem("hxn_ready")
    xn_turned = sem("hxn_turned")
    XT_ready = sem("XT_ready")
    qk_done = sem("qk_done")
    qk_read = [sem("qk_read_dve"), sem("qk_read_act")]
    qp_done = sem("qp_done")
    qp_read = [sem("qp_read_dve"), sem("qp_read_act")]
    qp_stored = [sem(f"qp_stored{u}") for u in range(NU)]
    v_done = sem("v_done")
    v_ready = sem("v_ready")
    hv_loaded = sem("hv_loaded")
    bo_loaded = sem("bo_loaded")
    x_biased = sem("hx_biased")
    NT = 2 * NI
    NQ = 2 * NT

    def tile_tokens(M, g, n):
        return M[:, g, (n % NT) // NI, n % NI, :, :]

    with nc.Block() as block:
        @block.sync
        def _(sp):
            sp.dma_start(rel[:, :], a["rel"][SPAN - S:SPAN + S]).then_inc(pos_loaded, 16)
            sp.dma_start(ln_g[:, :], a["ln_g"].broadcast_to([P, D])).then_inc(pos_loaded, 16)
            sp.dma_start(ln_b[:, :], a["ln_b"].broadcast_to([P, D])).then_inc(pos_loaded, 16)
            sp.dma_start(hcols[:, :, :], a["hcols"]).then_inc(pos_loaded, 16)
            sp.dma_start(Wv[:, :, :], a["hWv"].rearrange("(c p) n -> p c n", p=P)).then_inc(hv_loaded, 16)
            sp.dma_start(bv[:, :], a["hbv"].broadcast_to([P, D])).then_inc(hv_loaded, 16)
            sp.dma_start(bo[:, :], a["hbo"].broadcast_to([P, D])).then_inc(bo_loaded, 16)
            for n in range(NQ):
                for e in range(2):
                    sp.wait_ge(qp_read[e], 2 * (n + 1))
                half, i = (n % NT) // NI, n % NI
                scr = scr_c2p if n < NT else scr_p2c
                dst = scr.rearrange("(b i) w -> b i w", b=B)[8 * half:8 * half + 8, IB * i:IB * i + IB, :]
                sp.dma_start(dst, qp[n % NU][:, :]).then_inc(qp_stored[n % NU], 16)
            for u in range(NU):
                sp.wait_ge(qp_stored[u], 16 * len(range(u, NQ, NU)))
            for t in range(NREL):
                load_relative(sp, t)

        @block.gpsimd
        def _(pool):
            def low_part(dst, src, high, ready):
                pool.tensor_tensor(dst, src, high.bitcast(F32), ALU.subtract).then_inc(ready, 1)

            for t in range(T):
                here = slice(t * P, (t + 1) * P)
                pool.wait_ge(a_hi_ready, t + 1)
                low_part(A_lo[:, :, here], AT[:, :, here], A_hi[:, :, here], a_lo_ready)
            pool.wait_ge(wqk_hi_ready, NC)
            for c in range(NC):
                low_part(Wq_lo[:, c, :], Wq[:, c, :], Wq_hi[:, c, :], wqk_lo_ready)
            for k in range(2):
                pool.memset(pos_bd[k][:, :, :, :], 0.0).then_inc(bd_zero, 1)
            pool.wait_ge(wqk_hi_ready, 2 * NC)
            for c in range(NC):
                low_part(Wk_lo[:, c, :], Wk[:, c, :], Wk_hi[:, c, :], wqk_lo_ready)
            pool.wait_ge(wv_hi_ready, NC)
            for c in range(NC):
                low_part(Wv_lo[:, c, :], Wv[:, c, :], Wv_hi[:, c, :], wv_lo_ready)
            pool.wait_ge(bo_loaded, 16)
            pool.wait_ge(xn_ready, T)
            for t in range(T):
                pool.tensor_tensor(X[:, t, :], X[:, t, :], bo[:, :], ALU.add).then_inc(x_biased, 1)
            retire(pool)

        @block.tensor
        def _(pe):
            def project(t):
                if t >= 2:
                    pe.wait_ge(x1_ready, t - 1)
                here = slice(t * P, (t + 1) * P)
                pe.wait_ge(a_hi_ready, t + 1)
                products(pe, bank[t % 2][:, :], lambda c: A_hi[:, c, here], lambda c: M2_hi[:, c, :], first=True,
                         chunk_ready=m2_hi_ready)
                products(pe, bank[t % 2][:, :], lambda c: A_hi[:, c, here], lambda c: M2_lo[:, c, :],
                         chunk_ready=m2_lo_ready)
                pe.wait_ge(a_lo_ready, t + 1)
                products(pe, bank[t % 2][:, :], lambda c: A_lo[:, c, here], lambda c: M2_hi[:, c, :], last=True
                         ).then_inc(x1_done, 1)

            def turn(t):
                pe.wait_ge(xn_ready, t + 1)
                if t >= 2:
                    pe.wait_ge(XT_lo_ready, t - 1)
                transposes(pe, bank[2 + t % 2], xn[t % 2], NC).then_inc(xn_turned, 1)

            def turn_positions():
                pe.wait_ge(relT_ready, 1)
                pe.wait_ge(proj_loaded, 64)
                for k, Wp in enumerate((Wpk, Wpq)):
                    for g in range(G):
                        for c in range(NC):
                            last = pe.matmul(bank[5 + k][:, g * R:(g + 1) * R], Wp[:, c, g * P:(g + 1) * P], relT[:, c, :],
                                             start=(c == 0), stop=(c == NC - 1))
                    last.then_inc(pos_done, 1)

            for t in range(T + 1):
                if t < T:
                    project(t)
                if t == T - 1:
                    turn_positions()
                if t == 1:
                    pe.wait_ge(rel_step, 4)
                    transposes(pe, bank[7], reln, NC).then_inc(rel_turned, 1)
                if t:
                    turn(t - 1)
            def heads(k, W_hi, W_lo):
                pe.wait_ge(wqk_hi_ready, NC * (k + 1))
                pe.wait_ge(wqk_lo_ready, NC * (k + 1))
                for half in range(2):
                    pe.wait_ge(XT_lo_ready, 4 * (half + 1))
                    there = slice(512 * half, 512 * half + 512)
                    for g in range(G):
                        rows = slice(g * P, (g + 1) * P)
                        n = 8 * k + 4 * half + g
                        if n >= 4:
                            pe.wait_ge(qk_read[g % 2], (n - 4) // 2 + 1)
                        if n in (1, 2):
                            pe.wait_ge(pos_ready, G * n)
                        products(pe, bank[4 + g][:, :], lambda c: W_hi[:, c, rows], lambda c: XT_hi[:, c, there],
                                 first=True)
                        products(pe, bank[4 + g][:, :], lambda c: W_hi[:, c, rows], lambda c: XT_lo[:, c, there])
                        products(pe, bank[4 + g][:, :], lambda c: W_lo[:, c, rows], lambda c: XT_hi[:, c, there],
                                 last=True).then_inc(qk_done, 1)

            def positions(k, M):
                pe.wait_ge(bd_ready, 8)
                if k == 0:
                    pe.wait_ge(x1_ready, T)
                    pe.wait_ge(XT_lo_ready, T)
                for n in range(NT * k, NT * k + NT):
                    lo = S - IB - IB * (n % NI)
                    if n % NI == 0:
                        for e in range(2):
                            pe.wait_ge(qk_read[e], 4 * k + 2 * (n % NT // NI + 1))
                    for g in range(G):
                        if n:
                            pe.wait_ge(qp_read[g % 2], 2 * (n - 1) + g // 2 + 1)
                        pe.matmul(bank[g][:, 0:4 * W], tile_tokens(M, g, n),
                                  pos_bd[k][:, g, lo:lo + W, :], start=True, stop=True).then_inc(qp_done, 1)

            heads(0, Wq_hi, Wq_lo)
            positions(0, QTh)
            heads(1, Wk_hi, Wk_lo)
            positions(1, KTh)
            for e in range(2):
                pe.wait_ge(qk_read[e], 8)
            pe.wait_ge(wv_hi_ready, NC)
            pe.wait_ge(wv_lo_ready, NC)
            for t in range(T):
                if t >= 4:
                    pe.wait_ge(v_ready, t - 3)
                here = slice(t * P, (t + 1) * P)
                products(pe, bank[4 + t % 4][:, :], lambda c: XT_hi[:, c, here], lambda c: Wv_hi[:, c, :], first=True)
                products(pe, bank[4 + t % 4][:, :], lambda c: XT_hi[:, c, here], lambda c: Wv_lo[:, c, :])
                products(pe, bank[4 + t % 4][:, :], lambda c: XT_lo[:, c, here], lambda c: Wv_hi[:, c, :], last=True
                         ).then_inc(v_done, 1)

        def read_heads(eng, k, e, write):
            M = (QTh, KTh)[k]
            for half in range(2):
                for g in range(e, G, 2):
                    eng.wait_ge(qk_done, 8 * k + 4 * half + g + 1)
                    write(M[:, g, half, :, :, :].rearrange("p i b w -> p b i w"),
                          bank[4 + g][:, :].rearrange("p (b i w) -> p b i w", b=8, i=NI), hcols[:, k, g:g + 1]
                          ).then_inc(qk_read[e], 1)

        def read_positions(eng, k, e, write):
            for n in range(NT * k, NT * k + NT):
                if n >= NU:
                    eng.wait_ge(qp_stored[n % NU], 16 * (n // NU))
                for g in range(e, G, 2):
                    eng.wait_ge(qp_done, G * n + g + 1)
                    if k == 0:
                        dst = qp[n % NU][:, :].rearrange("p (w h) -> p w h", h=H)[:, :, 4 * g:4 * g + 4]
                    else:
                        dst = qp[n % NU][:, (g // 2) * W * 8:(g // 2 + 1) * W * 8].rearrange(
                            "p (w h) -> p w h", h=8)[:, :, 4 * (g % 2):4 * (g % 2) + 4]
                    write(dst, bank[g][:, 0:4 * W].rearrange("p (w h) -> p w h", h=4)).then_inc(qp_read[e], 1)

        @block.vector
        def _(dve):
            for c in range(NC):
                dve.wait_ge(m2_hi_ready, c + 1)
                dve.tensor_tensor(M2_lo[:, c, :], M2[:, c, :], M2_hi[:, c, :].bitcast(F32), ALU.subtract
                                  ).then_inc(m2_lo_ready, 1)
            dve.wait_ge(pos_loaded, 64)
            dve.bn_stats(stats[:, T, :], rel[:, :]).then_inc(stats_ready, 1)
            dve.wait_ge(stats_ready, 1)
            dve.bn_aggr(mv[:, T, :], stats[:, T, :]).then_inc(mv_ready, 1)
            dve.wait_ge(std_ready, 1)
            dve.reciprocal(rstd[:, T:T + 1], std[:, T:T + 1]).then_inc(rstd_ready, 1)
            dve.wait_ge(rstd_ready, 1)
            dve.tensor_scalar(rel[:, :], rel[:, :], mv[:, T, 0:1], rstd[:, T:T + 1], ALU.subtract, ALU.mult
                              ).then_inc(rel_step, 1)
            dve.wait_ge(rel_step, 1)
            dve.tensor_tensor(reln[:, :], rel[:, :], ln_g[:, :], ALU.mult).then_inc(rel_step, 1)
            dve.wait_ge(rel_step, 2)
            dve.tensor_tensor(reln[:, :], reln[:, :], ln_b[:, :], ALU.add).then_inc(rel_step, 2)
            def low_tokens(t):
                dve.wait_ge(XT_ready, t + 1)
                dve.tensor_tensor(XT_lo[:, :, t * P:(t + 1) * P],
                                  bank[2 + t % 2][:, :].rearrange("p (c n) -> p c n", c=NC),
                                  XT_hi[:, :, t * P:(t + 1) * P].bitcast(F32), ALU.subtract).then_inc(XT_lo_ready, 1)

            for t in range(T):
                dve.wait_ge(x1_done, t + 1)
                dve.tensor_tensor(X[:, t, :], bank[t % 2][:, :], X[:, t, :], ALU.add).then_inc(x1_ready, 1)
                dve.wait_ge(x1_ready, t + 1)
                dve.bn_stats(stats[:, t, :], X[:, t, :]).then_inc(stats_ready, 1)
                dve.wait_ge(stats_ready, t + 2)
                dve.bn_aggr(mv[:, t, :], stats[:, t, :]).then_inc(mv_ready, 1)
                dve.wait_ge(std_ready, t + 2)
                dve.reciprocal(rstd[:, t:t + 1], std[:, t:t + 1]).then_inc(rstd_ready, 1)
                dve.wait_ge(rstd_ready, t + 2)
                if t >= 2:
                    dve.wait_ge(xn_turned, t - 1)
                dve.tensor_scalar(xn[t % 2][:, :], X[:, t, :], mv[:, t, 0:1], rstd[:, t:t + 1],
                                  ALU.subtract, ALU.mult).then_inc(xn_ready, 1)
                if t:
                    low_tokens(t - 1)
            low_tokens(T - 1)
            for k in range(2):
                dve.wait_ge(pos_done, k + 1)
                for g in range(G):
                    dve.tensor_scalar(pos[k][:, g, :], bank[5 + k][:, g * R:(g + 1) * R], hcols[:, 2 + k, g:g + 1],
                                      POS_SCALE, ALU.add, ALU.mult).then_inc(pos_ready, 1)
            dve.wait_ge(pos_ready, 2 * G)
            dve.wait_ge(bd_zero, 2)
            for k in range(2):
                for h in range(4):
                    src = pos[k][32 * h:32 * h + 32, :, :]
                    src = src[:, :, ::-1] if k == 0 else src
                    dve.tensor_copy(pos_bd[k][32 * h:32 * h + 32, :, :, h], src).then_inc(bd_ready, 1)
            for k in range(2):
                read_heads(dve, k, 0, lambda o, i, b: dve.tensor_scalar(o, i, b, None, ALU.add))
                read_positions(dve, k, 0, lambda o, i: dve.tensor_copy(o, i))
            dve.wait_ge(hv_loaded, 32)
            for t in range(T):
                dve.wait_ge(v_done, t + 1)
                dve.tensor_tensor(XT[:, :, t * P:(t + 1) * P], bank[4 + t % 4][:, :].rearrange("p (c n) -> p c n", c=NC),
                                  bv[:, :].rearrange("p (c n) -> p c n", c=NC), ALU.add).then_inc(v_ready, 1)

        @block.scalar
        def _(act):
            def high_part(dst, src, ready):
                act.activation(dst, src, ACT.Copy).then_inc(ready, 1)

            def high_attended(t):
                high_part(A_hi[:, :, t * P:(t + 1) * P], AT[:, :, t * P:(t + 1) * P], a_hi_ready)

            high_attended(0)
            for c in range(NC):
                high_part(M2_hi[:, c, :], M2[:, c, :], m2_hi_ready)
            high_attended(1)
            act.wait_ge(mv_ready, 1)
            act.activation(std[:, T:T + 1], mv[:, T, 1:2], ACT.Sqrt, bias=eps[:, :]).then_inc(std_ready, 1)
            act.wait_ge(proj_loaded, 64)
            for t in range(T + 1):
                if t + 2 < T:
                    high_attended(t + 2)
                if t:
                    Wh, W_hi = (Wq, Wq_hi) if t <= NC else (Wk, Wk_hi)
                    high_part(W_hi[:, (t - 1) % NC, :], Wh[:, (t - 1) % NC, :], wqk_hi_ready)
                if t < T:
                    act.wait_ge(mv_ready, t + 2)
                    act.activation(std[:, t:t + 1], mv[:, t, 1:2], ACT.Sqrt, bias=eps[:, :]).then_inc(std_ready, 1)
                if t == 1:
                    act.wait_ge(rel_turned, 1)
                    act.activation(relT[:, :, :], bank[7][:, :].rearrange("p (c n) -> p c n", c=NC), ACT.Copy
                                   ).then_inc(relT_ready, 1)
                if t:
                    act.wait_ge(xn_turned, t)
                    act.activation(XT_hi[:, :, (t - 1) * P:t * P],
                                   bank[2 + (t - 1) % 2][:, :].rearrange("p (c n) -> p c n", c=NC),
                                   ACT.Copy).then_inc(XT_ready, 1)
            act.wait_ge(pos_done, 2)
            act.wait_ge(hv_loaded, 32)
            for c in range(NC):
                high_part(Wv_hi[:, c, :], Wv[:, c, :], wv_hi_ready)
            for k in range(2):
                read_heads(act, k, 1, lambda o, i, b: act.activation(o, i, ACT.Identity, bias=b))
                read_positions(act, k, 1, lambda o, i: act.activation(o, i, ACT.Copy))


def phase_attention(nc, a, sem, retire, sb, over, bank, ident, V, QTh, KTh, c2p, p2c, AT,
                    rel_loaded, load_relative, Wo, W1, wo_loaded, w1_loaded):
    k_bd = [sb(f"k_bd{u}", [P, G, 4, NI, 2, IB]) for u in range(2)]
    q_of = [sb(f"q_of{u}", [P, G, 2, S]) for u in range(2)]
    v_bd = [sb(f"v_bd{u}", [P, 2, 8, 2, HD]) for u in range(2)]
    sc = [sb(f"sc{u}", [P, 8, 2, S]) for u in range(2)]
    pr = [sb(f"pr{u}", [P, 8, 2, S]) for u in range(2)]
    prT = [over(f"prT{u}", [P, 8, P], "hWv", u, F32) for u in range(2)]
    att = [sb(f"hatt{u}", [P, 2, 8, HD]) for u in range(2)]
    smax = [sb(f"hsmax{u}", [P, H]) for u in range(2)]
    ssum = [sb(f"hssum{u}", [P, H]) for u in range(2)]
    srec = [sb(f"hsrec{u}", [P, H]) for u in range(2)]

    s_banks, p_banks, o_bank, at_bank = (bank[0:2], bank[2:4]), bank[4:6], bank[6], bank[7]

    k_zero = [sem(f"k_bd_zero{u}") for u in range(2)]
    v_zero = sem("v_bd_zero")
    k_ready = sem("k_bd_ready")
    q0_ready = sem("q_of_0_ready")
    q_ready = sem("q_of_ready")
    vbd_ready = sem("v_bd_ready")
    vbd_act_ready = sem("v_bd_act_ready")
    sc_done = sem("hsc_done")
    sc_ready = sem("hsc_ready")
    smax_ready = sem("hsmax_ready")
    shifted = sem("hshifted")
    pr_ready = sem("hpr_ready")
    ssum_ready = sem("hssum_ready")
    srec_ready = sem("hsrec_ready")
    pr_turned = sem("hpr_turned")
    prT_ready = sem("hprT_ready")
    pv_done = sem("hpv_done")
    att_ready = sem("hatt_ready")
    att_turned = sem("hatt_turned")
    AT_ready = sem("hAT_ready")
    NR = 6
    NREL = len(c2p)

    with nc.Block() as block:
        @block.sync
        def _(sp):
            sp.dma_start(Wo[:, :, :], a["hWo"].rearrange("(c p) n -> p c n", p=P)).then_inc(wo_loaded, 16)
            for t in range(NREL, T):
                sp.wait_ge(sc_ready, 2 * (t - NREL + 1))
                load_relative(sp, t)
            sp.dma_start(W1[:, :, :, :].rearrange("p a c n -> p (a c n)"),
                         a["w1"].rearrange("p e c n -> p (e c n)")).then_inc(w1_loaded, 16)

        @block.gpsimd
        def _(pool):
            def queries(t):
                if t >= 2:
                    pool.wait_ge(sc_done, t - 1)
                for b in range(2):
                    pool.tensor_copy(q_of[t % 2][:, :, b, :].rearrange("p g (i w) -> p g i w", i=NI),
                                     QTh[:, :, t // 4, :, 2 * (t % 4) + b, :]).then_inc(q_ready, 1)

            pool.memset(k_bd[0][:, 2:4, :, :, :, :], 0.0).then_inc(k_zero[0], 1)
            pool.memset(k_bd[1][:, :, :, :, :, :], 0.0).then_inc(k_zero[1], 1)
            queries(1)
            pool.memset(v_bd[1][:, :, :, :, :], 0.0).then_inc(v_zero, 1)
            for t in range(T):
                if t + 2 < T:
                    queries(t + 2)
                pool.wait_ge(smax_ready, t + 1)
                pool.tensor_tensor(sc[t % 2][:, :, :, :].rearrange("p a b j -> p (a b) j"),
                                   sc[t % 2][:, :, :, :].rearrange("p a b j -> p (a b) j"),
                                   smax[t % 2][:, :].unsqueeze(2).broadcast_to([P, H, S]), ALU.subtract
                                   ).then_inc(shifted, 1)
            retire(pool)

        @block.tensor
        def _(pe):
            def scores(t):
                pe.wait_ge(k_ready, 4 * (t + 1))
                if t == 0:
                    pe.wait_ge(q0_ready, 2)
                else:
                    pe.wait_ge(q_ready, 2 * t)
                if t >= 2:
                    pe.wait_ge(sc_ready, 2 * (t - 1))
                for g in range(G):
                    for b in range(2):
                        o = s_banks[t % 2][g % 2][64 * b:64 * b + 64, :].rearrange("p (h x j) -> p h x j", h=4, x=2)
                        pe.matmul(o[:, :, g // 2, :], q_of[t % 2][:, g, b, :],
                                  k_bd[t % 2][:, g, :, :, b, :], start=(g < 2), stop=False, skip_group_check=True)
                pe.wait_ge(rel_loaded[t % NREL], 16 * NR * (t // NREL + 1))
                for h in range(8):
                    last = pe.matmul(s_banks[t % 2][h // 4][:, (h % 4) * P:(h % 4 + 1) * P], p2c[t % NREL][:, :, :, h],
                                     ident[:, :], start=False, stop=(h % 4 == 3), is_transpose=True,
                                     skip_group_check=True)
                last.then_inc(sc_done, 1)

            def turn_probs(t):
                pe.wait_ge(pr_ready, t + 1)
                if t:
                    pe.wait_ge(prT_ready, 2 * t)
                for h in range(8):
                    last = pe.transpose(p_banks[h // 4][:, (h % 4) * P:(h % 4 + 1) * P], pr[t % 2][:, h, :, :],
                                        ident[:, :])
                    if h % 4 == 3:
                        last.then_inc(pr_turned, 1)

            def attend(t):
                pe.wait_ge(vbd_ready, 2 * (t + 1))
                pe.wait_ge(vbd_act_ready, 2 * (t + 1))
                if t:
                    pe.wait_ge(att_ready, t)
                for h in range(8):
                    if h % 4 == 0:
                        pe.wait_ge(prT_ready, 2 * t + h // 4 + 1)
                    for b in range(2):
                        o = o_bank[64 * b:64 * b + 64, :].rearrange("p (x h d) -> p x h d", x=2, h=8)
                        last = pe.matmul(o[:, :, h, :], prT[t % 2][:, h, 64 * b:64 * b + 64],
                                         v_bd[t % 2][:, b, h, :, :], start=(h == 0), stop=(h == 7),
                                         skip_group_check=True)
                last.then_inc(pv_done, 1)

            def turn_attended(t):
                pe.wait_ge(att_ready, t + 1)
                if t:
                    pe.wait_ge(AT_ready, t)
                for c in range(NC):
                    last = pe.transpose(at_bank[:, c * P:(c + 1) * P], att[t % 2][:, c // 2, 4 * (c % 2):4 * (c % 2) + 4, :],
                                        ident[:, :])
                last.then_inc(att_turned, 1)

            for t in range(T + 3):
                if t < T:
                    scores(t)
                if 2 <= t < T + 2:
                    turn_probs(t - 2)
                if t >= 3:
                    turn_attended(t - 3)
                if 2 <= t < T + 2:
                    attend(t - 2)

        def value_block(t, b, x):
            return (v_bd[t % 2][64 * x:64 * x + 64, b, :, x, :].rearrange("p (c h) d -> p c h d", c=2),
                    V[64 * b:64 * b + 64, 2 * x:2 * x + 2, t * P:(t + 1) * P].rearrange("p c (h d) -> p c h d", h=4))

        @block.vector
        def _(dve):
            def values(t):
                if t >= 2:
                    dve.wait_ge(pv_done, t - 1)
                for x in range(2):
                    dve.tensor_copy(*value_block(t, 0, x)).then_inc(vbd_ready, 1)

            dve.memset(k_bd[0][:, 0:2, :, :, :, :], 0.0).then_inc(k_zero[0], 1)
            for b in range(2):
                dve.tensor_copy(q_of[0][:, :, b, :].rearrange("p g (i w) -> p g i w", i=NI),
                                QTh[:, :, 0, :, b, :]).then_inc(q0_ready, 1)
            dve.memset(v_bd[0][:, :, :, :, :], 0.0).then_inc(v_zero, 1)
            for t in range(T + 2):
                if t < T:
                    dve.wait_ge(sc_done, t + 1)
                    if t >= 2:
                        dve.wait_ge(pr_ready, t - 1)
                    for k in range(2):
                        dve.tensor_tensor(
                            sc[t % 2][:, 4 * k:4 * k + 4, :, :],
                            s_banks[t % 2][k][:, :].rearrange("p (h x j) -> p h x j", h=4, x=2),
                            c2p[t % NREL][:, :, :].rearrange("p j (x h) -> p h x j", x=2)[:, 4 * k:4 * k + 4, :, :],
                            ALU.add).then_inc(sc_ready, 1)
                    dve.wait_ge(sc_ready, 2 * (t + 1))
                    if t >= 2:
                        dve.wait_ge(shifted, t - 1)
                    dve.tensor_reduce(smax[t % 2][:, :], sc[t % 2][:, :, :, :].rearrange("p a b j -> p (a b) j"),
                                      AX_X, ALU.max).then_inc(smax_ready, 1)
                if t >= 2:
                    v = t - 2
                    dve.wait_ge(srec_ready, v + 1)
                    dve.wait_ge(pv_done, v + 1)
                    if v >= 2:
                        dve.wait_ge(att_turned, v - 1)
                    dve.tensor_tensor(att[v % 2][:, :, :, :], o_bank[:, :].rearrange("p (x h d) -> p x h d", x=2, h=8),
                                      srec[v % 2][:, :].rearrange("p (h x) -> p x h", x=2).unsqueeze(3)
                                      .broadcast_to([P, 2, 8, HD]), ALU.mult).then_inc(att_ready, 1)
                if t < T:
                    if t == 0:
                        dve.wait_ge(v_zero, 2)
                    values(t)
                if 1 <= t <= T:
                    v = t - 1
                    dve.wait_ge(pr_ready, t)
                    if v >= 2:
                        dve.wait_ge(att_ready, v - 1)
                    dve.tensor_reduce(ssum[v % 2][:, :], pr[v % 2][:, :, :, :].rearrange("p a b j -> p (a b) j"),
                                      AX_X, ALU.add).then_inc(ssum_ready, 1)
                    dve.wait_ge(ssum_ready, t)
                    dve.reciprocal(srec[v % 2][:, :], ssum[v % 2][:, :]).then_inc(srec_ready, 1)

        @block.scalar
        def _(act):
            def keys(t):
                if t >= 2:
                    act.wait_ge(sc_done, t - 1)
                for h in range(4):
                    act.activation(k_bd[t % 2][32 * h:32 * h + 32, :, h, :, :, :].rearrange("p g i b w -> p g i (b w)"),
                                   KTh[32 * h:32 * h + 32, :, t // 4, :, 2 * (t % 4):2 * (t % 4) + 2, :]
                                   .rearrange("p g i b w -> p g i (b w)"), ACT.Copy).then_inc(k_ready, 1)

            def exps(t):
                act.wait_ge(shifted, t + 1)
                if t >= 2:
                    act.wait_ge(pr_turned, 2 * (t - 1))
                    act.wait_ge(ssum_ready, t - 1)
                act.activation(pr[t % 2][:, :, :, :].rearrange("p a b j -> p (a b j)"),
                               sc[t % 2][:, :, :, :].rearrange("p a b j -> p (a b j)"), ACT.Exp,
                               scale=ATT_SCALE).then_inc(pr_ready, 1)

            def values(t):
                if t >= 2:
                    act.wait_ge(pv_done, t - 1)
                for x in range(2):
                    place, block = value_block(t, 1, x)
                    act.activation(place, block, ACT.Copy).then_inc(vbd_act_ready, 1)

            act.wait_ge(k_zero[0], 2)
            keys(0)
            act.wait_ge(k_zero[1], 1)
            act.wait_ge(v_zero, 2)
            for t in range(T + 3):
                if t + 1 < T:
                    keys(t + 1)
                if 1 <= t <= T:
                    values(t - 1)
                if 2 <= t < T + 2:
                    v = t - 2
                    if v >= 2:
                        act.wait_ge(pv_done, v - 1)
                    for k in range(2):
                        act.wait_ge(pr_turned, 2 * v + k + 1)
                        act.activation(prT[v % 2][:, 4 * k:4 * k + 4, :],
                                       p_banks[k][:, :].rearrange("p (h n) -> p h n", h=4), ACT.Copy
                                       ).then_inc(prT_ready, 1)
                if 1 <= t <= T:
                    exps(t - 1)
                if t >= 3:
                    act.wait_ge(att_turned, t - 2)
                    act.activation(AT[:, :, (t - 3) * P:(t - 2) * P],
                                   at_bank[:, :].rearrange("p (c n) -> p c n", c=NC), ACT.Copy).then_inc(AT_ready, 1)


def phase_norms(nc, a, sem, retire, sb, over, bank, X, ones, transposes,
                AT, Wo, wo_loaded, XN, LG, cmax, MU):
    ln_g = sb("fln_g", [P, D])
    ln_b = sb("fln_b", [P, D])
    scale = sb("fscale", [P, 1])
    musq = sb("musq", [P, NC, ES])
    munorm = sb("munorm", [P, ES])
    zn = [sb(f"zn{u}", [P, D]) for u in range(2)]
    sq = [sb(f"sq{u}", [P, D]) for u in range(2)]
    XNT = [sb(f"XNT{u}", [P, NC, P]) for u in range(2)]
    Wo_hi, Wo_lo = sb("Wo_hi", [P, NC, D], F32R), over("Wo_lo", [P, NC, D], "M2")
    A_hi, A_lo = sb("A_hi", [P, NC, TOK], F32R), over("A_lo", [P, NC, TOK], "AT")
    eps2 = sb("eps_squared", [P, 1])
    stats = sb("fstats", [P, T, 6])
    mv = sb("fmv", [P, T, 2])
    std = sb("fstd", [P, 2, T])
    rec = sb("frec", [P, 2, T])
    ss = sb("fss", [P, T])

    f_loaded = sem("f_loaded")
    wo_hi_ready = sem("wo_hi_ready")
    wo_lo_ready = sem("wo_lo_ready")
    a_hi_ready = sem("a_hi_ready")
    a_lo_ready = sem("a_lo_ready")
    mu_loaded = sem("mu_loaded")
    musq_ready = sem("musq_ready")
    mu_summed = sem("mu_summed")
    munorm_ready = sem("munorm_ready")
    mu_step = sem("mu_step")
    x2_done = sem("x2_done")
    x2_ready = sem("x2_ready")
    stats_ready = sem("fstats_ready")
    mv_ready = sem("fmv_ready")
    std_ready = sem("fstd_ready")
    rec_ready = sem("frec_ready")
    eps2_ready = sem("eps2_ready")
    zn_ready = sem("zn_ready")
    zg_ready = sem("zg_ready")
    XN_ready = sem("XN_ready")
    ss_ready = sem("ss_ready")
    norm_ready = sem("norm_ready")
    guarded = sem("norm_guarded")
    inv_ready = sem("inv_norm_ready")
    xn_turned = sem("xn_turned")
    XNT_ready = sem("XNT_ready")
    l_done = sem("l_done")
    LG_ready = sem("LG_ready")

    with nc.Block() as block:
        @block.sync
        def _(sp):
            sp.dma_start(MU[:, :, :], a["mu"].rearrange("(c p) n -> p c n", p=P)).then_inc(mu_loaded, 16)
            sp.dma_start(ln_g[:, :], a["fln_g"].broadcast_to([P, D])).then_inc(f_loaded, 16)
            sp.dma_start(ln_b[:, :], a["fln_b"].broadcast_to([P, D])).then_inc(f_loaded, 16)
            sp.dma_start(scale[:, :], a["fscale"].broadcast_to([P, 1])).then_inc(f_loaded, 16)

        @block.gpsimd
        def _(pool):
            def low_part(t):
                pool.wait_ge(a_hi_ready, t + 1)
                pool.tensor_tensor(A_lo[:, :, t * P:(t + 1) * P], AT[:, :, t * P:(t + 1) * P],
                                   A_hi[:, :, t * P:(t + 1) * P].bitcast(F32), ALU.subtract).then_inc(a_lo_ready, 1)

            for t in range(4):
                low_part(t)
            pool.wait_ge(f_loaded, 48)
            for t in range(T):
                if t + 4 < T:
                    low_part(t + 4)
                pool.wait_ge(zn_ready, t + 1)
                pool.tensor_tensor(XN[:, t, :], zn[t % 2][:, :], ln_g[:, :], ALU.mult).then_inc(zg_ready, 1)
                pool.wait_ge(zg_ready, t + 1)
                pool.tensor_tensor(XN[:, t, :], XN[:, t, :], ln_b[:, :], ALU.add).then_inc(XN_ready, 1)
            retire(pool)

        @block.tensor
        def _(pe):
            def project(t):
                if t >= 4:
                    pe.wait_ge(x2_ready, t - 3)
                here = slice(t * P, (t + 1) * P)
                pe.wait_ge(a_hi_ready, t + 1)
                products(pe, bank[t % 4][:, :], lambda c: A_hi[:, c, here], lambda c: Wo_hi[:, c, :], first=True,
                         chunk_ready=wo_hi_ready)
                products(pe, bank[t % 4][:, :], lambda c: A_hi[:, c, here], lambda c: Wo_lo[:, c, :],
                         chunk_ready=wo_lo_ready)
                pe.wait_ge(a_lo_ready, t + 1)
                last = products(pe, bank[t % 4][:, :], lambda c: A_lo[:, c, here], lambda c: Wo_hi[:, c, :],
                                last=True)
                last.then_inc(x2_done, 1)

            def turn(t):
                pe.wait_ge(XN_ready, t + 1)
                if t >= 2:
                    pe.wait_ge(XNT_ready, t - 1)
                transposes(pe, bank[4 + t % 2], XN[:, t, :], NC).then_inc(xn_turned, 1)

            def logits(t):
                pe.wait_ge(XNT_ready, t + 1)
                if t == 0:
                    pe.wait_ge(mu_step, 2 + NC)
                if t:
                    pe.wait_ge(LG_ready, t)
                for c in range(NC):
                    last = pe.matmul(bank[6][:, 0:ES], XNT[t % 2][:, c, :], MU[:, c, :],
                                     start=(c == 0), stop=(c == NC - 1))
                last.then_inc(l_done, 1)

            for t in range(T + 4):
                if t < T:
                    project(t)
                if t == 1:
                    pe.wait_ge(musq_ready, 1)
                    for c in range(NC):
                        last = pe.matmul(bank[7][:, 0:ES], ones[:, :], musq[:, c, :],
                                         start=(c == 0), stop=(c == NC - 1))
                    last.then_inc(mu_summed, 1)
                if 3 <= t < T + 3:
                    turn(t - 3)
                if t >= 4:
                    logits(t - 4)

        @block.scalar
        def _(act):
            def high_part(t):
                act.activation(A_hi[:, :, t * P:(t + 1) * P], AT[:, :, t * P:(t + 1) * P], ACT.Copy
                               ).then_inc(a_hi_ready, 1)

            act.wait_ge(wo_loaded, 16)
            for c in range(NC):
                act.activation(Wo_hi[:, c, :], Wo[:, c, :], ACT.Copy).then_inc(wo_hi_ready, 1)
                if c == 0:
                    high_part(0)
            for t in range(1, 4):
                high_part(t)
            for t in range(T + 3):
                if t + 4 < T:
                    high_part(t + 4)
                if t < T:
                    if t == 0:
                        act.wait_ge(eps2_ready, 1)
                    act.wait_ge(mv_ready, t + 1)
                    act.activation(std[:, 0, t:t + 1], mv[:, t, 1:2], ACT.Sqrt, bias=eps2[:, :], scale=1 + LN_EPS
                                   ).then_inc(std_ready, 1)
                if t == 1:
                    act.wait_ge(mu_summed, 1)
                    act.activation(munorm[:, :], bank[7][:, 0:ES], ACT.Sqrt).then_inc(munorm_ready, 1)
                if t >= 3:
                    v = t - 3
                    act.wait_ge(XN_ready, v + 1)
                    act.activation(sq[v % 2][:, :], XN[:, v, :], ACT.Square, accum_out=ss[:, v:v + 1]
                                   ).then_inc(ss_ready, 1)
                    act.wait_ge(xn_turned, v + 1)
                    if v >= 2:
                        act.wait_ge(l_done, v - 1)
                    act.activation(XNT[v % 2][:, :, :], bank[4 + v % 2][:, :].rearrange("p (c n) -> p c n", c=NC),
                                   ACT.Copy).then_inc(XNT_ready, 1)
                    act.wait_ge(ss_ready, v + 1)
                    act.activation(std[:, 1, v:v + 1], ss[:, v:v + 1], ACT.Sqrt).then_inc(norm_ready, 1)

        @block.vector
        def _(dve):
            dve.memset(eps2[:, :], LN_EPS ** 2).then_inc(eps2_ready, 1)
            for c in range(NC):
                dve.wait_ge(wo_hi_ready, c + 1)
                dve.tensor_tensor(Wo_lo[:, c, :], Wo[:, c, :], Wo_hi[:, c, :].bitcast(F32), ALU.subtract
                                  ).then_inc(wo_lo_ready, 1)
            for t in range(T + 4):
                if t < T:
                    dve.wait_ge(x2_done, t + 1)
                    dve.tensor_tensor(X[:, t, :], bank[t % 4][:, :], X[:, t, :], ALU.add).then_inc(x2_ready, 1)
                    dve.wait_ge(x2_ready, t + 1)
                    dve.bn_stats(stats[:, t, :], X[:, t, :]).then_inc(stats_ready, 1)
                    dve.wait_ge(stats_ready, t + 1)
                    dve.bn_aggr(mv[:, t, :], stats[:, t, :]).then_inc(mv_ready, 1)
                if t == 0:
                    dve.wait_ge(mu_loaded, 16)
                    dve.wait_ge(f_loaded, 48)
                    dve.tensor_tensor(musq[:, :, :], MU[:, :, :], MU[:, :, :], ALU.mult).then_inc(musq_ready, 1)
                if 1 <= t < T + 1:
                    v = t - 1
                    dve.wait_ge(std_ready, v + 1)
                    dve.reciprocal(rec[:, 0, v:v + 1], std[:, 0, v:v + 1]).then_inc(rec_ready, 1)
                    dve.wait_ge(rec_ready, v + 1)
                    if v >= 2:
                        dve.wait_ge(zg_ready, v - 1)
                    dve.tensor_scalar(zn[v % 2][:, :], X[:, v, :], mv[:, v, 0:1], rec[:, 0, v:v + 1],
                                      ALU.subtract, ALU.mult).then_inc(zn_ready, 1)
                if t == 1:
                    dve.wait_ge(munorm_ready, 1)
                    dve.tensor_scalar(munorm[:, :], munorm[:, :], NORM_EPS, None, ALU.max).then_inc(mu_step, 1)
                    dve.wait_ge(mu_step, 1)
                    dve.reciprocal(munorm[:, :], munorm[:, :]).then_inc(mu_step, 1)
                if t == 2:
                    dve.wait_ge(mu_step, 2)
                    for c in range(NC):
                        dve.tensor_tensor(MU[:, c, :], MU[:, c, :], munorm[:, :], ALU.mult).then_inc(mu_step, 1)
                if t >= 4:
                    v = t - 4
                    dve.wait_ge(norm_ready, v + 1)
                    dve.tensor_scalar(std[:, 1, v:v + 1], std[:, 1, v:v + 1], NORM_EPS, None, ALU.max
                                      ).then_inc(guarded, 1)
                    dve.wait_ge(guarded, v + 1)
                    dve.reciprocal(rec[:, 1, v:v + 1], std[:, 1, v:v + 1]).then_inc(inv_ready, 1)
                    dve.wait_ge(inv_ready, v + 1)
                    dve.wait_ge(l_done, v + 1)
                    dve.tensor_scalar(LG[:, v, :], bank[6][:, 0:ES], rec[:, 1, v:v + 1], scale[:, :],
                                      ALU.mult, ALU.mult).then_inc(LG_ready, 1)
                    dve.wait_ge(LG_ready, v + 1)
                    dve.tensor_reduce(cmax[:, v:v + 1], LG[:, v, :], AX_X, ALU.max, negate=True)


def phase_routing_and_experts(nc, a, sem, retire, sb, over, bank, X, ident, transposes, XN, LG, cmax, AT, M2, WR,
                              w1_loaded, stored, out):
    SI = sb("SI", [P, NC, E, B, SL])
    W1 = WR[:, :, :, :].rearrange("p a c n -> p (a c n)").rearrange("p (e c n) -> p e c n", e=E, c=NC)
    combT_hi = sb("combT_hi", [P, T, EG, P], F32R)
    combT_lo = sb("combT_lo", [P, T, EG, P], F32R)

    with ExitStack() as rt:
        def rb(name, shape, dt=F32):
            return rt.enter_context(nc.sbuf_tensor(name, shape, dt))
        ce = [over(f"ce{u}", [P, EG, 4, SL], "M2", u, F32) for u in range(2)]
        le = [over(f"le{u}", [P, 4, S], "M2", 2 + u, F32) for u in range(2)]
        c_bd = [over(f"c_bd{u}", [P, EG, 4, 2, SL], "M2", 2 + u, F32) for u in range(2)]
        d_bd = [rb(f"d_bd{u}", [P, 2, ES]) for u in range(2)]
        csum = rb("csum", [P, T])
        crec = rb("crec", [P, T])
        dmax = [rb(f"dmax{u}", [P, 4]) for u in range(2)]
        dsum = [rb(f"dsum{u}", [P, 4]) for u in range(2)]
        drec = [rb(f"drec{u}", [P, 4]) for u in range(2)]
        lt_banks, d_bank, c_bank, si_banks = bank[0:2], bank[2], bank[3], bank[4:8]
        bd_zero = sem("r_bd_zero")
        ce_ready = sem("ce_ready")
        crec_ready = sem("crec_ready")
        cbd_ready = sem("cbd_ready")
        comb_turned = sem("comb_turned")
        combT_ready = sem("combT_ready")
        l_turned = sem("l_turned")
        dmax_ready = sem("dmax_ready")
        dsub_ready = sem("dsub_ready")
        de_ready = sem("de_ready")
        dsum_ready = sem("dsum_ready")
        drec_ready = sem("drec_ready")
        disp_ready = sem("disp_ready")
        disp_turned = sem("disp_turned")
        dbd_ready = sem("dbd_ready")
        comb_hi_ready = sem("comb_hi_ready")
        si_done = sem("si_done")
        si_read = [sem("si_read_dve"), sem("si_read_act")]

        with nc.Block() as block:
            @block.gpsimd
            def _(pool):
                for u in range(2):
                    pool.memset(c_bd[u][:, :, :, :, :], 0.0).then_inc(bd_zero, 1)
                    pool.memset(d_bd[u][:, :, :], 0.0).then_inc(bd_zero, 1)
                pool.wait_ge(bd_zero, 4)
                for t in range(T):
                    pool.wait_ge(crec_ready, t + 1)
                    if t >= 2:
                        pool.wait_ge(comb_turned, t - 1)
                    for b in range(2):
                        q = slice(64 * b, 64 * b + 64)
                        if t or b:
                            pool.wait_ge(cbd_ready, 2 * t + b)
                        pool.tensor_scalar(c_bd[t % 2][q, :, :, b, :].rearrange("p g e s -> p (g e) s"),
                                           ce[t % 2][q, :, :, :].rearrange("p g e s -> p (g e) s"),
                                           crec[q, t:t + 1], None, ALU.mult).then_inc(cbd_ready, 1)
                retire(pool)

            @block.tensor
            def _(pe):
                def turn_logits(t):
                    if t >= 2:
                        pe.wait_ge(dsub_ready, t - 1)
                    transposes(pe, lt_banks[t % 2], LG[:, t, :], 2).then_inc(l_turned, 1)

                def turn_dispatch(t):
                    pe.wait_ge(disp_ready, t + 1)
                    if t:
                        pe.wait_ge(dbd_ready, 2 * t)
                    for k in range(2):
                        last = pe.transpose(d_bank[:, k * P:(k + 1) * P], le[t % 2][:, 2 * k:2 * k + 2, :], ident[:, :])
                    last.then_inc(disp_turned, 1)

                def turn_combine(t):
                    pe.wait_ge(cbd_ready, 2 * (t + 1))
                    if t:
                        pe.wait_ge(combT_ready, t)
                    for g in range(EG):
                        last = pe.transpose(c_bank[:, g * P:(g + 1) * P], c_bd[t % 2][:, g, :, :, :], ident[:, :])
                    last.then_inc(comb_turned, 1)

                def slot_inputs(t):
                    pe.wait_ge(dbd_ready, 2 * (t + 1))
                    for c in range(NC):
                        if t:
                            if c == 0:
                                pe.wait_ge(si_read[0], t)
                            else:
                                pe.wait_ge(si_read[1], (NC - 1) * (t - 1) + c)
                        pe.matmul(si_banks[c][:, :], XN[:, t, c * P:(c + 1) * P], d_bd[t % 2][:, :, :],
                                  start=True, stop=True).then_inc(si_done, 1)

                for t in range(T + 2):
                    if t < T:
                        turn_logits(t)
                    if 1 <= t <= T:
                        turn_dispatch(t - 1)
                    if t >= 2:
                        slot_inputs(t - 2)
                    if 1 <= t <= T:
                        turn_combine(t - 1)

            def read_slots(eng, e, t, copy):
                for c in ((0,), (1, 2, 3))[e]:
                    eng.wait_ge(si_done, NC * t + c + 1)
                    copy(SI[:, c, :, 2 * t:2 * t + 2, :].rearrange("p e b s -> p b e s"),
                         si_banks[c][:, :].rearrange("p (b e s) -> p b e s", b=2, e=E)).then_inc(si_read[e], 1)

            @block.vector
            def _(dve):
                for t in range(T + 2):
                    if t < T:
                        u = t % 2
                        lt = lt_banks[u][:, 0:ES].rearrange("p (k n) -> p k n", k=4)
                        dve.wait_ge(l_turned, t + 1)
                        dve.tensor_reduce(dmax[u][:, :], lt, AX_X, ALU.max).then_inc(dmax_ready, 1)
                        dve.wait_ge(dmax_ready, t + 1)
                        if t >= 2:
                            dve.wait_ge(disp_turned, t - 1)
                        dve.tensor_tensor(le[u][:, :, :], lt, dmax[u][:, :].unsqueeze(2).broadcast_to([P, 4, S]),
                                          ALU.subtract).then_inc(dsub_ready, 1)
                    if 1 <= t <= T:
                        v = t - 1
                        if t == 1:
                            dve.wait_ge(bd_zero, 4)
                        dve.wait_ge(disp_turned, t)
                        if v >= 2:
                            dve.wait_ge(si_done, NC * (v - 1))
                        for b in range(2):
                            q = slice(64 * b, 64 * b + 64)
                            dve.tensor_copy(d_bd[v % 2][q, b, :], d_bank[q, 0:ES]).then_inc(dbd_ready, 1)
                    if t < T:
                        dve.wait_ge(ce_ready, t + 1)
                        dve.reciprocal(crec[:, t:t + 1], csum[:, t:t + 1]).then_inc(crec_ready, 1)
                        dve.wait_ge(de_ready, t + 1)
                        dve.tensor_reduce(dsum[u][:, :], le[u][:, :, :], AX_X, ALU.add).then_inc(dsum_ready, 1)
                        dve.wait_ge(dsum_ready, t + 1)
                        dve.reciprocal(drec[u][:, :], dsum[u][:, :]).then_inc(drec_ready, 1)
                        dve.wait_ge(drec_ready, t + 1)
                        dve.tensor_tensor(le[u][:, :, :], le[u][:, :, :],
                                          drec[u][:, :].unsqueeze(2).broadcast_to([P, 4, S]), ALU.mult
                                          ).then_inc(disp_ready, 1)
                    if t >= 2:
                        read_slots(dve, 0, t - 2, lambda o, i: dve.tensor_copy(o, i))
                    if 1 <= t <= T:
                        dve.wait_ge(comb_hi_ready, t)
                        dve.tensor_tensor(combT_lo[:, t - 1, :, :], c_bank[:, :].rearrange("p (g n) -> p g n", g=EG),
                                          combT_hi[:, t - 1, :, :].bitcast(F32), ALU.subtract).then_inc(combT_ready, 1)

            @block.scalar
            def _(act):
                for t in range(T + 2):
                    if t < T:
                        if t >= 2:
                            act.wait_ge(cbd_ready, 2 * (t - 1))
                        act.activation(ce[t % 2][:, :, :, :].rearrange("p g e s -> p (g e s)"), LG[:, t, :],
                                       ACT.Exp, bias=cmax[:, t:t + 1], accum_out=csum[:, t:t + 1]
                                       ).then_inc(ce_ready, 1)
                        act.wait_ge(dsub_ready, t + 1)
                        act.activation(le[t % 2][:, :, :], le[t % 2][:, :, :], ACT.Exp).then_inc(de_ready, 1)
                    if t >= 2:
                        read_slots(act, 1, t - 2, lambda o, i: act.activation(o, i, ACT.Copy))
                    if 1 <= t <= T:
                        act.wait_ge(comb_turned, t)
                        act.activation(combT_hi[:, t - 1, :, :], c_bank[:, :].rearrange("p (g n) -> p g n", g=EG),
                                       ACT.Copy).then_inc(comb_hi_ready, 1)

    NSO = 4
    W2 = [XN[:, :, :], AT[:, :, :].rearrange("p c n -> p (c n)").rearrange("p (e n) -> p e n", e=8)]
    b2x = M2
    Hs = [over("Hs0", [P, E // 2, B * SL], "LG", 0, F32), sb("Hs1", [P, E // 2, B * SL])]
    b1c = sb("b1c", [P, E])
    so = [over(f"so{i}", [P, D], "SI", i, F32) for i in range(NSO)]
    so_hi = [over(f"so_hi{i}", [P, D], "SI", NSO + i) for i in range(NSO)]
    so_lo = [over(f"so_lo{i}", [P, D], "SI", 2 * NSO + i) for i in range(NSO)]
    fin = [over(f"fin{u}", [P, D], "SI", 3 * NSO + u, F32)[:, :] for u in range(2)]
    w2_loaded = sem("w2_loaded")
    eb_loaded = sem("eb_loaded")
    h_done = sem("h_done")
    h_ready = sem("h_ready")
    so_done = sem("so_done")
    so_ready = sem("so_ready")
    so_hi_ready = sem("so_hi_ready")
    so_lo_ready = sem("so_lo_ready")
    last_lo_ready = sem("last_lo_ready")
    y_done = sem("y_done")
    fin_ready = sem("fin_ready")

    def low_outputs(eng, n, ready):
        eng.wait_ge(so_hi_ready, n + 1)
        if n >= NSO:
            eng.wait_ge(y_done, n - NSO + 1)
        eng.tensor_tensor(so_lo[n % NSO][:, :], so[n % NSO][:, :], so_hi[n % NSO][:, :].bitcast(F32),
                          ALU.subtract).then_inc(ready, 1)

    with nc.Block() as block:
        @block.sync
        def _(sp):
            sp.dma_start(b1c[:, :], a["b1c"]).then_inc(eb_loaded, 16)
            for g in range(EG):
                sp.dma_start(b2x[:, g, :], bass.AP(a["b2"].tensor, 4 * g * D, [[D, 4], [0, 32], [1, D]])
                             ).then_inc(eb_loaded, 16)
            w2 = a["w2"].rearrange("e h d -> h e d")
            for k in range(2):
                sp.dma_start(W2[k], w2[:, 8 * k:8 * k + 8, :]).then_inc(w2_loaded, 16)
            for t in range(T):
                sp.wait_ge(fin_ready, t + 1)
                sp.dma_start(out[t * P:(t + 1) * P, :], fin[t % 2]).then_inc(stored[t % 2], 16)
            for u in range(2):
                sp.wait_ge(stored[u], 16 * T // 2)

        @block.tensor
        def _(pe):
            pe.wait_ge(w1_loaded, 16)
            for e in range(E):
                if e >= 4:
                    pe.wait_ge(h_ready, e - 3)
                for c in range(NC):
                    last = pe.matmul(bank[e % 4][:, 0:B * SL], W1[:, e, c, :], SI[:, c, e, :, :],
                                     start=(c == 0), stop=(c == NC - 1))
                last.then_inc(h_done, 1)
            pe.wait_ge(w2_loaded, 32)
            pe.wait_ge(h_ready, E)

            def slot_outputs(t):
                for g in range(EG):
                    if t:
                        pe.wait_ge(so_ready, EG * (t - 1) + g + 1)
                    for k in range(4):
                        e = 4 * g + k
                        last = pe.matmul(bank[g][32 * k:32 * k + 32, :], Hs[e // 8][:, e % 8, 32 * t:32 * t + 32],
                                         W2[e // 8][:, e % 8, :], start=True, stop=True)
                    last.then_inc(so_done, 1)

            def combine(t):
                if t >= 2:
                    pe.wait_ge(fin_ready, t - 1)
                for g in range(EG):
                    n = EG * t + g
                    pe.wait_ge(so_hi_ready, n + 1)
                    pe.matmul(bank[4 + t % 2][:, :], combT_hi[:, t, g, :], so_hi[n % NSO][:, :],
                              start=(g == 0), stop=False)
                    pe.matmul(bank[4 + t % 2][:, :], combT_lo[:, t, g, :], so_hi[n % NSO][:, :],
                              start=False, stop=False)
                    if t < T - 1:
                        pe.wait_ge(so_lo_ready, n + 1)
                    else:
                        pe.wait_ge(last_lo_ready, g + 1)
                    pe.matmul(bank[4 + t % 2][:, :], combT_hi[:, t, g, :], so_lo[n % NSO][:, :],
                              start=False, stop=(g == EG - 1)).then_inc(y_done, 1)

            for t in range(T + 1):
                if t < T:
                    slot_outputs(t)
                if t:
                    combine(t - 1)

        @block.gpsimd
        def _(pool):
            for n in range(EG * (T - 1)):
                low_outputs(pool, n, so_lo_ready)

        @block.scalar
        def _(act):
            act.wait_ge(eb_loaded, 80)
            for e in range(E):
                act.wait_ge(h_done, e + 1)
                act.activation(Hs[e // 8][:, e % 8, :], bank[e % 4][:, 0:B * SL], ACT.Gelu, bias=b1c[:, e:e + 1]
                               ).then_inc(h_ready, 1)
            for n in range(EG * T):
                act.wait_ge(so_ready, n + 1)
                if n >= NSO:
                    act.wait_ge(y_done, n - NSO + 1)
                act.activation(so_hi[n % NSO][:, :], so[n % NSO][:, :], ACT.Copy).then_inc(so_hi_ready, 1)

        @block.vector
        def _(dve):
            dve.wait_ge(eb_loaded, 80)
            dve.wait_ge(h_done, E)
            for t in range(T + 1):
                for g in range(EG):
                    n = EG * t + g
                    if t < T:
                        dve.wait_ge(so_done, n + 1)
                        if n >= NSO:
                            dve.wait_ge(so_lo_ready, n - NSO + 1)
                        dve.tensor_tensor(so[n % NSO][:, :], bank[g][:, :], b2x[:, g, :], ALU.add
                                          ).then_inc(so_ready, 1)
                if t == T - 1:
                    for g in range(EG):
                        low_outputs(dve, EG * t + g, last_lo_ready)
                if t:
                    v = t - 1
                    dve.wait_ge(y_done, EG * t)
                    if v >= 2:
                        dve.wait_ge(stored[v % 2], 16 * (v // 2))
                    dve.tensor_tensor(fin[v % 2], bank[4 + v % 2][:, :], X[:, v, :], ALU.add
                                      ).then_inc(fin_ready, 1)


def kernel(**inputs):
    import numpy as _np
    import concourse.bacc as _bacc
    from concourse import mybir as _mybir
    from concourse.bass_utils import run_bass_kernel_spmd as _run

    def arr(name):
        return _np.asarray(inputs[name])

    def cols(*names):
        return _np.stack([arr(n).reshape(-1, P).T for n in names], axis=1)

    xbk, xbv = arr("L0_xattn_bk")[:D], arr("L0_xattn_bk")[D:]
    mask = arr("mask_BxS2_bk0").view(_np.uint8)
    data = {
        "x": arr("x").reshape(TOK, D),
        "ctx": arr("ctx_1024"),
        "mask": mask.reshape(B, P, KB).transpose(0, 2, 1).reshape(B, KEYS).copy().view(_np.uint32),
        "xWq": arr("L0_xattn_Wq"),
        "xWk": arr("L0_xattn_Wk"),
        "xWfcT": arr("L0_xattn_Wfc").T,
        "xcols": _np.stack([v.reshape(-1, P).T for v in (arr("L0_xattn_bq"), xbk, xbv)], axis=1),
        "xbfc": arr("L0_xattn_bfc").reshape(1, D),
        "hWq": arr("L0_attn_Wq"), "hWk": arr("L0_attn_Wk"), "hWv": arr("L0_attn_Wv"), "hWo": arr("L0_attn_Wo"),
        "Wpk": arr("L0_attn_Wpk"), "Wpq": arr("L0_attn_Wpq"),
        "hcols": cols("L0_attn_bq", "L0_attn_bk", "L0_attn_bpk", "L0_attn_bpq"),
        "hbv": arr("L0_attn_bv").reshape(1, D), "hbo": arr("L0_attn_bo").reshape(1, D),
        "rel": arr("L0_attn_rel_emb"),
        "ln_g": arr("L0_attn_ln_g").reshape(1, D), "ln_b": arr("L0_attn_ln_b").reshape(1, D),
        "fln_g": arr("L0_ffn_ln_gamma").reshape(1, D), "fln_b": arr("L0_ffn_ln_beta").reshape(1, D),
        "mu": arr("L0_ffn_mu").reshape(D, ES),
        "fscale": arr("L0_ffn_scale").reshape(1, 1),
        "w1": arr("L0_ffn_w1").reshape(E, NC, P, HID).transpose(2, 0, 1, 3),
        "b1c": arr("L0_ffn_b1").T,
        "w2": arr("L0_ffn_w2"),
        "b2": arr("L0_ffn_b2"),
    }
    nc = _bacc.Bacc("TRN2", target_bir_lowering=False, num_devices=1)
    arrays, aps = {}, {}
    for name, v in data.items():
        v = _np.ascontiguousarray(v)
        arrays[f"in_{name}"] = v
        aps[name] = nc.dram_tensor(f"in_{name}", v.shape, _mybir.dt.from_np(v.dtype), kind="ExternalInput").ap()
    out = nc.dram_tensor("out", (TOK, D), F32, kind="ExternalOutput").ap()
    build(nc, aps, out)
    r = _run(nc, [arrays], core_ids=[0])
    return r.results[0]["out"].reshape(B, S, D)
```
